# Optimizing a Trainium2 kernel written in Bass

```python
import numpy as np
import jax
import jax.numpy as jnp

def _softmax(x, axis=-1):
    return jax.nn.softmax(x, axis=axis)

def _gelu(x):
    return jax.nn.gelu(x, approximate=True)

def _silu(x):
    return jax.nn.silu(x)

def _sigmoid(x):
    return jax.nn.sigmoid(x)

def _layernorm(x, axis=-1, eps=1e-05):
    m = jnp.mean(x, axis=axis, keepdims=True)
    v = jnp.var(x, axis=axis, keepdims=True)
    return (x - m) / jnp.sqrt(v + eps)

def _scatter_add(tgt, idx, src, axis=0):
    return tgt.at[idx].add(src)

def _segment_sum(src, seg, n):
    return jax.ops.segment_sum(src, seg, n)
kernel_name = 'mk_adaln_d1_jaxref_r4_37875c'

def setup_inputs(seed: int=0):
    np.random.seed(seed)
    _w = jnp.asarray

    def _L0_attn_setup():
        import jax, jax.numpy as jnp
        import numpy as np
        B, L, D_MODEL = (4, 512, 256)
        EXPAND = 2
        D_INNER = EXPAND * D_MODEL
        D_STATE = 16
        D_CONV = 4
        DT_RANK = (D_MODEL + 15) // 16
        EPS = 1e-05

        def _rmsnorm(x, w):
            return x * jax.lax.rsqrt(jnp.mean(x * x, axis=-1, keepdims=True) + EPS) * w

        def _causal_depthwise_conv(x, w, b):
            xp = jnp.pad(x, ((0, 0), (0, 0), (D_CONV - 1, 0)))
            y = jax.lax.conv_general_dilated(xp, w[:, None, :], window_strides=(1,), padding='VALID', dimension_numbers=('NCH', 'OIH', 'NCH'), feature_group_count=D_INNER)
            return y + b[None, :, None]

        def _selective_scan(u, delta, A, Bm, Cm, D):

            def step(s, inp):
                d_t, B_t, C_t, u_t = inp
                dA = jnp.exp(d_t[..., None] * A)
                dBu = d_t[..., None] * B_t[:, None, :] * u_t[..., None]
                s = s * dA + dBu
                y = jnp.einsum('bds,bs->bd', s, C_t)
                return (s, y)
            s0 = jnp.zeros((u.shape[0], D_INNER, D_STATE), u.dtype)
            xs = (delta.swapaxes(0, 1), Bm.swapaxes(0, 1), Cm.swapaxes(0, 1), u.swapaxes(0, 1))
            _, ys = jax.lax.scan(step, s0, xs)
            return ys.swapaxes(0, 1) + u * D
        key = jax.random.key(seed)
        ks = jax.random.split(key, 10)
        s = 0.02
        return {'x': jax.random.normal(ks[0], (B, L, D_MODEL), jnp.float32), 'norm_w': jnp.ones((D_MODEL,), jnp.float32), 'in_proj_w': jax.random.normal(ks[1], (2 * D_INNER, D_MODEL), jnp.float32) * s, 'conv_w': jax.random.normal(ks[2], (D_INNER, D_CONV), jnp.float32) * s, 'conv_b': jnp.zeros((D_INNER,), jnp.float32), 'x_proj_w': jax.random.normal(ks[3], (DT_RANK + 2 * D_STATE, D_INNER), jnp.float32) * s, 'dt_proj_w': jax.random.normal(ks[4], (D_INNER, DT_RANK), jnp.float32) * s, 'dt_proj_b': jnp.log(jnp.expm1(jnp.full((D_INNER,), 0.01, jnp.float32))), 'A_log': jnp.log(jnp.broadcast_to(jnp.arange(1, D_STATE + 1, dtype=jnp.float32), (D_INNER, D_STATE))), 'D': jnp.ones((D_INNER,), jnp.float32), 'out_proj_w': jax.random.normal(ks[5], (D_MODEL, D_INNER), jnp.float32) * s}
    _L0_attn_in = _L0_attn_setup()

    def _L0_ffn_setup():
        import jax, jax.numpy as jnp
        import numpy as np
        B, S, D, H, E, K = (2, 256, 256, 128, 16, 4)
        HS = 2 * H

        def silu(z):
            return z * jax.nn.sigmoid(z)
        key = jax.random.key(seed)
        ks = jax.random.split(key, 8)
        sc = lambda fan_in: 1.0 / np.sqrt(fan_in)
        x = jax.random.normal(ks[0], (B, S, D), jnp.float32)
        gate_w = jax.random.normal(ks[1], (E, D), jnp.float32) * sc(D)
        ws_in = jax.random.normal(ks[2], (D, HS), jnp.float32) * sc(D)
        vs_in = jax.random.normal(ks[3], (D, HS), jnp.float32) * sc(D)
        ws_out = jax.random.normal(ks[4], (HS, D), jnp.float32) * sc(HS)
        e_win = jax.random.normal(ks[5], (E, D, H), jnp.float32) * sc(D)
        e_vin = jax.random.normal(ks[6], (E, D, H), jnp.float32) * sc(D)
        e_wout = jax.random.normal(ks[7], (E, H, D), jnp.float32) * sc(H)
        return {'x': x, 'gate_w': gate_w, 'ws_in': ws_in, 'vs_in': vs_in, 'ws_out': ws_out, 'e_win': e_win, 'e_vin': e_vin, 'e_wout': e_wout}
    _L0_ffn_in = _L0_ffn_setup()
    _L0_c = _w((lambda *s: np.random.randn(*s).astype(np.float32) * 0.05)(8, 256))
    _L0_wmod = _w((lambda *s: np.random.randn(*s).astype(np.float32) * 0.05)(256, 6 * 256) * 256 ** (-0.5))
    _d = {'L0_attn_x': _L0_attn_in['x'], 'L0_attn_norm_w': _L0_attn_in['norm_w'], 'L0_attn_in_proj_w': _L0_attn_in['in_proj_w'], 'L0_attn_conv_w': _L0_attn_in['conv_w'], 'L0_attn_conv_b': _L0_attn_in['conv_b'], 'L0_attn_x_proj_w': _L0_attn_in['x_proj_w'], 'L0_attn_dt_proj_w': _L0_attn_in['dt_proj_w'], 'L0_attn_dt_proj_b': _L0_attn_in['dt_proj_b'], 'L0_attn_A_log': _L0_attn_in['A_log'], 'L0_attn_D': _L0_attn_in['D'], 'L0_attn_out_proj_w': _L0_attn_in['out_proj_w'], 'L0_ffn_gate_w': _L0_ffn_in['gate_w'], 'L0_ffn_ws_in': _L0_ffn_in['ws_in'], 'L0_ffn_vs_in': _L0_ffn_in['vs_in'], 'L0_ffn_ws_out': _L0_ffn_in['ws_out'], 'L0_ffn_e_win': _L0_ffn_in['e_win'], 'L0_ffn_e_vin': _L0_ffn_in['e_vin'], 'L0_ffn_e_wout': _L0_ffn_in['e_wout'], 'L0_c': _L0_c, 'L0_wmod': _L0_wmod}
    _x0 = _d['L0_attn_x']
    _d['L0_attn_x'] = jax.random.normal(jax.random.fold_in(jax.random.key(seed), 1), (8, 1024, 256), dtype=_x0.dtype)
    del _x0
    return _d

def reference(L0_attn_x, L0_attn_norm_w, L0_attn_in_proj_w, L0_attn_conv_w, L0_attn_conv_b, L0_attn_x_proj_w, L0_attn_dt_proj_w, L0_attn_dt_proj_b, L0_attn_A_log, L0_attn_D, L0_attn_out_proj_w, L0_ffn_gate_w, L0_ffn_ws_in, L0_ffn_vs_in, L0_ffn_ws_out, L0_ffn_e_win, L0_ffn_e_vin, L0_ffn_e_wout, L0_c, L0_wmod):

    def _L0_attn_ref(x, norm_w, in_proj_w, conv_w, conv_b, x_proj_w, dt_proj_w, dt_proj_b, A_log, D, out_proj_w):
        import jax, jax.numpy as jnp
        import numpy as np
        B, L, D_MODEL = (4, 512, 256)
        EXPAND = 2
        D_INNER = EXPAND * D_MODEL
        D_STATE = 16
        D_CONV = 4
        DT_RANK = (D_MODEL + 15) // 16
        EPS = 1e-05

        def _rmsnorm(x, w):
            return x * jax.lax.rsqrt(jnp.mean(x * x, axis=-1, keepdims=True) + EPS) * w

        def _causal_depthwise_conv(x, w, b):
            xp = jnp.pad(x, ((0, 0), (0, 0), (D_CONV - 1, 0)))
            y = jax.lax.conv_general_dilated(xp, w[:, None, :], window_strides=(1,), padding='VALID', dimension_numbers=('NCH', 'OIH', 'NCH'), feature_group_count=D_INNER)
            return y + b[None, :, None]

        def _selective_scan(u, delta, A, Bm, Cm, D):

            def step(s, inp):
                d_t, B_t, C_t, u_t = inp
                dA = jnp.exp(d_t[..., None] * A)
                dBu = d_t[..., None] * B_t[:, None, :] * u_t[..., None]
                s = s * dA + dBu
                y = jnp.einsum('bds,bs->bd', s, C_t)
                return (s, y)
            s0 = jnp.zeros((u.shape[0], D_INNER, D_STATE), u.dtype)
            xs = (delta.swapaxes(0, 1), Bm.swapaxes(0, 1), Cm.swapaxes(0, 1), u.swapaxes(0, 1))
            _, ys = jax.lax.scan(step, s0, xs)
            return ys.swapaxes(0, 1) + u * D
        h = _rmsnorm(x, norm_w)
        xz = jnp.einsum('bld,ed->ble', h, in_proj_w)
        xi, z = jnp.split(xz, 2, axis=-1)
        xi = _causal_depthwise_conv(xi.swapaxes(1, 2), conv_w, conv_b).swapaxes(1, 2)
        xi = jax.nn.silu(xi)
        x_dbl = jnp.einsum('bld,ed->ble', xi, x_proj_w)
        dt, Bm, Cm = jnp.split(x_dbl, [DT_RANK, DT_RANK + D_STATE], axis=-1)
        delta = jax.nn.softplus(jnp.einsum('blr,dr->bld', dt, dt_proj_w) + dt_proj_b)
        A = -jnp.exp(A_log)
        y = _selective_scan(xi, delta, A, Bm, Cm, D)
        y = y * jax.nn.silu(z)
        out = jnp.einsum('bld,ed->ble', y, out_proj_w)
        return out + x

    def _L0_ffn_ref(x, gate_w, ws_in, vs_in, ws_out, e_win, e_vin, e_wout):
        import jax, jax.numpy as jnp
        import numpy as np
        B, S, D, H, E, K = (2, 256, 256, 128, 16, 4)
        HS = 2 * H

        def silu(z):
            return z * jax.nn.sigmoid(z)
        b, s, d = x.shape
        T = b * s
        xf = x.reshape(T, d)
        g = jax.nn.sigmoid(xf @ gate_w.T)
        topv, topi = jax.lax.top_k(g, K)
        wn = topv / jnp.sum(topv, axis=-1, keepdims=True)
        combine = jnp.zeros_like(g).at[jnp.arange(T)[:, None], topi].add(wn)
        hin = jnp.einsum('td,edh->eth', xf, e_win)
        vin = jnp.einsum('td,edh->eth', xf, e_vin)
        h = silu(hin) * vin * combine.T[:, :, None]
        routed = jnp.einsum('eth,ehd->td', h, e_wout)
        shared = silu(xf @ ws_in) * (xf @ vs_in) @ ws_out
        return (shared + routed).reshape(b, s, d)
    x = L0_attn_x
    mod = (_silu(L0_c) @ L0_wmod).reshape(L0_c.shape[0], 6, 1, -1)
    sa, ca, ga, sb, cb, gb = (mod[:, 0], mod[:, 1], mod[:, 2], mod[:, 3], mod[:, 4], mod[:, 5])
    ga = (2 * (ga >= 0) - 1) * jnp.maximum(jnp.abs(ga), 0.25)
    gb = (2 * (gb >= 0) - 1) * jnp.maximum(jnp.abs(gb), 0.25)
    h = _layernorm(x, axis=-1) * (1 + ca) + sa
    x = x + ga * _L0_attn_ref(h, L0_attn_norm_w, L0_attn_in_proj_w, L0_attn_conv_w, L0_attn_conv_b, L0_attn_x_proj_w, L0_attn_dt_proj_w, L0_attn_dt_proj_b, L0_attn_A_log, L0_attn_D, L0_attn_out_proj_w)
    h = _layernorm(x, axis=-1) * (1 + cb) + sb
    x = x + gb * _L0_ffn_ref(h, L0_ffn_gate_w, L0_ffn_ws_in, L0_ffn_vs_in, L0_ffn_ws_out, L0_ffn_e_win, L0_ffn_e_vin, L0_ffn_e_wout)
    return x

_drawn_inputs = setup_inputs


def setup_inputs(seed=0):
    import zlib

    import numpy as np

    out = dict(_drawn_inputs(seed))
    spreads = {'L0_attn_norm_w': (1.0, 0.6),
     'L0_attn_conv_b': (0.0, 0.8),
     'L0_attn_dt_proj_b': (-4.600166320800781, 0.6),
     'L0_attn_D': (1.0, 0.6)}
    factors = {'L0_attn_in_proj_w': 8.0,
     'L0_attn_conv_w': 8.0,
     'L0_attn_x_proj_w': 8.0,
     'L0_attn_dt_proj_w': 8.0,
     'L0_attn_A_log': 8.0,
     'L0_attn_out_proj_w': 8.0,
     'L0_ffn_gate_w': 8.0,
     'L0_ffn_ws_in': 8.0,
     'L0_ffn_vs_in': 8.0,
     'L0_ffn_ws_out': 8.0,
     'L0_ffn_e_win': 8.0,
     'L0_ffn_e_vin': 8.0,
     'L0_ffn_e_wout': 8.0}
    for name, (base, spread) in spreads.items():
        noise = np.random.default_rng([zlib.crc32(name.encode()), seed]).standard_normal(out[name].shape)
        drawn = base * np.exp(spread * noise) if base else spread * noise
        out[name] = jnp.asarray(drawn.astype(out[name].dtype))
    for name, factor in factors.items():
        out[name] = (out[name] * factor).astype(out[name].dtype)
    return out
```

```python
from contextlib import ExitStack

import numpy as np

import concourse.bass as bass
from concourse import mybir

F32 = mybir.dt.float32
ALU = mybir.AluOpType
ACT = mybir.ActivationFunctionType
AX = mybir.AxisListType

BATCH, SEQ, DM = 8, 1024, 256
DI, NS, CONV, RANK = 512, 16, 4, 16
NE, TOPK, HID = 16, 4, 128
P = 128
CH = 512
NJ = CH // P
NC = BATCH * SEQ // CH
NB = DI // P
NK = DM // P
XD = RANK + 2 * NS
NPAIR = NE // 2 + 1
UNITS = NPAIR * NJ
EPS = 1e-5



def scan_steps(t):
    out = []
    for s in range(NS):
        for i in range(NB):
            out.append((4 * s - 2.1 + 0.45 * i, ("exp", t, s, i)))
            if i < 2:
                out.append((4 * s - 3.8 + i, ("scaled", t, s, i)))
            out.append((4 * s + i + 0.10, ("cols", t, s, i)))
            out.append((4 * s + i + 0.20, ("scan", t, s, i)))
            out.append((4 * s + 4 + 0.5 * i + 0.11, ("rows", t, s, i)))
            out.append((4 * s + 4 + 0.5 * i + 0.21, ("gather", t, s, i)))
        out.append((4 * s + 3.25, ("carry", t, s)))
    return out


def prepare_steps(t):
    out = [(0, ("x_load", t))]
    for j in range(NJ):
        out.append((1 + 0.5 * j, ("x_stat", t, j)))
    out += [(3.5, ("x_rstd", t))] + [(4.5 + 0.3 * j, ("x_norm", t, j)) for j in range(NJ)]
    out += [(6, ("x_scale", t)), (7, ("x_shift", t))]
    out += [(8 + 0.3 * j, ("h_square", t, j)) for j in range(NJ)]
    out += [(10, ("h_rms", t)), (10.5, ("r_gate", t)), (11.5, ("r_add", t)), (11.6, ("r_store", t))]
    for j in range(NJ):
        out.append((12.5 + 0.4 * j, ("h_scale", t, j)))
    for k in range(NK):
        out += [(14.5 + 2 * k, ("hn_t", t, k)), (14.6 + 2 * k, ("hn_evac", t, k))]
    for b in range(NB):
        at = 19 + 3.2 * b
        out += [(at, ("xi", t, b)), (at + 0.1, ("xi_center", t, b)), (at + 0.2, ("xi_copy", t, b)),
                (at + 0.3, ("halo", t, b))]
        out += [(at + 0.8 + 0.6 * n, ("tap", t, b, n)) for n in range(CONV - 1)]
        out += [(at + 2.7, ("u_tanh", t, b)), (at + 3.5, ("u", t, b))]
    out += [(33.5, ("xd", t)), (34, ("xd_evac", t))]
    out += [(35, ("dt_t", t)), (35.1, ("dt_evac", t))]
    for b in range(NB):
        out += [(38 + 0.8 * b, ("dtp", t, b)), (38.2 + 0.8 * b, ("dt_bias", t, b))]
        out += [(42 + 0.01 * b, ("soft", t, b)), (42.5 + b, ("delta", t, b)), (44 + 2 * b, ("du", t, b)),
                (45.5 + 2 * b, ("skip", t, b))]
        out += [(46.8 + 2 * b, ("skip_t", t, b)), (46.9 + 2 * b, ("skip_evac", t, b)),
                (46 + 2 * b, ("du_t", t, b)), (46.1 + 2 * b, ("du_evac", t, b))]
    return out


def mix_steps(t):
    out = [(-0.9, ("r_load", t))]
    for j in range(NJ):
        at = -0.8 + j
        out += [(at, ("z", t, j)), (at + 0.1, ("z_tanh", t, j)), (at + 0.3, ("z_gate", t, j)), (at + 0.4, ("y_gate", t, j))]
        out += [(at + 1.5, ("y_t", t, j)), (at + 1.55, ("y_evac", t, j))]
        out += [(at + 2.5, ("op", t, j)), (at + 2.6, ("op_gate", t, j)), (at + 2.7, ("x1", t, j)), (at + 2.8, ("x1_stat", t, j))]
    out += [(6.2, ("x1_rstd", t))] + [(6.9 + 0.2 * j, ("x1_norm", t, j)) for j in range(NJ)]
    out += [(7.8, ("x1_scale", t)), (8.2, ("x1_shift", t))]
    for k in range(NK):
        out += [(9 + k, ("h2_t", t, k)), (9.1 + k, ("h2_evac", t, k))]
    out += [(11.2, ("logit", t)), (11.3, ("logit_exp", t)), (11.8, ("router", t))]
    first, tick = 12.0, 51.0 / UNITS
    for u in range(UNITS):
        at = first + tick * u
        out += [(at, ("expert_in", t, u)), (at + 0.1, ("e_tanh", t, u)), (at + 0.3, ("e_act", t, u)),
                (at + 0.4, ("e_mul", t, u)), (at + 0.5, ("e_weigh", t, u)),
                (at + 0.7 + tick, ("e_t", t, u)), (at + 0.8 + tick, ("e_evac", t, u)),
                (at + 0.6 + 2 * tick, ("expert_out", t, u))]
        if u % (2 * NPAIR) == 2 * NPAIR - 1:
            out += [(at + 0.65 + 2 * tick, ("out_gate", t, u // (2 * NPAIR))), (at + 0.66 + 2 * tick, ("out_add", t, u // (2 * NPAIR))),
                    (at + 0.67 + 2 * tick, ("out_store", t, u // (2 * NPAIR)))]
    return out


def schedule(slots):
    out = []
    for t, (s, p, m) in enumerate(slots):
        steps = []
        if s is not None:
            steps += scan_steps(t)
        if p is not None:
            steps += prepare_steps(t)
        if m is not None:
            steps += mix_steps(t)
        out += [(100 * t + at, t, n, what) for n, (at, what) in enumerate(steps)]
    out = [((100 * (t - 1) + 66 + 0.001 * n if what[0] in ("exp", "scaled") and what[2] == 0 and t > 0 else at), t, n, what)
           for at, t, n, what in out]
    order = [what for _, _, _, what in sorted(out, key=lambda x: (x[0], x[1], x[2]))]
    placed, done, filled = [], set(), {"wide": [], "narrow": []}
    for what in order:
        if what in done:
            continue
        ring, depth = ("wide", 2) if what[0] in WIDE else ("narrow", 1) if what[0] in NARROW else (None, 0)
        if ring:
            if len(filled[ring]) >= depth:
                old = filled[ring][-depth]
                for reader in (WIDE if ring == "wide" else NARROW)[old[0]]:
                    if (reader, *old[1:]) not in done:
                        done.add((reader, *old[1:]))
                        placed.append((reader, *old[1:]))
            filled[ring].append(what)
        done.add(what)
        placed.append(what)
    return placed


WIDE = {"xi": ("xi_center", "xi_copy"), "xd": ("xd_evac",), "dtp": ("dt_bias",), "z": ("z_tanh", "z_gate"),
        "op": ("op_gate",), "logit": ("logit_exp",), "expert_in": ("e_tanh", "e_act", "e_mul")}
NARROW = {"hn_t": ("hn_evac",), "dt_t": ("dt_evac",), "du_t": ("du_evac",), "skip_t": ("skip_evac",),
          "y_t": ("y_evac",), "h2_t": ("h2_evac",), "e_t": ("e_evac",)}


def fills(order, names):
    return {what: n for n, what in enumerate(w for w in order if w[0] in names)}


def adaln_block(nc, x, norm_w, in_w, conv_w, conv_b, xproj_w, dt_w, dt_b, a_log, d_skip, out_w,
                gate_w, e_in, e_out, c_t, w_mod, out):
    ctx = ExitStack()
    with ctx:
        def sb(name, shape):
            return ctx.enter_context(nc.sbuf_tensor(name, shape, F32))

        def pb(name, shape):
            return ctx.enter_context(nc.psum_tensor(name, shape, F32))

        in_sb = sb("in_sb", [P, NK, 2 * DI])
        out_sb = sb("out_sb", [P, NB, DM])
        ein_sb = sb("ein_sb", [P, NK, NPAIR, 2 * 2 * HID])
        eout_sb = sb("eout_sb", [P, 2 * NPAIR, DM])
        xproj_sb = sb("xproj_sb", [P, NB, XD])
        dtw_sb = sb("dtw_sb", [RANK, DI])
        gate_sb = sb("gate_sb", [P, NK, NE])
        norm_sb = sb("norm_sb", [P, NK])
        convw_sb = sb("convw_sb", [P, NB, CONV])
        convb_sb = sb("convb_sb", [P, NB])
        dtb_sb = sb("dtb_sb", [P, NB])
        skip_sb = sb("skip_sb", [P, NB])
        a_sb = sb("a_sb", [P, NB, NS])
        ident = sb("ident", [P, P])
        minus_half = sb("minus_half", [P, NJ])
        restart = sb("restart", [P, NJ, NE])
        mod_p = sb("mod_p", [P, 3, DM])
        mod_m = sb("mod_m", [P, 4, DM])
        x_sb = sb("x_sb", [P, NJ, DM])
        h_sb = sb("h_sb", [P, NJ, DM])
        hnT = sb("hnT", [P, 2, NK, CH])
        xi_pad = sb("xi_pad", [P, 2, CONV - 1 + CH])
        halo_sb = sb("halo_sb", [P, NB, CONV - 1])
        conv = sb("conv", [P, 2, CH])
        r_sb = conv[:, :, :].rearrange("p a (b n) -> p (a b) n", n=DM)
        th_p = sb("th_p", [P, 2, CH])
        u_sb = sb("u_sb", [P, NB, CH])
        dtT = th_p[0:RANK, 1, :]
        du_sb = sb("du_sb", [P, 2, CH])
        square = sb("square", [P, DM])
        delta = sb("delta", [P, 2, NB, CH])
        xd_sb = sb("xd_sb", [P, 2, NJ, XD])
        duT = sb("duT", [P, 2, NJ, DI])
        y_sb = sb("y_sb", [P, 2, NJ, DI])
        dub = sb("dub", [P, 3, NJ, DI // 2])
        states = sb("states", [P, 2 * NB, CH])
        carry = sb("carry", [P, NS, NB])
        zg = sb("zg", [P, 2, DI])
        yT = sb("yT", [P, 2, NB, P])
        x1 = sb("x1", [P, NJ, DM])
        gated = sb("gated", [P, 2, DM])
        h2 = zg[:, :, :].rearrange("p a (b n) -> p (a b) n", n=DM)
        h2T = sb("h2T", [P, NK, CH])
        act = sb("act", [P, 3, 2, HID])
        hidT = sb("hidT", [P, 2, 2, P])
        g_sb = sb("g_sb", [P, NJ, NE])
        rt = [sb(f"rt{n}", [P, NJ, NE]) for n in range(4)]
        rt_small = [sb(f"rt_small{n}", [P, NJ]) for n in range(2)]
        top = sb("top", [P, NJ, 8])
        weigh = sb("weigh", [P, NJ, 2 * NPAIR])
        bn = sb("bn", [P, 2, NJ, 6])
        mv = sb("mv", [P, 2, NJ, 2])
        rstd = sb("rstd", [P, 2, 2, NJ])
        ssq = sb("ssq", [P, NJ])
        rms = sb("rms", [P, 2, NJ])

        cols_ps = [pb(f"cols_ps{n}", [P, CH]) for n in range(2)]
        rows_ps = [pb(f"rows_ps{n}", [P, DI]) for n in range(2)]
        wide_ps = [pb(f"wide_ps{n}", [P, 512]) for n in range(2)]
        narrow_ps = pb("narrow_ps", [P, 512])
        moe_ps = pb("moe_ps", [P, 2, DM])

        mod_dram = nc.dram_tensor("mod_dram", (BATCH, 6, DM), F32, kind="Internal").ap()
        r_dram = nc.dram_tensor("r_dram", (NC, P, NJ * DM), F32, kind="Internal").ap()

        SEMS = ("weights_in", "const_made", "act_made", "folded", "mod_mm", "mod_made", "mod_stored",
                "mod_in_p", "mod_in_m", "x_in", "r_out", "r_in", "y_out",
                "x_bn", "x_mv", "x_rstd_tmp", "x_rstd_done", "x_norm_done", "h_made", "h_squared", "h_rms_done",
                "r_gated", "r_made", "h_scaled", "xi_centered", "halo_set", "tapped", "u_tanhed", "u_made",
                "halo_saved", "soft_done", "delta_made", "du_made", "skip_made",
                "x1_bn", "x1_mv", "x1_rstd_done", "x1_normed", "h2_made", "z_tanhed", "z_gated", "y_gated",
                "x1_made", "logit_exped", "router_step", "router_done",
                "e_tanhed", "e_acted", "e_weighed", "expert_out_done", "out_gated", "out_added",
                "exp_done", "scaled_done", "cols_full", "scan_done", "carried", "rows_full", "gathered",
                "wide_full0", "wide_full1", "wide_free0", "wide_free1",
                "narrow_full", "narrow_free")
        sem = {name: ctx.enter_context(nc.semaphore(name)) for name in SEMS}

        def clear_semaphores():
            for s in sem.values():
                nc.sync.sem_clear(s)
            nc.all_engine_barrier()

        wmod_sb = y_sb[:, :, :, :].rearrange("p a j n -> p (a j n)")[:, 0:NK * 6 * DM]
        wmod_sb = wmod_sb.rearrange("p (k n) -> p k n", k=NK)
        ct_sb = th_p[:, 0, 0:NK * BATCH].rearrange("p (k b) -> p k b", k=NK)
        ct_half = th_p[:, 1, 0:NK * BATCH].rearrange("p (k b) -> p k b", k=NK)
        ct_tanh = conv[:, 0, 0:NK * BATCH].rearrange("p (k b) -> p k b", k=NK)
        mod_row = h_sb[0:BATCH, :, :].rearrange("b j n -> b (j n)")
        mod_row2 = conv[0:BATCH, 1, :]
        mod_tmp = x_sb[0:BATCH, 0:2, :].rearrange("b j n -> b (j n)")

        LOADS = [(in_sb[:, :, :], in_w), (out_sb[:, :, :], out_w), (ein_sb[:, :, :, :], e_in), (eout_sb[:, :, :], e_out),
                 (xproj_sb[:, :, :], xproj_w), (dtw_sb[:, :], dt_w), (gate_sb[:, :, :], gate_w), (norm_sb[:, :], norm_w),
                 (convw_sb[:, :, :], conv_w), (convb_sb[:, :], conv_b), (dtb_sb[:, :], dt_b), (skip_sb[:, :], d_skip),
                 (a_sb[:, :, :], a_log), (wmod_sb, w_mod), (ct_sb, c_t)]
        with nc.Block() as block:
            @block.sync
            def _(sp):
                for dst, src in LOADS:
                    sp.dma_start(dst, src).then_inc(sem["weights_in"], 16)
                sp.wait_ge(sem["mod_made"], 11)
                rows = [mod_row[:, 512 * n:512 * n + 512] for n in range(2)] + [mod_row2]
                for n in range(3):
                    sp.dma_start(mod_dram[:, 2 * n:2 * n + 2, :].rearrange("b a n -> b (a n)"), rows[n]).then_inc(sem["mod_stored"], 16)
                sp.wait_ge(sem["mod_stored"], 3 * 16)

            @block.gpsimd
            def _(pool):
                pool.memset(ident[:, :], 0.0).then_inc(sem["const_made"], 1)
                pool.memset(minus_half[:, :], -0.5).then_inc(sem["const_made"], 1)
                pool.memset(restart[:, :, :], 1.0).then_inc(sem["const_made"], 1)
                pool.memset(weigh[:, :, :], 0.5).then_inc(sem["const_made"], 1)
                pool.wait_ge(sem["const_made"], 4)
                pool.affine_select(out=ident[:, :], in_=ident[:, :], compare_op=ALU.not_equal, fill=1.0, base=0,
                                   pattern=[[-1, P]], channel_multiplier=1).then_inc(sem["const_made"], 1)
                pool.memset(restart[:, :, 0:1], 0.0).then_inc(sem["const_made"], 1)

            @block.scalar
            def _(act_e):
                act_e.wait_ge(sem["weights_in"], 16 * len(LOADS))
                act_e.activation(a_sb[:, :, :], a_sb[:, :, :], ACT.Exp).then_inc(sem["act_made"], 1)
                act_e.activation(ct_tanh, ct_sb, ACT.Tanh, scale=0.5).then_inc(sem["act_made"], 1)

            @block.vector
            def _(v):
                v.wait_ge(sem["weights_in"], 16 * len(LOADS))
                for k in range(NK):
                    v.tensor_scalar(in_sb[:, k, :], in_sb[:, k, :], norm_sb[:, k:k + 1], None, ALU.mult).then_inc(sem["folded"], 1)
                v.tensor_scalar(convw_sb[:, :, :], convw_sb[:, :, :], 0.5, None, ALU.mult).then_inc(sem["folded"], 1)
                v.tensor_scalar(convb_sb[:, :], convb_sb[:, :], 0.5, None, ALU.mult).then_inc(sem["folded"], 1)
                v.tensor_scalar(out_sb[:, :, :], out_sb[:, :, :], 0.5, None, ALU.mult).then_inc(sem["folded"], 1)
                v.tensor_scalar(ct_half, ct_sb, 0.5, None, ALU.mult).then_inc(sem["folded"], 1)
                v.wait_ge(sem["act_made"], 2)
                v.tensor_scalar(a_sb[:, :, :], a_sb[:, :, :], -1.0, None, ALU.mult).then_inc(sem["folded"], 1)
                v.wait_ge(sem["folded"], NK + 5)
                v.scalar_tensor_tensor(ct_half, ct_tanh, 1.0, ct_half, ALU.add, ALU.mult).then_inc(sem["mod_made"], 1)
                v.wait_ge(sem["mod_mm"], 1)
                v.tensor_copy(mod_row[:, 0:512], wide_ps[0][0:BATCH, :]).then_inc(sem["mod_made"], 1)
                v.tensor_copy(mod_row[:, 512:1024], wide_ps[1][0:BATCH, :]).then_inc(sem["mod_made"], 1)
                v.tensor_copy(mod_row2, rows_ps[0][0:BATCH, :]).then_inc(sem["mod_made"], 1)
                v.wait_ge(sem["mod_made"], 4)
                v.tensor_scalar(mod_row[:, DM:2 * DM], mod_row[:, DM:2 * DM], 1.0, None, ALU.add).then_inc(sem["mod_made"], 1)
                v.tensor_scalar(mod_row2[:, 0:DM], mod_row2[:, 0:DM], 1.0, None, ALU.add).then_inc(sem["mod_made"], 1)
                gates = [mod_row[:, 2 * DM:3 * DM], mod_row2[:, DM:2 * DM]]
                for n, g in enumerate(gates):
                    v.tensor_scalar(mod_tmp[:, DM * n:DM * n + DM], g, 0.0, 2.0, ALU.is_ge, ALU.mult).then_inc(sem["mod_made"], 1)
                v.wait_ge(sem["mod_made"], 8)
                v.tensor_scalar(mod_tmp, mod_tmp, 1.0, None, ALU.subtract).then_inc(sem["mod_made"], 1)
                v.wait_ge(sem["mod_made"], 9)
                for n, g in enumerate(gates):
                    v.tensor_tensor(g, g, mod_tmp[:, DM * n:DM * n + DM], ALU.mult).then_inc(sem["folded"], 1)
                v.wait_ge(sem["folded"], NK + 7)
                for n, g in enumerate(gates):
                    v.scalar_tensor_tensor(g, g, 0.25, mod_tmp[:, DM * n:DM * n + DM], ALU.max, ALU.mult).then_inc(sem["mod_made"], 1)

            @block.tensor
            def _(pe):
                pe.wait_ge(sem["mod_made"], 1)
                for n, bank in enumerate((wide_ps[0], wide_ps[1], rows_ps[0])):
                    for k in range(NK):
                        last = pe.matmul(bank[0:BATCH, :], ct_half[:, k, :], wmod_sb[:, k, 512 * n:512 * n + 512],
                                         start=(k == 0), stop=(k == NK - 1))
                last.then_inc(sem["mod_mm"], 1)
        clear_semaphores()

        def run_slots(slots, load_mod_p=None, load_mod_m=None):
            order = schedule(slots)
            wide = fills(order, WIDE)
            narrow = fills(order, NARROW)

            def stages_before(t, kind):
                return sum(slots[n][kind] is not None for n in range(t))

            def nS(t):
                return stages_before(t, 0)

            def nP(t):
                return stages_before(t, 1)

            def nM(t):
                return stages_before(t, 2)

            def wide_bank(key):
                return wide_ps[wide[key] % 2][:, :]

            def wide_room(key):
                return sem[f"wide_free{wide[key] % 2}"], wide[key] // 2

            def wide_full(key):
                return sem[f"wide_full{wide[key] % 2}"], wide[key] // 2 + 1

            def wide_read(key):
                return sem[f"wide_free{wide[key] % 2}"], wide[key] // 2 + 1

            def narrow_room(key):
                return sem["narrow_free"], narrow[key]

            def narrow_full(key):
                return sem["narrow_full"], narrow[key] + 1

            def narrow_read(key):
                return sem["narrow_free"], narrow[key] + 1

            def soft_place(b):
                return (th_p, conv)[b // 2][:, b % 2, :]

            def walk(steps):
                for name, *where in order:
                    if name in steps:
                        steps[name](*where)

            def pair_of(u):
                return u % (2 * NPAIR) // 2

            def tile_of(u):
                return 2 * (u // (2 * NPAIR)) + u % 2

            with nc.Block() as block:
                @block.sync
                def _(sp):
                    if load_mod_p is not None:
                        row = mod_dram[bass.ds(load_mod_p, 1), 0:3, :].rearrange("o a n -> o (a n)")
                        sp.dma_start(mod_p[:, :, :].rearrange("p a n -> p (a n)"), row.broadcast_to([P, 3 * DM])).then_inc(sem["mod_in_p"], 16)
                    if load_mod_m is not None:
                        row = mod_dram[bass.ds(load_mod_m, 1), 2:6, :].rearrange("o a n -> o (a n)")
                        sp.dma_start(mod_m[:, :, :].rearrange("p a n -> p (a n)"), row.broadcast_to([P, 4 * DM])).then_inc(sem["mod_in_m"], 16)

                    def x_load(t):
                        if nP(t):
                            sp.wait_ge(sem["r_made"], nP(t))
                        sp.dma_start(x_sb[:, :, :], x[bass.ds(slots[t][1][1], 1)].rearrange("o p j n -> (o p) j n")).then_inc(sem["x_in"], 16)

                    def r_store(t):
                        sp.wait_ge(sem["r_made"], nP(t) + 1)
                        sp.dma_start(r_dram[bass.ds(slots[t][1][1], 1)].rearrange("o p n -> (o p) n"),
                                     conv[:, :, :].rearrange("p a n -> p (a n)")).then_inc(sem["r_out"], 16)

                    def r_load(t):
                        if nM(t):
                            sp.wait_ge(sem["y_out"], nM(t) * 32)
                        sp.dma_start(x1[:, :, :].rearrange("p j n -> p (j n)"),
                                     r_dram[bass.ds(slots[t][2][1], 1)].rearrange("o p n -> (o p) n")).then_inc(sem["r_in"], 16)

                    def out_store(t, q):
                        sp.wait_ge(sem["out_added"], 2 * nM(t) + q + 1)
                        sp.dma_start(out[bass.ds(slots[t][2][1], 1), :, 2 * q:2 * q + 2, :].rearrange("o p j n -> (o p) j n"),
                                     x1[:, 2 * q:2 * q + 2, :]).then_inc(sem["y_out"], 16)

                    walk({"x_load": x_load, "r_store": r_store, "r_load": r_load, "out_store": out_store})
                    sp.wait_ge(sem["r_out"], 16 * nP(len(slots)))
                    sp.wait_ge(sem["y_out"], 32 * nM(len(slots)))

                @block.gpsimd
                def _(pool):
                    def x_rstd(t):
                        pool.wait_ge(sem["x_mv"], NJ * (nP(t) + 1))
                        pool.tensor_scalar(rstd[:, 0, 0, :], mv[:, 0, :, 1], EPS, None, ALU.add).then_inc(sem["x_rstd_tmp"], 1)
                        own[0] += 1
                        pool.wait_ge(sem["x_rstd_tmp"], own[0])
                        pool.tensor_tensor(rstd[:, 0, 1, :], rstd[:, 0, 0, :], minus_half[:, :], ALU.pow).then_inc(sem["x_rstd_done"], 1)

                    def h_rms(t):
                        pool.wait_ge(sem["h_squared"], NJ * (nP(t) + 1))
                        pool.tensor_scalar(rms[:, 0, :], ssq[:, :], 1.0 / DM, EPS, ALU.mult, ALU.add).then_inc(sem["x_rstd_tmp"], 1)
                        own[0] += 1
                        pool.wait_ge(sem["x_rstd_tmp"], own[0])
                        pool.tensor_tensor(rms[:, 1, :], rms[:, 0, :], minus_half[:, :], ALU.pow).then_inc(sem["h_rms_done"], 1)

                    def r_gate(t):
                        pool.wait_ge(sem["h_made"], 2 * (nP(t) + 1))
                        if nP(t):
                            pool.wait_ge(sem["delta_made"], NB * nP(t))
                        pool.tensor_tensor(r_sb[:, :, :], h_sb[:, :, :], mod_p[:, 2:3, :].broadcast_to([P, NJ, DM]), ALU.mult).then_inc(sem["r_gated"], 1)

                    def r_add(t):
                        pool.wait_ge(sem["r_gated"], nP(t) + 1)
                        pool.tensor_tensor(r_sb[:, :, :], r_sb[:, :, :], x_sb[:, :, :], ALU.add).then_inc(sem["r_made"], 1)

                    def du(t, b):
                        n = NB * nP(t) + b
                        pool.wait_ge(sem["delta_made"], n + 1)
                        if n >= 2:
                            pool.wait_ge(*narrow_full(du_key(n - 2)))
                        pool.tensor_tensor(du_sb[:, b % 2, :], delta[:, slots[t][1][0], b, :], u_sb[:, b, :], ALU.mult).then_inc(sem["du_made"], 1)

                    def du_key(n):
                        tt = [t for t in range(len(slots)) if slots[t][1] is not None][n // NB]
                        return ("du_t", tt, n % NB)

                    def scaled(t, s, half):
                        par = slots[t][0][0]
                        n = (NS * nS(t) + s) * 2 + half
                        if t > 0 and slots[t - 1][1] is not None:
                            pool.wait_ge(*narrow_read(("du_t", t - 1, NB - 1)))
                        pool.wait_ge(sem["cols_full"], max(0, 2 * (n - 3) + 2))
                        pool.tensor_tensor(dub[:, n % 3, :, :], duT[:, par, :, half * 256:half * 256 + 256],
                                           xd_sb[:, par, :, RANK + s:RANK + s + 1].broadcast_to([P, NJ, 256]), ALU.mult).then_inc(sem["scaled_done"], 1)

                    def x1_rstd(t):
                        pool.wait_ge(sem["x1_mv"], NJ * (nM(t) + 1))
                        pool.tensor_scalar(rstd[:, 1, 0, :], mv[:, 1, :, 1], EPS, None, ALU.add).then_inc(sem["x_rstd_tmp"], 1)
                        own[0] += 1
                        pool.wait_ge(sem["x_rstd_tmp"], own[0])
                        pool.tensor_tensor(rstd[:, 1, 1, :], rstd[:, 1, 0, :], minus_half[:, :], ALU.pow).then_inc(sem["x1_rstd_done"], 1)

                    def e_weigh(t, u):
                        pool.wait_ge(sem["router_done"], nM(t) + 1)
                        pool.wait_ge(*wide_read(("expert_in", t, u)))
                        place = act[:, u % 3, :, :]
                        pool.tensor_tensor(place, place, weigh[:, tile_of(u), 2 * pair_of(u):2 * pair_of(u) + 2].unsqueeze(2).broadcast_to([P, 2, HID]),
                                           ALU.mult).then_inc(sem["e_weighed"], 1)

                    own = [0]
                    if load_mod_p is not None:
                        pool.wait_ge(sem["mod_in_p"], 16)
                    walk({"x_rstd": x_rstd, "h_rms": h_rms, "r_gate": r_gate, "r_add": r_add, "du": du,
                          "scaled": scaled, "x1_rstd": x1_rstd, "e_weigh": e_weigh})

                @block.scalar
                def _(ac):
                    def h_square(t, j):
                        ac.wait_ge(sem["h_made"], 2 * (nP(t) + 1))
                        if nP(t):
                            ac.wait_ge(sem["h_rms_done"], nP(t))
                        ac.wait_ge(sem["h_squared"], NJ * nP(t) + j)
                        ac.activation(square[:, :], h_sb[:, j, :], ACT.Square, accum_out=ssq[:, j:j + 1]).then_inc(sem["h_squared"], 1)

                    def h_scale(t, j):
                        ac.wait_ge(sem["h_rms_done"], nP(t) + 1)
                        ac.wait_ge(sem["r_gated"], nP(t) + 1)
                        ac.wait_ge(sem["h_squared"], NJ * nP(t) + j + 1)
                        ac.activation(h_sb[:, j, :], h_sb[:, j, :], ACT.Copy, scale=rms[:, 1, j:j + 1]).then_inc(sem["h_scaled"], 1)

                    def hn_evac(t, k):
                        if slots[t][2] is not None:
                            for j in range(2, NJ):
                                ac.wait_ge(*wide_full(("z", t, j)))
                        ac.wait_ge(*narrow_full(("hn_t", t, k)))
                        ac.activation(hnT[:, slots[t][1][0], k, :], narrow_ps[:, :], ACT.Copy).then_inc(sem["narrow_free"], 1)

                    def xi_center(t, b):
                        key = ("xi", t, b)
                        n = NB * nP(t) + b
                        ac.wait_ge(*wide_full(key))
                        ac.wait_ge(sem["u_made"], max(0, n - 1))
                        ac.wait_ge(sem["r_out"], 16 * (nP(t) + 1))
                        ac.activation(conv[:, b % 2, :], wide_bank(key), ACT.Identity, scale=convw_sb[:, b, CONV - 1:CONV],
                                      bias=convb_sb[:, b:b + 1]).then_inc(sem["xi_centered"], 1)

                    def xi_copy(t, b):
                        key = ("xi", t, b)
                        n = NB * nP(t) + b
                        ac.wait_ge(sem["tapped"], max(0, (CONV - 1) * (n - 1)))
                        ac.wait_ge(sem["halo_saved"], max(0, n - 1))
                        ac.activation(xi_pad[:, b % 2, CONV - 1:], wide_bank(key), ACT.Copy).then_inc(wide_read(key)[0], 1)

                    def u_tanh(t, b):
                        n = NB * nP(t) + b
                        ac.wait_ge(sem["tapped"], (CONV - 1) * (n + 1))
                        ac.wait_ge(sem["u_made"], max(0, n - 1))
                        if nP(t):
                            ac.wait_ge(sem["delta_made"], NB * nP(t))
                        ac.activation(th_p[:, b % 2, :], conv[:, b % 2, :], ACT.Tanh).then_inc(sem["u_tanhed"], 1)

                    def dt_evac(t):
                        ac.wait_ge(sem["u_made"], NB * (nP(t) + 1))
                        ac.wait_ge(*narrow_full(("dt_t", t)))
                        ac.activation(dtT, narrow_ps[0:RANK, :], ACT.Copy).then_inc(sem["narrow_free"], 1)

                    def dt_bias(t, b):
                        key = ("dtp", t, b)
                        ac.wait_ge(*wide_full(key))
                        ac.activation(delta[:, slots[t][1][0], b, :], wide_bank(key), ACT.Identity, bias=dtb_sb[:, b:b + 1]).then_inc(wide_read(key)[0], 1)

                    def soft(t, b):
                        n = NB * nP(t) + b
                        for m in range(NB):
                            ac.wait_ge(*wide_read(("dtp", t, m)))
                        place = soft_place(b)
                        ac.activation(place, delta[:, slots[t][1][0], b, :], ACT.Abs).then_inc(sem["soft_done"], 1)
                        ac.wait_ge(sem["soft_done"], 3 * n + 1)
                        ac.activation(place, place, ACT.Exp, scale=-1.0).then_inc(sem["soft_done"], 1)
                        ac.wait_ge(sem["soft_done"], 3 * n + 2)
                        ac.activation(place, place, ACT.Ln, bias=1.0).then_inc(sem["soft_done"], 1)

                    def du_evac(t, b):
                        ac.wait_ge(*narrow_full(("du_t", t, b)))
                        ac.activation(duT[:, slots[t][1][0], :, b * P:b * P + P],
                                      narrow_ps[:, :].rearrange("p (j n) -> p j n", j=NJ), ACT.Copy).then_inc(sem["narrow_free"], 1)

                    def skip_evac(t, b):
                        if slots[t][2] is not None:
                            ac.wait_ge(*narrow_full(("y_t", t, NJ - 1)))
                        ac.wait_ge(*narrow_full(("skip_t", t, b)))
                        ac.activation(y_sb[:, slots[t][1][0], :, b * P:b * P + P],
                                      narrow_ps[:, :].rearrange("p (j n) -> p j n", j=NJ), ACT.Copy).then_inc(sem["narrow_free"], 1)

                    def exp(t, s, b):
                        n = (NS * nS(t) + s) * NB + b
                        if t > 0 and slots[t - 1][1] is not None:
                            if nP(t):
                                ac.wait_ge(sem["delta_made"], NB * nP(t))
                        ac.wait_ge(sem["rows_full"], max(0, (n // NB - 2) * NJ + NJ))
                        ac.wait_ge(sem["carried"], carries(n // NB - 2))
                        ac.activation(states[:, n % (2 * NB), :], delta[:, slots[t][0][0], b, :], ACT.Exp,
                                      scale=a_sb[:, b, s:s + 1]).then_inc(sem["exp_done"], 1)

                    def z_tanh(t, j):
                        key = ("z", t, j)
                        n = NJ * nM(t) + j
                        ac.wait_ge(*wide_full(key))
                        ac.wait_ge(sem["y_gated"], max(0, n - 1))
                        if nM(t):
                            last = [q for q in range(t) if slots[q][2] is not None][-1]
                            for k in range(NK):
                                ac.wait_ge(*narrow_full(("h2_t", last, k)))
                        ac.activation(zg[:, j % 2, :], wide_bank(key), ACT.Tanh, scale=0.5).then_inc(sem["z_tanhed"], 1)

                    def y_evac(t, j):
                        n = NJ * nM(t) + j
                        ac.wait_ge(*narrow_full(("y_t", t, j)))
                        if n >= 2:
                            ac.wait_ge(*wide_full(op_key(n - 2)))
                        ac.activation(yT[:, j % 2, :, :], narrow_ps[:, :].rearrange("p (b n) -> p b n", b=NB), ACT.Copy).then_inc(sem["narrow_free"], 1)

                    def op_key(n):
                        tt = [q for q in range(len(slots)) if slots[q][2] is not None][n // NJ]
                        return ("op", tt, n % NJ)

                    def h2_evac(t, k):
                        ac.wait_ge(*narrow_full(("h2_t", t, k)))
                        if nM(t):
                            last = [n for n in range(t) if slots[n][2] is not None][-1]
                            ac.wait_ge(*wide_full(("expert_in", last, UNITS - 1)))
                            ac.wait_ge(*wide_full(("expert_in", last, UNITS - 2)))
                        ac.activation(h2T[:, k, :], narrow_ps[:, :], ACT.Copy).then_inc(sem["narrow_free"], 1)

                    def logit_exp(t):
                        key = ("logit", t)
                        ac.wait_ge(*wide_full(key))
                        if nM(t):
                            ac.wait_ge(sem["router_done"], nM(t))
                        ac.activation(g_sb[:, :, :], wide_bank(key)[:, 0:NJ * NE].rearrange("p (j e) -> p j e", j=NJ), ACT.Exp, scale=-1.0).then_inc(wide_read(key)[0], 1)

                    def e_tanh(t, u):
                        key = ("expert_in", t, u)
                        n = UNITS * nM(t) + u
                        ac.wait_ge(*wide_full(key))
                        if n >= 3:
                            ac.wait_ge(*narrow_full(unit_key("e_t", n - 3)))
                        hin = wide_bank(key).rearrange("p (e a h) -> p e a h", e=2, a=2)[:, :, 0, :]
                        ac.activation(act[:, u % 3, :, :], hin, ACT.Tanh, scale=0.5).then_inc(sem["e_tanhed"], 1)

                    def unit_key(name, n):
                        tt = [t for t in range(len(slots)) if slots[t][2] is not None][n // UNITS]
                        return (name, tt, n % UNITS)

                    def e_evac(t, u):
                        n = UNITS * nM(t) + u
                        ac.wait_ge(*narrow_full(("e_t", t, u)))
                        ac.wait_ge(sem["expert_out_done"], max(0, n - 1))
                        ac.activation(hidT[:, u % 2, :, :], narrow_ps[:, 0:2 * P].rearrange("p (e n) -> p e n", e=2), ACT.Copy).then_inc(sem["narrow_free"], 1)

                    def carries(step):
                        halves = (t for t in range(len(slots)) if slots[t][0] is not None and slots[t][0][0] == 0)
                        return sum(max(0, min(NS, step + 1 - NS * nS(t))) for t in halves)

                    walk({"h_square": h_square, "h_scale": h_scale, "hn_evac": hn_evac, "xi_center": xi_center,
                          "xi_copy": xi_copy, "u_tanh": u_tanh, "dt_evac": dt_evac, "dt_bias": dt_bias, "soft": soft,
                          "du_evac": du_evac, "skip_evac": skip_evac, "exp": exp, "z_tanh": z_tanh, "y_evac": y_evac,
                          "h2_evac": h2_evac, "logit_exp": logit_exp, "e_tanh": e_tanh, "e_evac": e_evac})

                @block.vector
                def _(v):
                    def x_stat(t, j):
                        v.wait_ge(sem["x_in"], 16 * (nP(t) + 1))
                        if nP(t):
                            v.wait_ge(sem["x_norm_done"], NJ * nP(t))
                        v.bn_stats(bn[:, 0, j, :], x_sb[:, j, :]).then_inc(sem["x_bn"], 1)
                        v.wait_ge(sem["x_bn"], NJ * nP(t) + j + 1)
                        v.bn_aggr(mv[:, 0, j, :], bn[:, 0, j, :]).then_inc(sem["x_mv"], 1)

                    def x_norm(t, j):
                        v.wait_ge(sem["x_rstd_done"], nP(t) + 1)
                        if nP(t):
                            last = [n for n in range(t) if slots[n][1] is not None][-1]
                            v.wait_ge(*narrow_full(("hn_t", last, NK - 1)))
                        v.tensor_scalar(h_sb[:, j, :], x_sb[:, j, :], mv[:, 0, j, 0:1], rstd[:, 0, 1, j:j + 1],
                                        ALU.subtract, ALU.mult).then_inc(sem["x_norm_done"], 1)

                    def x_scale(t):
                        if load_mod_p is not None:
                            v.wait_ge(sem["mod_in_p"], 16)
                        v.wait_ge(sem["x_norm_done"], NJ * (nP(t) + 1))
                        v.tensor_tensor(h_sb[:, :, :], h_sb[:, :, :], mod_p[:, 1:2, :].broadcast_to([P, NJ, DM]), ALU.mult).then_inc(sem["h_made"], 1)

                    def x_shift(t):
                        v.wait_ge(sem["h_made"], 2 * nP(t) + 1)
                        v.tensor_tensor(h_sb[:, :, :], h_sb[:, :, :], mod_p[:, 0:1, :].broadcast_to([P, NJ, DM]), ALU.add).then_inc(sem["h_made"], 1)

                    def halo(t, b):
                        n = NB * nP(t) + b
                        par = slots[t][1][0]
                        v.wait_ge(sem["tapped"], max(0, (CONV - 1) * (n - 1)))
                        v.wait_ge(sem["halo_saved"], max(0, n - 1))
                        if par == 0:
                            v.memset(xi_pad[:, b % 2, 0:CONV - 1], 0.0).then_inc(sem["halo_set"], 1)
                        else:
                            if nP(t):
                                v.wait_ge(sem["halo_saved"], NB * nP(t))
                            v.tensor_copy(xi_pad[:, b % 2, 0:CONV - 1], halo_sb[:, b, :]).then_inc(sem["halo_set"], 1)
                        v.wait_ge(sem["halo_set"], n + 1)
                        v.wait_ge(*wide_read(("xi", t, b)))
                        v.tensor_copy(halo_sb[:, b, :], xi_pad[:, b % 2, CH:CH + CONV - 1]).then_inc(sem["halo_saved"], 1)

                    def tap(t, b, k):
                        n = NB * nP(t) + b
                        v.wait_ge(sem["xi_centered"], n + 1)
                        v.wait_ge(sem["tapped"], (CONV - 1) * n + k)
                        place = conv[:, b % 2, :]
                        v.scalar_tensor_tensor(place, xi_pad[:, b % 2, k:k + CH], convw_sb[:, b, k:k + 1], place, ALU.mult, ALU.add).then_inc(sem["tapped"], 1)

                    def u(t, b):
                        n = NB * nP(t) + b
                        v.wait_ge(sem["u_tanhed"], n + 1)
                        if nP(t):
                            last = [q for q in range(t) if slots[q][1] is not None][-1]
                            v.wait_ge(*narrow_full(("skip_t", last, NB - 1)))
                        v.scalar_tensor_tensor(u_sb[:, b, :], th_p[:, b % 2, :], 1.0, conv[:, b % 2, :], ALU.add, ALU.mult).then_inc(sem["u_made"], 1)

                    def xd_evac(t):
                        key = ("xd", t)
                        v.wait_ge(*wide_full(key))
                        v.tensor_copy(xd_sb[:, slots[t][1][0], :, :], wide_bank(key)[:, 0:NJ * XD].rearrange("p (j n) -> p j n", j=NJ)).then_inc(wide_read(key)[0], 1)

                    def delta_(t, b):
                        n = NB * nP(t) + b
                        v.wait_ge(sem["soft_done"], 3 * (n + 1))
                        place = delta[:, slots[t][1][0], b, :]
                        v.scalar_tensor_tensor(place, place, 0.0, soft_place(b), ALU.max, ALU.add).then_inc(sem["delta_made"], 1)

                    def skip(t, b):
                        n = NB * nP(t) + b
                        v.wait_ge(sem["du_made"], n + 1)
                        v.tensor_scalar(u_sb[:, b, :], u_sb[:, b, :], skip_sb[:, b:b + 1], None, ALU.mult).then_inc(sem["skip_made"], 1)

                    def scan(t, s, b):
                        n = (NS * nS(t) + s) * NB + b
                        par = slots[t][0][0]
                        v.wait_ge(sem["exp_done"], n + 1)
                        v.wait_ge(sem["cols_full"], n + 1)
                        first = 0.0
                        if par == 1:
                            first = carry[:, s, b:b + 1]
                            if t > 0:
                                v.wait_ge(sem["carried"], carries_before(t))
                        place = states[:, n % (2 * NB), :]
                        v.tensor_tensor_scan(place, place, cols_ps[n % 2][:, :], first, ALU.mult, ALU.add).then_inc(sem["scan_done"], 1)

                    def carries_before(t):
                        return NS * sum(slots[q][0] is not None and slots[q][0][0] == 0 for q in range(t))

                    def carry_(t, s):
                        if slots[t][0][0] == 1:
                            return
                        n = NS * nS(t) + s
                        v.wait_ge(sem["scan_done"], NB * (n + 1))
                        at = n % 2 * NB
                        v.tensor_copy(carry[:, s, :], states[:, at:at + NB, CH - 1]).then_inc(sem["carried"], 1)

                    def gather(t, s, j):
                        n = (NS * nS(t) + s) * NJ + j
                        par = slots[t][0][0]
                        v.wait_ge(sem["rows_full"], n + 1)
                        v.wait_ge(sem["gathered"], max(0, n - NJ + 1))
                        if s == 0 and t > 0 and slots[t - 1][1] is not None:
                            v.wait_ge(*narrow_read(("skip_t", t - 1, NB - 1)))
                        place = y_sb[:, par, j, :]
                        v.scalar_tensor_tensor(place, rows_ps[n % 2][:, :], xd_sb[:, par, j, RANK + NS + s:RANK + NS + s + 1], place,
                                               ALU.mult, ALU.add).then_inc(sem["gathered"], 1)

                    def z_gate(t, j):
                        key = ("z", t, j)
                        v.wait_ge(sem["z_tanhed"], NJ * nM(t) + j + 1)
                        place = zg[:, j % 2, :]
                        v.scalar_tensor_tensor(place, place, 1.0, wide_bank(key), ALU.add, ALU.mult).then_inc(wide_read(key)[0], 1)

                    def y_gate(t, j):
                        v.wait_ge(*wide_read(("z", t, j)))
                        if nS(t):
                            v.wait_ge(sem["gathered"], nS(t) * NS * NJ)
                        place = y_sb[:, slots[t][2][0], j, :]
                        v.tensor_tensor(place, place, zg[:, j % 2, :], ALU.mult).then_inc(sem["y_gated"], 1)

                    def op_gate(t, j):
                        key = ("op", t, j)
                        v.wait_ge(*wide_full(key))
                        if load_mod_m is not None:
                            v.wait_ge(sem["mod_in_m"], 16)
                        v.wait_ge(sem["x1_made"], max(0, NJ * nM(t) + j - 1))
                        v.tensor_tensor(gated[:, j % 2, :], wide_bank(key)[:, 0:DM], mod_m[:, 0, :], ALU.mult).then_inc(wide_read(key)[0], 1)

                    def x1_(t, j):
                        v.wait_ge(*wide_read(("op", t, j)))
                        v.wait_ge(sem["r_in"], 16 * (nM(t) + 1))
                        v.tensor_tensor(x1[:, j, :], x1[:, j, :], gated[:, j % 2, :], ALU.add).then_inc(sem["x1_made"], 1)

                    def x1_stat(t, j):
                        v.wait_ge(sem["x1_made"], NJ * nM(t) + j + 1)
                        if nM(t):
                            v.wait_ge(sem["x1_normed"], NJ * nM(t))
                        v.bn_stats(bn[:, 1, j, :], x1[:, j, :]).then_inc(sem["x1_bn"], 1)
                        v.wait_ge(sem["x1_bn"], NJ * nM(t) + j + 1)
                        v.bn_aggr(mv[:, 1, j, :], bn[:, 1, j, :]).then_inc(sem["x1_mv"], 1)

                    def x1_norm(t, j):
                        v.wait_ge(sem["x1_rstd_done"], nM(t) + 1)
                        v.wait_ge(sem["y_gated"], NJ * (nM(t) + 1))
                        if nM(t):
                            last = [n for n in range(t) if slots[n][2] is not None][-1]
                            v.wait_ge(*narrow_full(("h2_t", last, NK - 1)))
                        v.tensor_scalar(h2[:, j, :], x1[:, j, :], mv[:, 1, j, 0:1], rstd[:, 1, 1, j:j + 1],
                                        ALU.subtract, ALU.mult).then_inc(sem["x1_normed"], 1)

                    def x1_scale(t):
                        v.wait_ge(sem["x1_normed"], NJ * (nM(t) + 1))
                        v.tensor_tensor(h2[:, :, :], h2[:, :, :], mod_m[:, 2:3, :].broadcast_to([P, NJ, DM]), ALU.mult).then_inc(sem["h2_made"], 1)

                    def x1_shift(t):
                        v.wait_ge(sem["h2_made"], 2 * nM(t) + 1)
                        v.tensor_tensor(h2[:, :, :], h2[:, :, :], mod_m[:, 1:2, :].broadcast_to([P, NJ, DM]), ALU.add).then_inc(sem["h2_made"], 1)

                    def router(t):
                        def done(instruction):
                            own[0] += 1
                            instruction.then_inc(sem["router_step"], 1)
                            v.wait_ge(sem["router_step"], own[0])

                        above, equal, rank, g = rt[0], rt[1], rt[2], rt[3]
                        count, total = rt_small
                        v.wait_ge(*wide_read(("logit", t)))
                        done(v.tensor_scalar(g_sb[:, :, :], g_sb[:, :, :], 1.0, None, ALU.add))
                        done(v.reciprocal(g[:, :, :], g_sb[:, :, :]))
                        for j in range(NJ):
                            last = v.max(top[:, j, :], g[:, j, :])
                            if j < NJ - 1:
                                last.then_inc(sem["router_step"], 1)
                                own[0] += 1
                        done(last)
                        fourth = top[:, :, TOPK - 1:TOPK].broadcast_to([P, NJ, NE])
                        done(v.tensor_tensor(above[:, :, :], g[:, :, :], fourth, ALU.is_gt))
                        done(v.tensor_tensor(equal[:, :, :], g[:, :, :], fourth, ALU.is_equal))
                        done(v.reduce_sum(count[:, :], above[:, :, :], axis=AX.X))
                        done(v.tensor_tensor_scan(rank[:, :, :].rearrange("p j e -> p (j e)"), restart[:, :, :].rearrange("p j e -> p (j e)"),
                                                  equal[:, :, :].rearrange("p j e -> p (j e)"), 0.0, ALU.mult, ALU.add))
                        done(v.tensor_tensor(rank[:, :, :], rank[:, :, :], count[:, :].unsqueeze(2).broadcast_to([P, NJ, NE]), ALU.add))
                        done(v.tensor_scalar(rank[:, :, :], rank[:, :, :], TOPK + 0.5, None, ALU.is_lt))
                        done(v.tensor_tensor(equal[:, :, :], equal[:, :, :], rank[:, :, :], ALU.mult))
                        done(v.tensor_tensor(above[:, :, :], above[:, :, :], equal[:, :, :], ALU.add))
                        done(v.tensor_tensor(g[:, :, :], g[:, :, :], above[:, :, :], ALU.mult))
                        done(v.reduce_sum(total[:, :], g[:, :, :], axis=AX.X))
                        done(v.reciprocal(total[:, :], total[:, :]))
                        if nM(t):
                            v.wait_ge(sem["e_weighed"], UNITS * nM(t))
                        v.scalar_tensor_tensor(weigh[:, :, 0:NE], g[:, :, :], 0.5, total[:, :].unsqueeze(2).broadcast_to([P, NJ, NE]),
                                               ALU.mult, ALU.mult).then_inc(sem["router_done"], 1)

                    def e_act(t, u):
                        key = ("expert_in", t, u)
                        v.wait_ge(sem["e_tanhed"], UNITS * nM(t) + u + 1)
                        place = act[:, u % 3, :, :]
                        hin = wide_bank(key).rearrange("p (e a h) -> p e a h", e=2, a=2)[:, :, 0, :]
                        v.scalar_tensor_tensor(place, place, 1.0, hin, ALU.add, ALU.mult).then_inc(sem["e_acted"], 1)

                    def e_mul(t, u):
                        key = ("expert_in", t, u)
                        v.wait_ge(sem["e_acted"], UNITS * nM(t) + u + 1)
                        place = act[:, u % 3, :, :]
                        vin = wide_bank(key).rearrange("p (e a h) -> p e a h", e=2, a=2)[:, :, 1, :]
                        v.tensor_tensor(place, place, vin, ALU.mult).then_inc(wide_read(key)[0], 1)

                    def out_gate(t, q):
                        n = 2 * nM(t) + q
                        v.wait_ge(sem["expert_out_done"], UNITS * nM(t) + 2 * NPAIR * (q + 1))
                        v.wait_ge(sem["out_added"], n)
                        v.tensor_tensor(gated[:, :, :], moe_ps[:, :, :], mod_m[:, 3:4, :].broadcast_to([P, 2, DM]), ALU.mult).then_inc(sem["out_gated"], 1)

                    def out_add(t, q):
                        v.wait_ge(sem["out_gated"], 2 * nM(t) + q + 1)
                        place = x1[:, 2 * q:2 * q + 2, :]
                        v.tensor_tensor(place, place, gated[:, :, :], ALU.add).then_inc(sem["out_added"], 1)

                    own = [0]
                    walk({"x_stat": x_stat, "x_norm": x_norm, "x_scale": x_scale, "x_shift": x_shift, "halo": halo, "tap": tap,
                          "u": u, "xd_evac": xd_evac, "delta": delta_, "skip": skip, "scan": scan, "carry": carry_, "gather": gather,
                          "z_gate": z_gate, "y_gate": y_gate, "op_gate": op_gate, "x1": x1_, "x1_stat": x1_stat, "x1_norm": x1_norm,
                          "x1_scale": x1_scale, "x1_shift": x1_shift, "router": router, "e_act": e_act, "e_mul": e_mul,
                          "out_gate": out_gate, "out_add": out_add})

                @block.tensor
                def _(pe):
                    def hn_t(t, k):
                        pe.wait_ge(sem["h_scaled"], NJ * (nP(t) + 1))
                        pe.wait_ge(*narrow_room(("hn_t", t, k)))
                        for n in range(NJ):
                            last = pe.transpose(narrow_ps[:, n * P:n * P + P], h_sb[:, n, k * P:k * P + P], ident[:, :])
                        last.then_inc(sem["narrow_full"], 1)

                    def xi(t, b):
                        key = ("xi", t, b)
                        pe.wait_ge(*narrow_read(("hn_t", t, NK - 1)))
                        pe.wait_ge(*wide_room(key))
                        for k in range(NK):
                            last = pe.matmul(wide_bank(key)[:, :], in_sb[:, k, b * P:b * P + P], hnT[:, slots[t][1][0], k, :],
                                             start=(k == 0), stop=(k == NK - 1))
                        last.then_inc(wide_full(key)[0], 1)

                    def xd(t):
                        key = ("xd", t)
                        pe.wait_ge(sem["u_made"], NB * (nP(t) + 1))
                        pe.wait_ge(*wide_room(key))
                        for j in range(NJ):
                            for b in range(NB):
                                last = pe.matmul(wide_bank(key)[:, j * XD:j * XD + XD], u_sb[:, b, j * P:j * P + P], xproj_sb[:, b, :],
                                                 start=(b == 0), stop=(b == NB - 1))
                        last.then_inc(wide_full(key)[0], 1)

                    def dt_t(t):
                        pe.wait_ge(*wide_read(("xd", t)))
                        pe.wait_ge(*narrow_room(("dt_t", t)))
                        for n in range(NJ):
                            last = pe.transpose(narrow_ps[0:RANK, n * P:n * P + P], xd_sb[:, slots[t][1][0], n, 0:RANK], ident[:, :])
                        last.then_inc(sem["narrow_full"], 1)

                    def dtp(t, b):
                        key = ("dtp", t, b)
                        pe.wait_ge(*narrow_read(("dt_t", t)))
                        pe.wait_ge(*wide_room(key))
                        pe.matmul(wide_bank(key)[:, :], dtw_sb[:, b * P:b * P + P], dtT[:, :], start=True, stop=True).then_inc(wide_full(key)[0], 1)

                    def skip_t(t, b):
                        pe.wait_ge(sem["skip_made"], NB * nP(t) + b + 1)
                        pe.wait_ge(*narrow_room(("skip_t", t, b)))
                        for n in range(NJ):
                            last = pe.transpose(narrow_ps[:, n * P:n * P + P], u_sb[:, b, n * P:n * P + P], ident[:, :])
                        last.then_inc(sem["narrow_full"], 1)

                    def du_t(t, b):
                        pe.wait_ge(sem["du_made"], NB * nP(t) + b + 1)
                        pe.wait_ge(*narrow_room(("du_t", t, b)))
                        for n in range(NJ):
                            last = pe.transpose(narrow_ps[:, n * P:n * P + P], du_sb[:, b % 2, n * P:n * P + P], ident[:, :])
                        last.then_inc(sem["narrow_full"], 1)

                    def cols(t, s, b):
                        n = (NS * nS(t) + s) * NB + b
                        pe.wait_ge(sem["scaled_done"], n // 2 + 1)
                        pe.wait_ge(sem["scan_done"], max(0, n - 1))
                        for j in range(NJ):
                            last = pe.transpose(cols_ps[n % 2][:, j * P:j * P + P], dub[:, n // 2 % 3, j, b % 2 * P:b % 2 * P + P], ident[:, :])
                        last.then_inc(sem["cols_full"], 1)

                    def rows(t, s, j):
                        n = (NS * nS(t) + s) * NJ + j
                        pe.wait_ge(sem["scan_done"], (n // NJ + 1) * NB)
                        pe.wait_ge(sem["gathered"], max(0, n - 1))
                        for b in range(NB):
                            place = states[:, n // NJ % 2 * NB + b, j * P:j * P + P]
                            last = pe.transpose(rows_ps[n % 2][:, b * P:b * P + P], place, ident[:, :])
                        last.then_inc(sem["rows_full"], 1)

                    def z(t, j):
                        key = ("z", t, j)
                        pe.wait_ge(*wide_room(key))
                        for k in range(NK):
                            last = pe.matmul(wide_bank(key)[:, :], hnT[:, slots[t][2][0], k, j * P:j * P + P], in_sb[:, k, DI:2 * DI],
                                             start=(k == 0), stop=(k == NK - 1))
                        last.then_inc(wide_full(key)[0], 1)

                    def y_t(t, j):
                        pe.wait_ge(sem["y_gated"], NJ * nM(t) + j + 1)
                        pe.wait_ge(*narrow_room(("y_t", t, j)))
                        for n in range(NB):
                            last = pe.transpose(narrow_ps[:, n * P:n * P + P], y_sb[:, slots[t][2][0], j, n * P:n * P + P], ident[:, :])
                        last.then_inc(sem["narrow_full"], 1)

                    def op(t, j):
                        key = ("op", t, j)
                        pe.wait_ge(*narrow_read(("y_t", t, j)))
                        pe.wait_ge(*wide_room(key))
                        for b in range(NB):
                            last = pe.matmul(wide_bank(key)[:, 0:DM], yT[:, j % 2, b, :], out_sb[:, b, :], start=(b == 0), stop=(b == NB - 1))
                        last.then_inc(wide_full(key)[0], 1)

                    def h2_t(t, k):
                        pe.wait_ge(sem["h2_made"], 2 * (nM(t) + 1))
                        pe.wait_ge(*narrow_room(("h2_t", t, k)))
                        for n in range(NJ):
                            last = pe.transpose(narrow_ps[:, n * P:n * P + P], h2[:, n, k * P:k * P + P], ident[:, :])
                        last.then_inc(sem["narrow_full"], 1)

                    def logit(t):
                        key = ("logit", t)
                        pe.wait_ge(*narrow_read(("h2_t", t, NK - 1)))
                        pe.wait_ge(*wide_room(key))
                        for j in range(NJ):
                            for k in range(NK):
                                last = pe.matmul(wide_bank(key)[:, j * NE:j * NE + NE], h2T[:, k, j * P:j * P + P], gate_sb[:, k, :],
                                                 start=(k == 0), stop=(k == NK - 1))
                        last.then_inc(wide_full(key)[0], 1)

                    def expert_in(t, u):
                        key = ("expert_in", t, u)
                        j = tile_of(u)
                        pe.wait_ge(*wide_room(key))
                        for k in range(NK):
                            last = pe.matmul(wide_bank(key)[:, :], h2T[:, k, j * P:j * P + P], ein_sb[:, k, pair_of(u), :],
                                             start=(k == 0), stop=(k == NK - 1))
                        last.then_inc(wide_full(key)[0], 1)

                    def e_t(t, u):
                        pe.wait_ge(sem["e_weighed"], UNITS * nM(t) + u + 1)
                        pe.wait_ge(*narrow_room(("e_t", t, u)))
                        for n in range(2):
                            last = pe.transpose(narrow_ps[:, n * P:n * P + P], act[:, u % 3, n, :], ident[:, :])
                        last.then_inc(sem["narrow_full"], 1)

                    def expert_out(t, u):
                        pe.wait_ge(*narrow_read(("e_t", t, u)))
                        first = u % (2 * NPAIR) == 0
                        if first:
                            pe.wait_ge(sem["out_gated"], 2 * nM(t) + u // (2 * NPAIR))
                        for n in range(2):
                            last = pe.matmul(moe_ps[:, u % 2, :], hidT[:, u % 2, n, :], eout_sb[:, 2 * pair_of(u) + n, :],
                                             start=first and n == 0, stop=pair_of(u) == NPAIR - 1 and n == 1, skip_group_check=True)
                        last.then_inc(sem["expert_out_done"], 1)

                    walk({"hn_t": hn_t, "xi": xi, "xd": xd, "dt_t": dt_t, "dtp": dtp, "skip_t": skip_t, "du_t": du_t,
                          "cols": cols, "rows": rows, "z": z, "y_t": y_t, "op": op, "h2_t": h2_t, "logit": logit,
                          "expert_in": expert_in, "e_t": e_t, "expert_out": expert_out})
            clear_semaphores()

        run_slots([(None, (0, 0), None), ((0, 0), (1, 1), None)], load_mod_p=0)
        with nc.Fori(0, BATCH - 1) as i:
            run_slots([((1, 2 * i + 1), (0, 2 * i + 2), (0, 2 * i)), ((0, 2 * i + 2), (1, 2 * i + 3), (1, 2 * i + 1))],
                      load_mod_p=i + 1, load_mod_m=i)
        run_slots([((1, NC - 1), None, (0, NC - 2)), (None, None, (1, NC - 1))], load_mod_m=BATCH - 1)


_INS = ("x", "norm_w", "in_w", "conv_w", "conv_b", "xproj_w", "dt_w", "dt_b", "a_log", "d_skip", "out_w",
        "gate_w", "e_in", "e_out", "c_t", "w_mod")


def kernel(L0_attn_x, L0_attn_norm_w, L0_attn_in_proj_w, L0_attn_conv_w, L0_attn_conv_b, L0_attn_x_proj_w,
           L0_attn_dt_proj_w, L0_attn_dt_proj_b, L0_attn_A_log, L0_attn_D, L0_attn_out_proj_w, L0_ffn_gate_w,
           L0_ffn_ws_in, L0_ffn_vs_in, L0_ffn_ws_out, L0_ffn_e_win, L0_ffn_e_vin, L0_ffn_e_wout, L0_c, L0_wmod):
    import concourse.bacc as bacc
    from concourse.bass_utils import run_bass_kernel_spmd

    def blocks(w):
        return np.ascontiguousarray(w.reshape(-1, P, w.shape[-1]).transpose(1, 0, 2))

    def chunks(a):
        return np.ascontiguousarray(a.reshape(NC, NJ, P, DM).transpose(0, 2, 1, 3))

    a = {k: np.asarray(v) for k, v in locals().items() if k.startswith("L0_")}
    win = np.concatenate([a["L0_ffn_e_win"], a["L0_ffn_ws_in"].reshape(DM, 2, HID).transpose(1, 0, 2)], 0)
    vin = np.concatenate([a["L0_ffn_e_vin"], a["L0_ffn_vs_in"].reshape(DM, 2, HID).transpose(1, 0, 2)], 0)
    e_in = np.concatenate([win, vin], 2)
    e_in = e_in.reshape(NPAIR, 2, NK, P, 2 * HID).transpose(3, 2, 0, 1, 4).reshape(P, NK, NPAIR, 4 * HID)
    e_out = np.concatenate([a["L0_ffn_e_wout"], a["L0_ffn_ws_out"].reshape(2, HID, DM)], 0).transpose(1, 0, 2)
    arrays = {
        "x": chunks(a["L0_attn_x"]),
        "norm_w": a["L0_attn_norm_w"].reshape(NK, P).T,
        "in_w": blocks(a["L0_attn_in_proj_w"].T),
        "conv_w": blocks(a["L0_attn_conv_w"]),
        "conv_b": a["L0_attn_conv_b"].reshape(NB, P).T,
        "xproj_w": blocks(a["L0_attn_x_proj_w"].T),
        "dt_w": a["L0_attn_dt_proj_w"].T,
        "dt_b": a["L0_attn_dt_proj_b"].reshape(NB, P).T,
        "a_log": blocks(a["L0_attn_A_log"]),
        "d_skip": a["L0_attn_D"].reshape(NB, P).T,
        "out_w": blocks(a["L0_attn_out_proj_w"].T),
        "gate_w": blocks(a["L0_ffn_gate_w"].T),
        "e_in": e_in,
        "e_out": e_out,
        "c_t": blocks(a["L0_c"].T),
        "w_mod": blocks(a["L0_wmod"]),
    }
    nc = bacc.Bacc("TRN2", target_bir_lowering=False, num_devices=1, dynamic_dma_scratch_size=1024)
    feed, args = {}, []
    for name in _INS:
        value = np.ascontiguousarray(arrays[name])
        feed[name + "_dram"] = value
        args.append(nc.dram_tensor(name + "_dram", value.shape, mybir.dt.from_np(value.dtype), kind="ExternalInput").ap())
    out = nc.dram_tensor("out_dram", (NC, P, NJ, DM), F32, kind="ExternalOutput").ap()
    adaln_block(nc, *args, out)
    r = run_bass_kernel_spmd(nc, [feed], core_ids=[0])
    got = r.results[0]["out_dram"]
    return np.ascontiguousarray(got.transpose(0, 2, 1, 3)).reshape(BATCH, SEQ, DM)
```

```python
from contextlib import ExitStack

import numpy as np

import concourse.bass as bass
from concourse import mybir

F32 = mybir.dt.float32
F16 = mybir.dt.float16
ALU = mybir.AluOpType
ACT = mybir.ActivationFunctionType
AX = mybir.AxisListType

BATCH, SEQ, DM = 8, 1024, 256
DI, NS, CONV, RANK = 512, 16, 4, 16
NE, TOPK, HID = 16, 4, 128
P = 128
CH = 512
NJ = CH // P
NC = BATCH * SEQ // CH
NB = DI // P
NK = DM // P
XD = RANK + 3 * NS
AT_C = RANK + 2 * NS
NBT = RANK + 2 * NS
LIFT = 64.0
NPAIR = NE // 2 + 1
UNITS = NPAIR * NJ
EPS = 1e-5



def scan_steps(t):
    out = []
    for s in range(NS):
        out += [(4 * s - 5.2, ("b_cast", t, s)), (4 * s - 5.1, ("b_evac", t, s))]
        for b in range(NB):
            out += [(4 * s - 3.75 + b, ("scaled", t, s, b)), (4 * s - 1.75 + b, ("exp", t, s, b)), (4 * s + b + 0.2, ("scan", t, s, b))]
        for j in range(NJ):
            at = 4 * s + 4 + 0.5 * j
            out += [(at + 0.11, ("rows", t, s, j)), (at + 0.21, ("gather", t, s, j))] if j < NJ - 1 else \
                   [(at + 0.11, ("rows", t, s, j)), (at + 0.21, ("c_scale", t, s)), (at + 0.31, ("c_add", t, s))]
        out.append((4 * s + 3.25, ("carry", t, s)))
    return out


def prepare_steps(t):
    out = [(0, ("x_load", t))]
    for j in range(NJ):
        out.append((1 + 0.5 * j, ("x_stat", t, j)))
    out += [(3.5, ("x_rstd", t))] + [(4.5 + 0.3 * j, ("x_norm", t, j)) for j in range(NJ)]
    out += [(6, ("x_scale", t)), (7, ("x_shift", t))]
    out += [(8 + 0.3 * j, ("h_square", t, j)) for j in range(NJ)]
    out += [(10, ("h_rms", t)), (10.5, ("r_gate", t)), (11.5, ("r_add", t)), (11.6, ("r_store", t))]
    for j in range(NJ):
        out.append((12.5 + 0.4 * j, ("h_scale", t, j)))
    for k in range(NK):
        out += [(14.5 + 2 * k, ("hn_t", t, k)), (14.6 + 2 * k, ("hn_high", t, k)), (14.7 + 2 * k, ("hn_low", t, k))]
    for b in range(NB):
        at = 19 + 3.2 * b
        out += [(at, ("xi", t, b)), (at + 0.1, ("xi_center", t, b)), (at + 0.2, ("xi_copy", t, b)),
                (at + 0.3, ("halo", t, b))]
        out += [(at + 0.8 + 0.6 * n, ("tap", t, b, n)) for n in range(CONV - 1)]
        out += [(at + 2.7, ("u_tanh", t, b)), (at + 3.5, ("u", t, b))]
    out += [(33.5, ("xd", t)), (34, ("xd_evac", t))]
    out += [(35, ("xd_t", t)), (35.1, ("xd_t_evac", t)), (35.2, ("b_high", t)), (35.3, ("b_low", t))]
    for b in range(NB):
        out += [(38 + 0.8 * b, ("dtp", t, b)), (38.2 + 0.8 * b, ("dt_bias", t, b))]
        out += [(42.5 + b, ("delta", t, b)), (44 + 2 * b, ("du", t, b)),
                (45.5 + 2 * b, ("skip", t, b))]
        out += [(46.8 + 2 * b, ("skip_t", t, b)), (46.9 + 2 * b, ("skip_evac", t, b))]
    out += [(42 + 0.01 * n, (("soft_exp", "soft_ln")[n // 2], t, n % 2)) for n in range(4)]
    return out


def mix_steps(t):
    out = [(-0.9, ("r_load", t))]
    for j in range(NJ):
        at = -0.8 + j
        out += [(at, ("z", t, j)), (at + 0.1, ("z_tanh", t, j)), (at + 0.3, ("z_gate", t, j)), (at + 0.95, ("y_gate", t, j))]
        out += [(at + 1.5, ("y_t", t, j)), (at + 1.55, ("y_evac", t, j))]
        out += [(at + 2.5, ("op", t, j)), (at + 2.6, ("op_gate", t, j)), (at + 2.7, ("x1", t, j)), (at + 2.8, ("x1_stat", t, j))]
    out += [(6.2, ("x1_rstd", t))] + [(6.9 + 0.2 * j, ("x1_norm", t, j)) for j in range(NJ)]
    out += [(7.8, ("x1_scale", t)), (8.2, ("x1_shift", t))]
    for k in range(NK):
        out += [(9 + k, ("h2_t", t, k)), (9.1 + k, ("h2_high", t, k)), (9.2 + k, ("h2_low", t, k))]
    out += [(11.2, ("logit", t)), (11.3, ("logit_exp", t)), (11.8, ("router", t))]
    first, tick = 12.0, 51.0 / UNITS
    for u in range(UNITS):
        at = first + tick * u
        out += [(at, ("expert_in", t, u)), (at + 0.1, ("e_tanh", t, u)), (at + 0.3, ("e_act", t, u)),
                (at + 0.4, ("e_mul", t, u)), (at + 0.5, ("e_weigh", t, u)),
                (at + 0.7 + tick, ("e_t", t, u)), (at + 0.8 + tick, ("e_evac", t, u)),
                (at + 0.6 + 2 * tick, ("expert_out", t, u))]
        if u % (2 * NPAIR) == 2 * NPAIR - 1:
            out += [(at + 0.65 + 2 * tick, ("out_gate", t, u // (2 * NPAIR))), (at + 0.66 + 2 * tick, ("out_add", t, u // (2 * NPAIR))),
                    (at + 0.67 + 2 * tick, ("out_store", t, u // (2 * NPAIR)))]
    return out


SLOT = 4 * NS + 2.0


def schedule(slots):
    out = []
    for t, (s, p, m) in enumerate(slots):
        steps = []
        if s is not None:
            steps += scan_steps(t)
        if p is not None:
            steps += prepare_steps(t)
        if m is not None:
            steps += mix_steps(t)
        out += [(SLOT * t + at, t, n, what) for n, (at, what) in enumerate(steps)]
    order = [what for _, _, _, what in sorted(out, key=lambda x: (x[0], x[1], x[2]))]
    placed, done, filled = [], set(), {"wide": [], "narrow": []}
    for what in order:
        if what in done:
            continue
        ring, depth = ("wide", 2) if what[0] in WIDE else ("narrow", 1) if what[0] in NARROW else (None, 0)
        if ring:
            if len(filled[ring]) >= depth:
                old = filled[ring][-depth]
                for reader in (WIDE if ring == "wide" else NARROW)[old[0]]:
                    if (reader, *old[1:]) not in done:
                        done.add((reader, *old[1:]))
                        placed.append((reader, *old[1:]))
            filled[ring].append(what)
        done.add(what)
        placed.append(what)
    return placed


SPLIT = [(k, first, second) for k in range(NK) for first, second in ((0, 0), (0, 1), (1, 0))]

WIDE = {"xi": ("xi_center", "xi_copy"), "xd": ("xd_evac",), "dtp": ("dt_bias",), "z": ("z_tanh", "z_gate"),
        "op": ("op_gate",), "logit": ("logit_exp",), "expert_in": ("e_tanh", "e_act", "e_mul"), "b_cast": ("b_evac",)}
NARROW = {"hn_t": ("hn_high", "hn_low"), "xd_t": ("xd_t_evac", "b_high"), "skip_t": ("skip_evac",),
          "y_t": ("y_evac",), "h2_t": ("h2_high", "h2_low"), "e_t": ("e_evac",)}


def fills(order, names):
    return {what: n for n, what in enumerate(w for w in order if w[0] in names)}


def adaln_block(nc, x, norm_w, in_w, conv_w, conv_b, xproj_w, dt_w, dt_b, a_log, d_skip, out_w,
                gate_w, e_in, e_out, c_t, w_mod, out):
    ctx = ExitStack()
    with ctx:
        def sb(name, shape, dtype=F32):
            return ctx.enter_context(nc.sbuf_tensor(name, shape, dtype))

        def pb(name, shape):
            return ctx.enter_context(nc.psum_tensor(name, shape, F32))

        in_w16 = [sb(f"in_w_{n}", [P, NK, 2 * DI], F16) for n in ("high", "low")]
        out_sb = sb("out_sb", [P, NB, DM])
        ein_w16 = [sb(f"ein_w_{n}", [P, NK, NPAIR, 2 * 2 * HID], F16) for n in ("high", "low")]
        eout_sb = sb("eout_sb", [P, 2 * NPAIR, DM])
        xproj_sb = sb("xproj_sb", [P, NB, XD])
        dtw_sb = sb("dtw_sb", [NBT, DI])
        gate_w16 = [sb(f"gate_w_{n}", [P, NK, NE], F16) for n in ("high", "low")]
        select = sb("select", [NBT, NS], F16)
        norm_sb = sb("norm_sb", [P, NK])
        convw_sb = sb("convw_sb", [P, NB, CONV])
        convb_sb = sb("convb_sb", [P, NB])
        dtb_sb = sb("dtb_sb", [P, NB])
        skip_sb = sb("skip_sb", [P, NB])
        a_sb = sb("a_sb", [P, NB, NS])
        ident = sb("ident", [P, P])
        minus_half = sb("minus_half", [P, NJ])
        restart = sb("restart", [P, NJ, NE])
        mod_p = sb("mod_p", [P, 3, DM])
        mod_m = sb("mod_m", [P, 4, DM])
        x_sb = sb("x_sb", [P, NJ, DM])
        hnT = [sb(f"hnT_{n}", [P, 2, NK, CH], F16) for n in ("high", "low")]
        xi_pad = sb("xi_pad", [P, 2, CONV - 1 + CH])
        halo_sb = sb("halo_sb", [P, NB, CONV - 1])
        conv = sb("conv", [P, 2, CH])
        r_sb = conv[:, :, :].rearrange("p a (b n) -> p (a b) n", n=DM)
        th_p = sb("th_p", [P, 2, CH])
        u_sb = sb("u_sb", [P, NB, CH])
        xdT = th_p[0:NBT, 1, :]
        delta = sb("delta", [P, 2, NB, CH])
        xd_sb = sb("xd_sb", [P, 2, NJ, XD])
        bT = sb("bT", [NBT, 2, CH], F16)
        du_sb = sb("du_sb", [P, 2, NB, CH])
        y_sb = sb("y_sb", [P, 2, NJ, DI])
        h_of = [y_sb[:, n, 0:2, :].rearrange("p a (b n) -> p (a b) n", n=DM) for n in range(2)]
        square = th_p[:, 0, 0:DM]
        b_sb = sb("b_sb", [P, 2, CH])
        db_sb = sb("db_sb", [P, NB, CH])
        states = sb("states", [P, 2 * NB, CH])
        c_rows = sb("c_rows", [P, 2, DI])
        carry = sb("carry", [P, NS, NB])
        zg = sb("zg", [P, 2, DI])
        yT = sb("yT", [P, 2, NB, P])
        x1 = sb("x1", [P, NJ, DM])
        gated = sb("gated", [P, 2, DM])
        h2 = zg[:, :, :].rearrange("p a (b n) -> p (a b) n", n=DM)
        h2T = [sb(f"h2T_{n}", [P, NK, CH], F16) for n in ("high", "low")]
        act = sb("act", [P, 3, 2, HID])
        hidT = sb("hidT", [P, 2, 2, P])
        g_sb = sb("g_sb", [P, NJ, NE])
        rt = [sb(f"rt{n}", [P, NJ, NE]) for n in range(4)]
        rt_small = [sb(f"rt_small{n}", [P, NJ]) for n in range(2)]
        top = sb("top", [P, NJ, 8])
        weigh = sb("weigh", [P, NJ, 2 * NPAIR])
        bn = sb("bn", [P, 2, NJ, 6])
        mv = sb("mv", [P, 2, NJ, 2])
        rstd = sb("rstd", [P, 2, 2, NJ])
        ssq = sb("ssq", [P, NJ])
        rms = sb("rms", [P, 2, NJ])

        da_ps = [pb(f"da_ps{n}", [P, CH]) for n in range(2)]
        rows_ps = [pb(f"rows_ps{n}", [P, DI]) for n in range(2)]
        wide_ps = [pb(f"wide_ps{n}", [P, 512]) for n in range(2)]
        narrow_ps = pb("narrow_ps", [P, 512])
        moe_ps = pb("moe_ps", [P, 2, DM])

        mod_dram = nc.dram_tensor("mod_dram", (BATCH, 6, DM), F32, kind="Internal").ap()
        r_dram = nc.dram_tensor("r_dram", (NC, P, NJ * DM), F32, kind="Internal").ap()

        SEMS = ("weights_in", "ein_in0", "ein_in1", "ein_in2", "ein_in3", "ein_lifted", "ein_split", "in_split", "const_made", "act_made", "folded", "mod_mm", "mod_made", "mod_stored",
                "mod_in_p", "mod_in_m", "x_in", "r_out", "r_in", "y_out",
                "x_bn", "x_mv", "x_rstd_tmp", "x_rstd_done", "x_norm_done", "h_made", "h_squared", "h_rms_done",
                "r_gated", "r_made", "h_scaled", "xi_centered", "halo_set", "tapped", "u_tanhed", "u_made",
                "halo_saved", "hn_high_done", "h2_high_done", "xd_t_read", "b_low_done", "soft_abs", "soft_exped", "soft_done", "delta_made", "du_made", "skip_made",
                "x1_bn", "x1_mv", "x1_rstd_done", "x1_normed", "h2_made", "z_tanhed", "z_gated", "y_gated",
                "x1_made", "logit_exped", "router_step", "router_done",
                "e_tanhed", "e_acted", "e_weighed", "expert_out_done", "out_gated", "out_added",
                "exp_done", "scaled_done", "c_scaled", "c_added", "scan_done", "carried", "rows_full", "gathered",
                "wide_full0", "wide_full1", "wide_free0", "wide_free1",
                "narrow_full", "narrow_free")
        sem = {name: ctx.enter_context(nc.semaphore(name)) for name in SEMS}

        def clear_semaphores():
            for s in sem.values():
                nc.sync.sem_clear(s)
            nc.all_engine_barrier()

        wmod_sb = y_sb[:, :, :, :].rearrange("p a j n -> p (a j n)")[:, 0:NK * 6 * DM]
        wmod_sb = wmod_sb.rearrange("p (k n) -> p k n", k=NK)
        ct_sb = th_p[:, 0, 0:NK * BATCH].rearrange("p (k b) -> p k b", k=NK)
        ct_half = th_p[:, 1, 0:NK * BATCH].rearrange("p (k b) -> p k b", k=NK)
        ct_tanh = conv[:, 0, 0:NK * BATCH].rearrange("p (k b) -> p k b", k=NK)
        mod_row = db_sb[0:BATCH, 0:2, :].rearrange("b j n -> b (j n)")
        mod_row2 = conv[0:BATCH, 1, :]
        mod_tmp = x_sb[0:BATCH, 0:2, :].rearrange("b j n -> b (j n)")

        in_raw = states[:, 0:4, :].rearrange("p a n -> p (a n)").rearrange("p (k n) -> p k n", k=NK)
        gate_raw = conv[:, 1, 0:NK * NE].rearrange("p (k e) -> p k e", k=NK)
        ein_raw = [delta[:, n, 0:NK, :] for n in range(2)] + [du_sb[:, n, 0:NK, :] for n in range(2)]
        LOADS = [(in_raw, in_w), (out_sb[:, :, :], out_w), (eout_sb[:, :, :], e_out),
                 (xproj_sb[:, :, :], xproj_w), (dtw_sb[:, :], dt_w), (gate_raw, gate_w), (norm_sb[:, :], norm_w),
                 (convw_sb[:, :, :], conv_w), (convb_sb[:, :], conv_b), (dtb_sb[:, :], dt_b), (skip_sb[:, :], d_skip),
                 (a_sb[:, :, :], a_log), (wmod_sb, w_mod), (ct_sb, c_t)]
        with nc.Block() as block:
            @block.sync
            def _(sp):
                for dst, src in LOADS:
                    sp.dma_start(dst, src).then_inc(sem["weights_in"], 16)
                for n in range(NPAIR):
                    if n >= 4:
                        sp.wait_ge(sem["ein_split"], 2 * (n - 3))
                    sp.dma_start(ein_raw[n % 4], e_in[:, :, n, :]).then_inc(sem[f"ein_in{n % 4}"], 16)
                sp.wait_ge(sem["mod_made"], 11)
                rows = [mod_row[:, 512 * n:512 * n + 512] for n in range(2)] + [mod_row2]
                for n in range(3):
                    sp.dma_start(mod_dram[:, 2 * n:2 * n + 2, :].rearrange("b a n -> b (a n)"), rows[n]).then_inc(sem["mod_stored"], 16)
                sp.wait_ge(sem["mod_stored"], 3 * 16)

            @block.gpsimd
            def _(pool):
                pool.memset(ident[:, :], 0.0).then_inc(sem["const_made"], 1)
                pool.memset(minus_half[:, :], -0.5).then_inc(sem["const_made"], 1)
                pool.memset(restart[:, :, :], 1.0).then_inc(sem["const_made"], 1)
                pool.memset(weigh[:, :, :], 0.5 / LIFT ** 2).then_inc(sem["const_made"], 1)
                pool.memset(select[:, :], 0.0).then_inc(sem["const_made"], 1)
                pool.wait_ge(sem["const_made"], 5)
                pool.affine_select(out=select[:, :], in_=select[:, :], compare_op=ALU.not_equal, fill=1.0, base=0,
                                   pattern=[[-1, NS]], channel_multiplier=1).then_inc(sem["const_made"], 1)
                pool.wait_ge(sem["const_made"], 6)
                pool.affine_select(out=select[:, :], in_=select[:, :], compare_op=ALU.not_equal, fill=1.0, base=-32,
                                   pattern=[[-1, NS]], channel_multiplier=1).then_inc(sem["const_made"], 1)
                pool.affine_select(out=ident[:, :], in_=ident[:, :], compare_op=ALU.not_equal, fill=1.0, base=0,
                                   pattern=[[-1, P]], channel_multiplier=1).then_inc(sem["const_made"], 1)
                pool.memset(restart[:, :, 0:1], 0.0).then_inc(sem["const_made"], 1)

            @block.scalar
            def _(act_e):
                act_e.wait_ge(sem["weights_in"], 16 * len(LOADS))
                act_e.activation(a_sb[:, :, :], a_sb[:, :, :], ACT.Exp).then_inc(sem["act_made"], 1)
                act_e.activation(ct_tanh, ct_sb, ACT.Tanh, scale=0.5).then_inc(sem["act_made"], 1)

            @block.vector
            def _(v):
                v.wait_ge(sem["weights_in"], 16 * len(LOADS))
                for k in range(NK):
                    v.tensor_scalar(in_raw[:, k, :], in_raw[:, k, :], norm_sb[:, k:k + 1], LIFT, ALU.mult, ALU.mult).then_inc(sem["folded"], 1)
                v.tensor_scalar(convw_sb[:, :, :], convw_sb[:, :, :], 0.5 / LIFT, None, ALU.mult).then_inc(sem["folded"], 1)
                v.tensor_scalar(convb_sb[:, :], convb_sb[:, :], 0.5, None, ALU.mult).then_inc(sem["folded"], 1)
                v.tensor_scalar(out_sb[:, :, :], out_sb[:, :, :], 0.5 / LIFT, None, ALU.mult).then_inc(sem["folded"], 1)
                v.tensor_scalar(ct_half, ct_sb, 0.5, None, ALU.mult).then_inc(sem["folded"], 1)
                v.wait_ge(sem["act_made"], 2)
                v.tensor_scalar(a_sb[:, :, :], a_sb[:, :, :], -1.0, None, ALU.mult).then_inc(sem["folded"], 1)
                v.tensor_scalar(gate_raw, gate_raw, LIFT, None, ALU.mult).then_inc(sem["folded"], 1)
                v.wait_ge(sem["folded"], NK + 6)
                v.tensor_copy(in_w16[0][:, :, :], in_raw).then_inc(sem["in_split"], 1)
                v.tensor_copy(gate_w16[0][:, :, :], gate_raw).then_inc(sem["in_split"], 1)
                v.wait_ge(sem["in_split"], 2)
                v.tensor_tensor(in_w16[1][:, :, :], in_raw, in_w16[0][:, :, :], ALU.subtract).then_inc(sem["in_split"], 1)
                v.tensor_tensor(gate_w16[1][:, :, :], gate_raw, gate_w16[0][:, :, :], ALU.subtract).then_inc(sem["in_split"], 1)
                v.scalar_tensor_tensor(ct_half, ct_tanh, 1.0, ct_half, ALU.add, ALU.mult).then_inc(sem["mod_made"], 1)
                v.wait_ge(sem["mod_mm"], 1)
                v.tensor_copy(mod_row[:, 0:512], wide_ps[0][0:BATCH, :]).then_inc(sem["mod_made"], 1)
                v.tensor_copy(mod_row[:, 512:1024], wide_ps[1][0:BATCH, :]).then_inc(sem["mod_made"], 1)
                v.tensor_copy(mod_row2, rows_ps[0][0:BATCH, :]).then_inc(sem["mod_made"], 1)
                v.wait_ge(sem["mod_made"], 4)
                v.tensor_scalar(mod_row[:, DM:2 * DM], mod_row[:, DM:2 * DM], 1.0, None, ALU.add).then_inc(sem["mod_made"], 1)
                v.tensor_scalar(mod_row2[:, 0:DM], mod_row2[:, 0:DM], 1.0, None, ALU.add).then_inc(sem["mod_made"], 1)
                gates = [mod_row[:, 2 * DM:3 * DM], mod_row2[:, DM:2 * DM]]
                for n, g in enumerate(gates):
                    v.tensor_scalar(mod_tmp[:, DM * n:DM * n + DM], g, 0.0, 2.0, ALU.is_ge, ALU.mult).then_inc(sem["mod_made"], 1)
                v.wait_ge(sem["mod_made"], 8)
                v.tensor_scalar(mod_tmp, mod_tmp, 1.0, None, ALU.subtract).then_inc(sem["mod_made"], 1)
                v.wait_ge(sem["mod_made"], 9)
                for n, g in enumerate(gates):
                    v.tensor_tensor(g, g, mod_tmp[:, DM * n:DM * n + DM], ALU.mult).then_inc(sem["folded"], 1)
                v.wait_ge(sem["folded"], NK + 8)
                for n, g in enumerate(gates):
                    v.scalar_tensor_tensor(g, g, 0.25, mod_tmp[:, DM * n:DM * n + DM], ALU.max, ALU.mult).then_inc(sem["mod_made"], 1)
                for n in range(NPAIR):
                    raw = ein_raw[n % 4]
                    v.wait_ge(sem[f"ein_in{n % 4}"], 16 * (n // 4 + 1))
                    v.tensor_scalar(raw, raw, LIFT, None, ALU.mult).then_inc(sem["ein_lifted"], 1)
                    v.wait_ge(sem["ein_lifted"], n + 1)
                    v.tensor_copy(ein_w16[0][:, :, n, :], raw).then_inc(sem["ein_split"], 1)
                    v.wait_ge(sem["ein_split"], 2 * n + 1)
                    v.tensor_tensor(ein_w16[1][:, :, n, :], raw, ein_w16[0][:, :, n, :], ALU.subtract).then_inc(sem["ein_split"], 1)

            @block.tensor
            def _(pe):
                pe.wait_ge(sem["mod_made"], 1)
                for n, bank in enumerate((wide_ps[0], wide_ps[1], rows_ps[0])):
                    for k in range(NK):
                        last = pe.matmul(bank[0:BATCH, :], ct_half[:, k, :], wmod_sb[:, k, 512 * n:512 * n + 512],
                                         start=(k == 0), stop=(k == NK - 1))
                last.then_inc(sem["mod_mm"], 1)
        clear_semaphores()

        def run_slots(slots, load_mod_p=None, load_mod_m=None):
            order = schedule(slots)
            wide = fills(order, WIDE)
            narrow = fills(order, NARROW)

            def stages_before(t, kind):
                return sum(slots[n][kind] is not None for n in range(t))

            def nS(t):
                return stages_before(t, 0)

            def nP(t):
                return stages_before(t, 1)

            def nM(t):
                return stages_before(t, 2)

            def wide_bank(key):
                return wide_ps[wide[key] % 2][:, :]

            def wide_room(key):
                return sem[f"wide_free{wide[key] % 2}"], wide[key] // 2

            def wide_full(key):
                return sem[f"wide_full{wide[key] % 2}"], wide[key] // 2 + 1

            def wide_read(key):
                return sem[f"wide_free{wide[key] % 2}"], wide[key] // 2 + 1

            def narrow_room(key):
                return sem["narrow_free"], narrow[key]

            def narrow_full(key):
                return sem["narrow_full"], narrow[key] + 1

            def narrow_read(key):
                return sem["narrow_free"], narrow[key] + 1

            def soft_place(b):
                return (th_p, conv)[b // 2][:, b % 2, :]

            def walk(steps):
                for name, *where in order:
                    if name in steps:
                        steps[name](*where)

            def pair_of(u):
                return u % (2 * NPAIR) // 2

            def tile_of(u):
                return 2 * (u // (2 * NPAIR)) + u % 2

            with nc.Block() as block:
                @block.sync
                def _(sp):
                    if load_mod_p is not None:
                        row = mod_dram[bass.ds(load_mod_p, 1), 0:3, :].rearrange("o a n -> o (a n)")
                        sp.dma_start(mod_p[:, :, :].rearrange("p a n -> p (a n)"), row.broadcast_to([P, 3 * DM])).then_inc(sem["mod_in_p"], 16)
                    if load_mod_m is not None:
                        row = mod_dram[bass.ds(load_mod_m, 1), 2:6, :].rearrange("o a n -> o (a n)")
                        sp.dma_start(mod_m[:, :, :].rearrange("p a n -> p (a n)"), row.broadcast_to([P, 4 * DM])).then_inc(sem["mod_in_m"], 16)

                    def x_load(t):
                        if nP(t):
                            sp.wait_ge(sem["r_made"], nP(t))
                        sp.dma_start(x_sb[:, :, :], x[bass.ds(slots[t][1][1], 1)].rearrange("o p j n -> (o p) j n")).then_inc(sem["x_in"], 16)

                    def r_store(t):
                        sp.wait_ge(sem["r_made"], nP(t) + 1)
                        sp.dma_start(r_dram[bass.ds(slots[t][1][1], 1)].rearrange("o p n -> (o p) n"),
                                     conv[:, :, :].rearrange("p a n -> p (a n)")).then_inc(sem["r_out"], 16)

                    def r_load(t):
                        if nM(t):
                            sp.wait_ge(sem["y_out"], nM(t) * 32)
                        sp.dma_start(x1[:, :, :].rearrange("p j n -> p (j n)"),
                                     r_dram[bass.ds(slots[t][2][1], 1)].rearrange("o p n -> (o p) n")).then_inc(sem["r_in"], 16)

                    def out_store(t, q):
                        sp.wait_ge(sem["out_added"], 2 * nM(t) + q + 1)
                        sp.dma_start(out[bass.ds(slots[t][2][1], 1), :, 2 * q:2 * q + 2, :].rearrange("o p j n -> (o p) j n"),
                                     x1[:, 2 * q:2 * q + 2, :]).then_inc(sem["y_out"], 16)

                    walk({"x_load": x_load, "r_store": r_store, "r_load": r_load, "out_store": out_store})
                    sp.wait_ge(sem["r_out"], 16 * nP(len(slots)))
                    sp.wait_ge(sem["y_out"], 32 * nM(len(slots)))

                @block.gpsimd
                def _(pool):
                    def x_rstd(t):
                        pool.wait_ge(sem["x_mv"], NJ * (nP(t) + 1))
                        pool.tensor_scalar(rstd[:, 0, 0, :], mv[:, 0, :, 1], EPS, None, ALU.add).then_inc(sem["x_rstd_tmp"], 1)
                        own[0] += 1
                        pool.wait_ge(sem["x_rstd_tmp"], own[0])
                        pool.tensor_tensor(rstd[:, 0, 1, :], rstd[:, 0, 0, :], minus_half[:, :], ALU.pow).then_inc(sem["x_rstd_done"], 1)

                    def h_rms(t):
                        pool.wait_ge(sem["h_squared"], NJ * (nP(t) + 1))
                        pool.tensor_scalar(rms[:, 0, :], ssq[:, :], 1.0 / DM, EPS, ALU.mult, ALU.add).then_inc(sem["x_rstd_tmp"], 1)
                        own[0] += 1
                        pool.wait_ge(sem["x_rstd_tmp"], own[0])
                        pool.tensor_tensor(rms[:, 1, :], rms[:, 0, :], minus_half[:, :], ALU.pow).then_inc(sem["h_rms_done"], 1)

                    def r_gate(t):
                        h_sb = h_of[slots[t][1][0]]
                        pool.wait_ge(sem["h_made"], 2 * (nP(t) + 1))
                        if nP(t):
                            pool.wait_ge(sem["delta_made"], NB * nP(t))
                        pool.tensor_tensor(r_sb[:, :, :], h_sb[:, :, :], mod_p[:, 2:3, :].broadcast_to([P, NJ, DM]), ALU.mult).then_inc(sem["r_gated"], 1)

                    def r_add(t):
                        pool.wait_ge(sem["r_gated"], nP(t) + 1)
                        pool.tensor_tensor(r_sb[:, :, :], r_sb[:, :, :], x_sb[:, :, :], ALU.add).then_inc(sem["r_made"], 1)

                    def du(t, b):
                        pool.wait_ge(sem["delta_made"], NB * nP(t) + b + 1)
                        pool.tensor_tensor(du_sb[:, slots[t][1][0], b, :], delta[:, slots[t][1][0], b, :], u_sb[:, b, :], ALU.mult).then_inc(sem["du_made"], 1)

                    def scaled(t, s, b):
                        n = (NS * nS(t) + s) * NB + b
                        pool.wait_ge(*wide_read(("b_cast", t, s)))
                        if nP(t):
                            pool.wait_ge(sem["du_made"], NB * nP(t))
                        pool.wait_ge(sem["scan_done"], max(0, n - NB + 1))
                        pool.tensor_tensor(db_sb[:, b, :], du_sb[:, slots[t][0][0], b, :], b_sb[:, s % 2, :], ALU.mult).then_inc(sem["scaled_done"], 1)

                    def c_add(t, s):
                        n = NS * nS(t) + s
                        pool.wait_ge(sem["c_scaled"], n + 1)
                        pool.wait_ge(sem["c_added"], n)
                        if s == 0 and t > 0 and slots[t - 1][1] is not None:
                            pool.wait_ge(*narrow_read(("skip_t", t - 1, NB - 1)))
                        place = y_sb[:, slots[t][0][0], NJ - 1, :]
                        pool.tensor_tensor(place, place, c_rows[:, n % 2, :], ALU.add).then_inc(sem["c_added"], 1)

                    def y_gate(t, j):
                        pool.wait_ge(*wide_read(("z", t, j)))
                        if nS(t):
                            pool.wait_ge(sem["gathered"], nS(t) * NS * (NJ - 1))
                            pool.wait_ge(sem["c_added"], nS(t) * NS)
                        place = y_sb[:, slots[t][2][0], j, :]
                        pool.tensor_tensor(place, place, zg[:, j % 2, :], ALU.mult).then_inc(sem["y_gated"], 1)

                    def x1_rstd(t):
                        pool.wait_ge(sem["x1_mv"], NJ * (nM(t) + 1))
                        pool.tensor_scalar(rstd[:, 1, 0, :], mv[:, 1, :, 1], EPS, None, ALU.add).then_inc(sem["x_rstd_tmp"], 1)
                        own[0] += 1
                        pool.wait_ge(sem["x_rstd_tmp"], own[0])
                        pool.tensor_tensor(rstd[:, 1, 1, :], rstd[:, 1, 0, :], minus_half[:, :], ALU.pow).then_inc(sem["x1_rstd_done"], 1)

                    def e_weigh(t, u):
                        pool.wait_ge(sem["router_done"], nM(t) + 1)
                        pool.wait_ge(*wide_read(("expert_in", t, u)))
                        place = act[:, u % 3, :, :]
                        pool.tensor_tensor(place, place, weigh[:, tile_of(u), 2 * pair_of(u):2 * pair_of(u) + 2].unsqueeze(2).broadcast_to([P, 2, HID]),
                                           ALU.mult).then_inc(sem["e_weighed"], 1)

                    own = [0]
                    if load_mod_p is not None:
                        pool.wait_ge(sem["mod_in_p"], 16)
                    walk({"x_rstd": x_rstd, "h_rms": h_rms, "r_gate": r_gate, "r_add": r_add, "du": du,
                          "scaled": scaled, "c_add": c_add, "y_gate": y_gate, "x1_rstd": x1_rstd, "e_weigh": e_weigh})

                @block.scalar
                def _(ac):
                    def h_square(t, j):
                        h_sb = h_of[slots[t][1][0]]
                        ac.wait_ge(sem["h_made"], 2 * (nP(t) + 1))
                        if nP(t):
                            ac.wait_ge(sem["h_rms_done"], nP(t))
                            ac.wait_ge(sem["delta_made"], NB * nP(t))
                        ac.wait_ge(sem["h_squared"], NJ * nP(t) + j)
                        ac.activation(square, h_sb[:, j, :], ACT.Square, accum_out=ssq[:, j:j + 1]).then_inc(sem["h_squared"], 1)

                    def h_scale(t, j):
                        h_sb = h_of[slots[t][1][0]]
                        ac.wait_ge(sem["h_rms_done"], nP(t) + 1)
                        ac.wait_ge(sem["r_gated"], nP(t) + 1)
                        ac.wait_ge(sem["h_squared"], NJ * nP(t) + j + 1)
                        ac.activation(h_sb[:, j, :], h_sb[:, j, :], ACT.Copy, scale=rms[:, 1, j:j + 1]).then_inc(sem["h_scaled"], 1)

                    def hn_high(t, k):
                        if slots[t][2] is not None:
                            for j in range(2, NJ):
                                ac.wait_ge(*wide_full(("z", t, j)))
                        ac.wait_ge(*narrow_full(("hn_t", t, k)))
                        ac.activation(hnT[0][:, slots[t][1][0], k, :], narrow_ps[:, :], ACT.Copy).then_inc(sem["hn_high_done"], 1)

                    def xi_center(t, b):
                        key = ("xi", t, b)
                        n = NB * nP(t) + b
                        ac.wait_ge(*wide_full(key))
                        ac.wait_ge(sem["u_made"], max(0, n - 1))
                        ac.wait_ge(sem["r_out"], 16 * (nP(t) + 1))
                        ac.activation(conv[:, b % 2, :], wide_bank(key), ACT.Identity, scale=convw_sb[:, b, CONV - 1:CONV],
                                      bias=convb_sb[:, b:b + 1]).then_inc(sem["xi_centered"], 1)

                    def xi_copy(t, b):
                        key = ("xi", t, b)
                        n = NB * nP(t) + b
                        ac.wait_ge(sem["tapped"], max(0, (CONV - 1) * (n - 1)))
                        ac.wait_ge(sem["halo_saved"], max(0, n - 1))
                        ac.activation(xi_pad[:, b % 2, CONV - 1:], wide_bank(key), ACT.Copy).then_inc(wide_read(key)[0], 1)

                    def u_tanh(t, b):
                        n = NB * nP(t) + b
                        ac.wait_ge(sem["tapped"], (CONV - 1) * (n + 1))
                        ac.wait_ge(sem["u_made"], max(0, n - 1))
                        if nP(t):
                            ac.wait_ge(sem["delta_made"], NB * nP(t))
                        ac.activation(th_p[:, b % 2, :], conv[:, b % 2, :], ACT.Tanh).then_inc(sem["u_tanhed"], 1)

                    def xd_t_evac(t):
                        ac.wait_ge(sem["u_made"], NB * (nP(t) + 1))
                        ac.wait_ge(*narrow_full(("xd_t", t)))
                        ac.activation(xdT, narrow_ps[0:NBT, :], ACT.Copy).then_inc(sem["xd_t_read"], 1)

                    def b_high(t):
                        if nS(t):
                            ac.wait_ge(sem["scaled_done"], NB * NS * nS(t))
                        ac.wait_ge(*narrow_full(("xd_t", t)))
                        ac.activation(bT[:, slots[t][1][0], :], narrow_ps[0:NBT, :], ACT.Copy).then_inc(sem["narrow_free"], 1)

                    def dt_bias(t, b):
                        key = ("dtp", t, b)
                        ac.wait_ge(*wide_full(key))
                        ac.activation(delta[:, slots[t][1][0], b, :], wide_bank(key), ACT.Identity, bias=dtb_sb[:, b:b + 1]).then_inc(wide_read(key)[0], 1)

                    def soft_exp(t, half):
                        n = 2 * nP(t) + half
                        for b in range(NB):
                            ac.wait_ge(*wide_read(("dtp", t, b)))
                        ac.wait_ge(sem["b_low_done"], nP(t) + 1)
                        place = (th_p, conv)[half][:, :, :]
                        ac.activation(place, delta[:, slots[t][1][0], 2 * half:2 * half + 2, :], ACT.Abs).then_inc(sem["soft_abs"], 1)
                        ac.wait_ge(sem["soft_abs"], n + 1)
                        ac.activation(place, place, ACT.Exp, scale=-1.0).then_inc(sem["soft_exped"], 1)

                    def soft_ln(t, half):
                        ac.wait_ge(sem["soft_exped"], 2 * nP(t) + half + 1)
                        place = (th_p, conv)[half][:, :, :]
                        ac.activation(place, place, ACT.Ln, bias=1.0).then_inc(sem["soft_done"], 1)

                    def b_evac(t, s):
                        ac.wait_ge(sem["scaled_done"], max(0, NB * (NS * nS(t) + s - 1)))
                        ac.wait_ge(*wide_full(("b_cast", t, s)))
                        ac.activation(b_sb[:, s % 2, :], wide_bank(("b_cast", t, s)), ACT.Copy).then_inc(wide_read(("b_cast", t, s))[0], 1)

                    def c_scale(t, s):
                        n = NS * nS(t) + s
                        ac.wait_ge(sem["rows_full"], NJ * (n + 1))
                        ac.wait_ge(sem["c_added"], max(0, n - 1))
                        ac.activation(c_rows[:, n % 2, :], rows_ps[1][:, :], ACT.Copy,
                                      scale=xd_sb[:, slots[t][0][0], NJ - 1, AT_C + s:AT_C + s + 1]).then_inc(sem["c_scaled"], 1)

                    def skip(t, b):
                        ac.wait_ge(sem["du_made"], NB * nP(t) + b + 1)
                        ac.activation(u_sb[:, b, :], u_sb[:, b, :], ACT.Copy, scale=skip_sb[:, b:b + 1]).then_inc(sem["skip_made"], 1)

                    def skip_evac(t, b):
                        if slots[t][2] is not None:
                            ac.wait_ge(*narrow_full(("y_t", t, NJ - 1)))
                        ac.wait_ge(*narrow_full(("skip_t", t, b)))
                        ac.activation(y_sb[:, slots[t][1][0], :, b * P:b * P + P],
                                      narrow_ps[:, :].rearrange("p (j n) -> p j n", j=NJ), ACT.Copy).then_inc(sem["narrow_free"], 1)

                    def exp(t, s, b):
                        n = (NS * nS(t) + s) * NB + b
                        if nP(t):
                            ac.wait_ge(sem["delta_made"], NB * nP(t))
                        ac.wait_ge(sem["scan_done"], max(0, n - 1))
                        ac.activation(da_ps[n % 2][:, :], delta[:, slots[t][0][0], b, :], ACT.Exp,
                                      scale=a_sb[:, b, s:s + 1]).then_inc(sem["exp_done"], 1)

                    def z_tanh(t, j):
                        key = ("z", t, j)
                        n = NJ * nM(t) + j
                        ac.wait_ge(*wide_full(key))
                        ac.wait_ge(sem["y_gated"], max(0, n - 1))
                        if nM(t):
                            last = [q for q in range(t) if slots[q][2] is not None][-1]
                            for k in range(NK):
                                ac.wait_ge(*narrow_full(("h2_t", last, k)))
                        ac.activation(zg[:, j % 2, :], wide_bank(key), ACT.Tanh, scale=0.5 / LIFT).then_inc(sem["z_tanhed"], 1)

                    def y_evac(t, j):
                        n = NJ * nM(t) + j
                        ac.wait_ge(*narrow_full(("y_t", t, j)))
                        if n >= 2:
                            ac.wait_ge(*wide_full(op_key(n - 2)))
                        ac.activation(yT[:, j % 2, :, :], narrow_ps[:, :].rearrange("p (b n) -> p b n", b=NB), ACT.Copy).then_inc(sem["narrow_free"], 1)

                    def op_key(n):
                        tt = [q for q in range(len(slots)) if slots[q][2] is not None][n // NJ]
                        return ("op", tt, n % NJ)

                    def h2_high(t, k):
                        ac.wait_ge(*narrow_full(("h2_t", t, k)))
                        if nM(t):
                            last = [n for n in range(t) if slots[n][2] is not None][-1]
                            ac.wait_ge(*wide_full(("expert_in", last, UNITS - 1)))
                            ac.wait_ge(*wide_full(("expert_in", last, UNITS - 2)))
                        ac.activation(h2T[0][:, k, :], narrow_ps[:, :], ACT.Copy).then_inc(sem["h2_high_done"], 1)

                    def logit_exp(t):
                        key = ("logit", t)
                        ac.wait_ge(*wide_full(key))
                        if nM(t):
                            ac.wait_ge(sem["router_done"], nM(t))
                        ac.activation(g_sb[:, :, :], wide_bank(key)[:, 0:NJ * NE].rearrange("p (j e) -> p j e", j=NJ), ACT.Exp, scale=-1.0 / LIFT).then_inc(wide_read(key)[0], 1)

                    def e_tanh(t, u):
                        key = ("expert_in", t, u)
                        n = UNITS * nM(t) + u
                        ac.wait_ge(*wide_full(key))
                        if n >= 3:
                            ac.wait_ge(*narrow_full(unit_key("e_t", n - 3)))
                        hin = wide_bank(key).rearrange("p (e a h) -> p e a h", e=2, a=2)[:, :, 0, :]
                        ac.activation(act[:, u % 3, :, :], hin, ACT.Tanh, scale=0.5 / LIFT).then_inc(sem["e_tanhed"], 1)

                    def unit_key(name, n):
                        tt = [t for t in range(len(slots)) if slots[t][2] is not None][n // UNITS]
                        return (name, tt, n % UNITS)

                    def e_evac(t, u):
                        n = UNITS * nM(t) + u
                        ac.wait_ge(*narrow_full(("e_t", t, u)))
                        ac.wait_ge(sem["expert_out_done"], max(0, n - 1))
                        ac.activation(hidT[:, u % 2, :, :], narrow_ps[:, 0:2 * P].rearrange("p (e n) -> p e n", e=2), ACT.Copy).then_inc(sem["narrow_free"], 1)

                    walk({"h_square": h_square, "h_scale": h_scale, "hn_high": hn_high, "xi_center": xi_center,
                          "xi_copy": xi_copy, "u_tanh": u_tanh, "xd_t_evac": xd_t_evac, "b_high": b_high, "dt_bias": dt_bias, "soft_exp": soft_exp, "soft_ln": soft_ln,
                          "b_evac": b_evac, "c_scale": c_scale, "skip": skip, "skip_evac": skip_evac, "exp": exp, "z_tanh": z_tanh, "y_evac": y_evac,
                          "h2_high": h2_high, "logit_exp": logit_exp, "e_tanh": e_tanh, "e_evac": e_evac})

                @block.vector
                def _(v):
                    def x_stat(t, j):
                        v.wait_ge(sem["x_in"], 16 * (nP(t) + 1))
                        if nP(t):
                            v.wait_ge(sem["x_norm_done"], NJ * nP(t))
                        v.bn_stats(bn[:, 0, j, :], x_sb[:, j, :]).then_inc(sem["x_bn"], 1)
                        v.wait_ge(sem["x_bn"], NJ * nP(t) + j + 1)
                        v.bn_aggr(mv[:, 0, j, :], bn[:, 0, j, :]).then_inc(sem["x_mv"], 1)

                    def x_norm(t, j):
                        v.wait_ge(sem["x_rstd_done"], nP(t) + 1)
                        h_sb = h_of[slots[t][1][0]]
                        if slots[t][2] is not None:
                            v.wait_ge(*narrow_full(("y_t", t, NJ - 1)))
                        v.tensor_scalar(h_sb[:, j, :], x_sb[:, j, :], mv[:, 0, j, 0:1], rstd[:, 0, 1, j:j + 1],
                                        ALU.subtract, ALU.mult).then_inc(sem["x_norm_done"], 1)

                    def x_scale(t):
                        h_sb = h_of[slots[t][1][0]]
                        if load_mod_p is not None:
                            v.wait_ge(sem["mod_in_p"], 16)
                        v.wait_ge(sem["x_norm_done"], NJ * (nP(t) + 1))
                        v.tensor_tensor(h_sb[:, :, :], h_sb[:, :, :], mod_p[:, 1:2, :].broadcast_to([P, NJ, DM]), ALU.mult).then_inc(sem["h_made"], 1)

                    def x_shift(t):
                        h_sb = h_of[slots[t][1][0]]
                        v.wait_ge(sem["h_made"], 2 * nP(t) + 1)
                        v.tensor_tensor(h_sb[:, :, :], h_sb[:, :, :], mod_p[:, 0:1, :].broadcast_to([P, NJ, DM]), ALU.add).then_inc(sem["h_made"], 1)

                    def halo(t, b):
                        n = NB * nP(t) + b
                        par = slots[t][1][0]
                        v.wait_ge(sem["tapped"], max(0, (CONV - 1) * (n - 1)))
                        v.wait_ge(sem["halo_saved"], max(0, n - 1))
                        if par == 0:
                            v.memset(xi_pad[:, b % 2, 0:CONV - 1], 0.0).then_inc(sem["halo_set"], 1)
                        else:
                            if nP(t):
                                v.wait_ge(sem["halo_saved"], NB * nP(t))
                            v.tensor_copy(xi_pad[:, b % 2, 0:CONV - 1], halo_sb[:, b, :]).then_inc(sem["halo_set"], 1)
                        v.wait_ge(sem["halo_set"], n + 1)
                        v.wait_ge(*wide_read(("xi", t, b)))
                        v.tensor_copy(halo_sb[:, b, :], xi_pad[:, b % 2, CH:CH + CONV - 1]).then_inc(sem["halo_saved"], 1)

                    def tap(t, b, k):
                        n = NB * nP(t) + b
                        v.wait_ge(sem["xi_centered"], n + 1)
                        v.wait_ge(sem["tapped"], (CONV - 1) * n + k)
                        place = conv[:, b % 2, :]
                        v.scalar_tensor_tensor(place, xi_pad[:, b % 2, k:k + CH], convw_sb[:, b, k:k + 1], place, ALU.mult, ALU.add).then_inc(sem["tapped"], 1)

                    def u(t, b):
                        n = NB * nP(t) + b
                        v.wait_ge(sem["u_tanhed"], n + 1)
                        if nP(t):
                            last = [q for q in range(t) if slots[q][1] is not None][-1]
                            v.wait_ge(*narrow_full(("skip_t", last, NB - 1)))
                        v.scalar_tensor_tensor(u_sb[:, b, :], th_p[:, b % 2, :], 1.0, conv[:, b % 2, :], ALU.add, ALU.mult).then_inc(sem["u_made"], 1)

                    def xd_evac(t):
                        key = ("xd", t)
                        v.wait_ge(*wide_full(key))
                        v.tensor_copy(xd_sb[:, slots[t][1][0], :, :], wide_bank(key)[:, 0:NJ * XD].rearrange("p (j n) -> p j n", j=NJ)).then_inc(wide_read(key)[0], 1)

                    def delta_(t, b):
                        n = NB * nP(t) + b
                        v.wait_ge(sem["soft_done"], 2 * nP(t) + b // 2 + 1)
                        place = delta[:, slots[t][1][0], b, :]
                        v.scalar_tensor_tensor(place, place, 0.0, soft_place(b), ALU.max, ALU.add).then_inc(sem["delta_made"], 1)

                    def hn_low(t, k):
                        v.wait_ge(sem["hn_high_done"], NK * nP(t) + k + 1)
                        par = slots[t][1][0]
                        v.tensor_tensor(hnT[1][:, par, k, :], narrow_ps[:, :], hnT[0][:, par, k, :], ALU.subtract).then_inc(sem["narrow_free"], 1)

                    def h2_low(t, k):
                        v.wait_ge(sem["h2_high_done"], NK * nM(t) + k + 1)
                        v.tensor_tensor(h2T[1][:, k, :], narrow_ps[:, :], h2T[0][:, k, :], ALU.subtract).then_inc(sem["narrow_free"], 1)

                    def b_low(t):
                        v.wait_ge(sem["xd_t_read"], nP(t) + 1)
                        v.wait_ge(*narrow_read(("xd_t", t)))
                        place = bT[32:NBT, slots[t][1][0], :]
                        v.tensor_tensor(place, xdT[32:NBT, :], place, ALU.subtract).then_inc(sem["b_low_done"], 1)

                    def scan(t, s, b):
                        n = (NS * nS(t) + s) * NB + b
                        par = slots[t][0][0]
                        v.wait_ge(sem["exp_done"], n + 1)
                        v.wait_ge(sem["scaled_done"], n + 1)
                        v.wait_ge(sem["rows_full"], max(0, (n // NB - 1) * NJ))
                        v.wait_ge(sem["carried"], carries(n // NB - 2))
                        first = 0.0
                        if par == 1:
                            first = carry[:, s, b:b + 1]
                            v.wait_ge(sem["carried"], carries(NS * nS(t) - 1))
                        v.tensor_tensor_scan(states[:, n % (2 * NB), :], da_ps[n % 2][:, :], db_sb[:, b, :], first,
                                             ALU.mult, ALU.add).then_inc(sem["scan_done"], 1)

                    def carries(step):
                        halves = (t for t in range(len(slots)) if slots[t][0] is not None and slots[t][0][0] == 0)
                        return sum(max(0, min(NS, step + 1 - NS * nS(t))) for t in halves)

                    def carry_(t, s):
                        if slots[t][0][0] == 1:
                            return
                        n = NS * nS(t) + s
                        v.wait_ge(sem["scan_done"], NB * (n + 1))
                        at = n % 2 * NB
                        v.tensor_copy(carry[:, s, :], states[:, at:at + NB, CH - 1]).then_inc(sem["carried"], 1)

                    def gather(t, s, j):
                        step = NS * nS(t) + s
                        par = slots[t][0][0]
                        v.wait_ge(sem["rows_full"], NJ * step + j + 1)
                        v.wait_ge(sem["gathered"], max(0, (NJ - 1) * (step - 1) + j + 1))
                        if s == 0 and t > 0 and slots[t - 1][1] is not None:
                            v.wait_ge(*narrow_read(("skip_t", t - 1, NB - 1)))
                        place = y_sb[:, par, j, :]
                        v.scalar_tensor_tensor(place, rows_ps[j % 2][:, :], xd_sb[:, par, j, AT_C + s:AT_C + s + 1], place,
                                               ALU.mult, ALU.add).then_inc(sem["gathered"], 1)

                    def z_gate(t, j):
                        key = ("z", t, j)
                        v.wait_ge(sem["z_tanhed"], NJ * nM(t) + j + 1)
                        place = zg[:, j % 2, :]
                        v.scalar_tensor_tensor(place, place, 1.0, wide_bank(key), ALU.add, ALU.mult).then_inc(wide_read(key)[0], 1)

                    def op_gate(t, j):
                        key = ("op", t, j)
                        v.wait_ge(*wide_full(key))
                        if load_mod_m is not None:
                            v.wait_ge(sem["mod_in_m"], 16)
                        v.wait_ge(sem["x1_made"], max(0, NJ * nM(t) + j - 1))
                        v.tensor_tensor(gated[:, j % 2, :], wide_bank(key)[:, 0:DM], mod_m[:, 0, :], ALU.mult).then_inc(wide_read(key)[0], 1)

                    def x1_(t, j):
                        v.wait_ge(*wide_read(("op", t, j)))
                        v.wait_ge(sem["r_in"], 16 * (nM(t) + 1))
                        v.tensor_tensor(x1[:, j, :], x1[:, j, :], gated[:, j % 2, :], ALU.add).then_inc(sem["x1_made"], 1)

                    def x1_stat(t, j):
                        v.wait_ge(sem["x1_made"], NJ * nM(t) + j + 1)
                        if nM(t):
                            v.wait_ge(sem["x1_normed"], NJ * nM(t))
                        v.bn_stats(bn[:, 1, j, :], x1[:, j, :]).then_inc(sem["x1_bn"], 1)
                        v.wait_ge(sem["x1_bn"], NJ * nM(t) + j + 1)
                        v.bn_aggr(mv[:, 1, j, :], bn[:, 1, j, :]).then_inc(sem["x1_mv"], 1)

                    def x1_norm(t, j):
                        v.wait_ge(sem["x1_rstd_done"], nM(t) + 1)
                        v.wait_ge(sem["y_gated"], NJ * (nM(t) + 1))
                        if nM(t):
                            last = [n for n in range(t) if slots[n][2] is not None][-1]
                            v.wait_ge(*narrow_full(("h2_t", last, NK - 1)))
                        v.tensor_scalar(h2[:, j, :], x1[:, j, :], mv[:, 1, j, 0:1], rstd[:, 1, 1, j:j + 1],
                                        ALU.subtract, ALU.mult).then_inc(sem["x1_normed"], 1)

                    def x1_scale(t):
                        v.wait_ge(sem["x1_normed"], NJ * (nM(t) + 1))
                        v.tensor_tensor(h2[:, :, :], h2[:, :, :], mod_m[:, 2:3, :].broadcast_to([P, NJ, DM]), ALU.mult).then_inc(sem["h2_made"], 1)

                    def x1_shift(t):
                        v.wait_ge(sem["h2_made"], 2 * nM(t) + 1)
                        v.tensor_tensor(h2[:, :, :], h2[:, :, :], mod_m[:, 1:2, :].broadcast_to([P, NJ, DM]), ALU.add).then_inc(sem["h2_made"], 1)

                    def router(t):
                        def done(instruction):
                            own[0] += 1
                            instruction.then_inc(sem["router_step"], 1)
                            v.wait_ge(sem["router_step"], own[0])

                        above, equal, rank, g = rt[0], rt[1], rt[2], rt[3]
                        count, total = rt_small
                        v.wait_ge(*wide_read(("logit", t)))
                        done(v.tensor_scalar(g_sb[:, :, :], g_sb[:, :, :], 1.0, None, ALU.add))
                        done(v.reciprocal(g[:, :, :], g_sb[:, :, :]))
                        for j in range(NJ):
                            last = v.max(top[:, j, :], g[:, j, :])
                            if j < NJ - 1:
                                last.then_inc(sem["router_step"], 1)
                                own[0] += 1
                        done(last)
                        fourth = top[:, :, TOPK - 1:TOPK].broadcast_to([P, NJ, NE])
                        done(v.tensor_tensor(above[:, :, :], g[:, :, :], fourth, ALU.is_gt))
                        done(v.tensor_tensor(equal[:, :, :], g[:, :, :], fourth, ALU.is_equal))
                        done(v.reduce_sum(count[:, :], above[:, :, :], axis=AX.X))
                        done(v.tensor_tensor_scan(rank[:, :, :].rearrange("p j e -> p (j e)"), restart[:, :, :].rearrange("p j e -> p (j e)"),
                                                  equal[:, :, :].rearrange("p j e -> p (j e)"), 0.0, ALU.mult, ALU.add))
                        done(v.tensor_tensor(rank[:, :, :], rank[:, :, :], count[:, :].unsqueeze(2).broadcast_to([P, NJ, NE]), ALU.add))
                        done(v.tensor_scalar(rank[:, :, :], rank[:, :, :], TOPK + 0.5, None, ALU.is_lt))
                        done(v.tensor_tensor(equal[:, :, :], equal[:, :, :], rank[:, :, :], ALU.mult))
                        done(v.tensor_tensor(above[:, :, :], above[:, :, :], equal[:, :, :], ALU.add))
                        done(v.tensor_tensor(g[:, :, :], g[:, :, :], above[:, :, :], ALU.mult))
                        done(v.reduce_sum(total[:, :], g[:, :, :], axis=AX.X))
                        done(v.reciprocal(total[:, :], total[:, :]))
                        if nM(t):
                            v.wait_ge(sem["e_weighed"], UNITS * nM(t))
                        v.scalar_tensor_tensor(weigh[:, :, 0:NE], g[:, :, :], 0.5 / LIFT ** 2, total[:, :].unsqueeze(2).broadcast_to([P, NJ, NE]),
                                               ALU.mult, ALU.mult).then_inc(sem["router_done"], 1)

                    def e_act(t, u):
                        key = ("expert_in", t, u)
                        v.wait_ge(sem["e_tanhed"], UNITS * nM(t) + u + 1)
                        place = act[:, u % 3, :, :]
                        hin = wide_bank(key).rearrange("p (e a h) -> p e a h", e=2, a=2)[:, :, 0, :]
                        v.scalar_tensor_tensor(place, place, 1.0, hin, ALU.add, ALU.mult).then_inc(sem["e_acted"], 1)

                    def e_mul(t, u):
                        key = ("expert_in", t, u)
                        v.wait_ge(sem["e_acted"], UNITS * nM(t) + u + 1)
                        place = act[:, u % 3, :, :]
                        vin = wide_bank(key).rearrange("p (e a h) -> p e a h", e=2, a=2)[:, :, 1, :]
                        v.tensor_tensor(place, place, vin, ALU.mult).then_inc(wide_read(key)[0], 1)

                    def out_gate(t, q):
                        n = 2 * nM(t) + q
                        v.wait_ge(sem["expert_out_done"], UNITS * nM(t) + 2 * NPAIR * (q + 1))
                        v.wait_ge(sem["out_added"], n)
                        v.tensor_tensor(gated[:, :, :], moe_ps[:, :, :], mod_m[:, 3:4, :].broadcast_to([P, 2, DM]), ALU.mult).then_inc(sem["out_gated"], 1)

                    def out_add(t, q):
                        v.wait_ge(sem["out_gated"], 2 * nM(t) + q + 1)
                        place = x1[:, 2 * q:2 * q + 2, :]
                        v.tensor_tensor(place, place, gated[:, :, :], ALU.add).then_inc(sem["out_added"], 1)

                    own = [0]
                    walk({"x_stat": x_stat, "x_norm": x_norm, "x_scale": x_scale, "x_shift": x_shift, "halo": halo, "tap": tap,
                          "u": u, "xd_evac": xd_evac, "delta": delta_, "hn_low": hn_low, "h2_low": h2_low, "b_low": b_low, "scan": scan, "carry": carry_, "gather": gather,
                          "z_gate": z_gate, "op_gate": op_gate, "x1": x1_, "x1_stat": x1_stat, "x1_norm": x1_norm,
                          "x1_scale": x1_scale, "x1_shift": x1_shift, "router": router, "e_act": e_act, "e_mul": e_mul,
                          "out_gate": out_gate, "out_add": out_add})

                @block.tensor
                def _(pe):
                    def hn_t(t, k):
                        h_sb = h_of[slots[t][1][0]]
                        pe.wait_ge(sem["h_scaled"], NJ * (nP(t) + 1))
                        pe.wait_ge(*narrow_room(("hn_t", t, k)))
                        for n in range(NJ):
                            last = pe.transpose(narrow_ps[:, n * P:n * P + P], h_sb[:, n, k * P:k * P + P], ident[:, :])
                        last.then_inc(sem["narrow_full"], 1)

                    def xi(t, b):
                        key = ("xi", t, b)
                        pe.wait_ge(*narrow_read(("hn_t", t, NK - 1)))
                        pe.wait_ge(*wide_room(key))
                        for n, (k, w, h) in enumerate(SPLIT):
                            last = pe.matmul(wide_bank(key), in_w16[w][:, k, b * P:b * P + P], hnT[h][:, slots[t][1][0], k, :],
                                             start=(n == 0), stop=(n == len(SPLIT) - 1))
                        last.then_inc(wide_full(key)[0], 1)

                    def xd(t):
                        key = ("xd", t)
                        pe.wait_ge(sem["u_made"], NB * (nP(t) + 1))
                        pe.wait_ge(*wide_room(key))
                        for j in range(NJ):
                            for b in range(NB):
                                last = pe.matmul(wide_bank(key)[:, j * XD:j * XD + XD], u_sb[:, b, j * P:j * P + P], xproj_sb[:, b, :],
                                                 start=(b == 0), stop=(b == NB - 1))
                        last.then_inc(wide_full(key)[0], 1)

                    def xd_t(t):
                        pe.wait_ge(*wide_read(("xd", t)))
                        pe.wait_ge(*narrow_room(("xd_t", t)))
                        for n in range(NJ):
                            last = pe.transpose(narrow_ps[0:NBT, n * P:n * P + P], xd_sb[:, slots[t][1][0], n, 0:NBT], ident[:, :])
                        last.then_inc(sem["narrow_full"], 1)

                    def dtp(t, b):
                        key = ("dtp", t, b)
                        pe.wait_ge(sem["xd_t_read"], nP(t) + 1)
                        pe.wait_ge(*wide_room(key))
                        pe.matmul(wide_bank(key), dtw_sb[:, b * P:b * P + P], xdT, start=True, stop=True).then_inc(wide_full(key)[0], 1)

                    def skip_t(t, b):
                        pe.wait_ge(sem["skip_made"], NB * nP(t) + b + 1)
                        pe.wait_ge(*narrow_room(("skip_t", t, b)))
                        for n in range(NJ):
                            last = pe.transpose(narrow_ps[:, n * P:n * P + P], u_sb[:, b, n * P:n * P + P], ident[:, :])
                        last.then_inc(sem["narrow_full"], 1)

                    def b_cast(t, s):
                        key = ("b_cast", t, s)
                        if nP(t):
                            pe.wait_ge(sem["b_low_done"], nP(t))
                        pe.wait_ge(*wide_room(key))
                        pe.matmul(wide_bank(key), select[:, s:s + 1].broadcast_to([NBT, P]), bT[:, slots[t][0][0], :], start=True, stop=True).then_inc(wide_full(key)[0], 1)

                    def rows(t, s, j):
                        step = NS * nS(t) + s
                        pe.wait_ge(sem["scan_done"], (step + 1) * NB)
                        if j == 1:
                            pe.wait_ge(sem["c_scaled"], step)
                        else:
                            pe.wait_ge(sem["gathered"], max(0, (NJ - 1) * step + (0, 0, 1, 2)[j]))
                        for b in range(NB):
                            last = pe.transpose(rows_ps[j % 2][:, b * P:b * P + P], states[:, step % 2 * NB + b, j * P:j * P + P], ident[:, :])
                        last.then_inc(sem["rows_full"], 1)

                    def z(t, j):
                        key = ("z", t, j)
                        pe.wait_ge(*wide_room(key))
                        for n, (k, h, w) in enumerate(SPLIT):
                            last = pe.matmul(wide_bank(key), hnT[h][:, slots[t][2][0], k, j * P:j * P + P], in_w16[w][:, k, DI:2 * DI],
                                             start=(n == 0), stop=(n == len(SPLIT) - 1))
                        last.then_inc(wide_full(key)[0], 1)

                    def y_t(t, j):
                        pe.wait_ge(sem["y_gated"], NJ * nM(t) + j + 1)
                        pe.wait_ge(*narrow_room(("y_t", t, j)))
                        for n in range(NB):
                            last = pe.transpose(narrow_ps[:, n * P:n * P + P], y_sb[:, slots[t][2][0], j, n * P:n * P + P], ident[:, :])
                        last.then_inc(sem["narrow_full"], 1)

                    def op(t, j):
                        key = ("op", t, j)
                        pe.wait_ge(*narrow_read(("y_t", t, j)))
                        pe.wait_ge(*wide_room(key))
                        for b in range(NB):
                            last = pe.matmul(wide_bank(key)[:, 0:DM], yT[:, j % 2, b, :], out_sb[:, b, :], start=(b == 0), stop=(b == NB - 1))
                        last.then_inc(wide_full(key)[0], 1)

                    def h2_t(t, k):
                        pe.wait_ge(sem["h2_made"], 2 * (nM(t) + 1))
                        pe.wait_ge(*narrow_room(("h2_t", t, k)))
                        for n in range(NJ):
                            last = pe.transpose(narrow_ps[:, n * P:n * P + P], h2[:, n, k * P:k * P + P], ident[:, :])
                        last.then_inc(sem["narrow_full"], 1)

                    def logit(t):
                        key = ("logit", t)
                        pe.wait_ge(*narrow_read(("h2_t", t, NK - 1)))
                        pe.wait_ge(*wide_room(key))
                        for j in range(NJ):
                            for n, (k, h, w) in enumerate(SPLIT):
                                last = pe.matmul(wide_bank(key)[:, j * NE:j * NE + NE], h2T[h][:, k, j * P:j * P + P], gate_w16[w][:, k, :],
                                                 start=(n == 0), stop=(n == len(SPLIT) - 1))
                        last.then_inc(wide_full(key)[0], 1)

                    def expert_in(t, u):
                        key = ("expert_in", t, u)
                        j = tile_of(u)
                        pe.wait_ge(*wide_room(key))
                        for n, (k, h, w) in enumerate(SPLIT):
                            last = pe.matmul(wide_bank(key), h2T[h][:, k, j * P:j * P + P], ein_w16[w][:, k, pair_of(u), :],
                                             start=(n == 0), stop=(n == len(SPLIT) - 1))
                        last.then_inc(wide_full(key)[0], 1)

                    def e_t(t, u):
                        pe.wait_ge(sem["e_weighed"], UNITS * nM(t) + u + 1)
                        pe.wait_ge(*narrow_room(("e_t", t, u)))
                        for n in range(2):
                            last = pe.transpose(narrow_ps[:, n * P:n * P + P], act[:, u % 3, n, :], ident[:, :])
                        last.then_inc(sem["narrow_full"], 1)

                    def expert_out(t, u):
                        pe.wait_ge(*narrow_read(("e_t", t, u)))
                        first = u % (2 * NPAIR) == 0
                        if first:
                            pe.wait_ge(sem["out_gated"], 2 * nM(t) + u // (2 * NPAIR))
                        for n in range(2):
                            last = pe.matmul(moe_ps[:, u % 2, :], hidT[:, u % 2, n, :], eout_sb[:, 2 * pair_of(u) + n, :],
                                             start=first and n == 0, stop=pair_of(u) == NPAIR - 1 and n == 1, skip_group_check=True)
                        last.then_inc(sem["expert_out_done"], 1)

                    walk({"hn_t": hn_t, "xi": xi, "xd": xd, "xd_t": xd_t, "dtp": dtp, "skip_t": skip_t,
                          "b_cast": b_cast, "rows": rows, "z": z, "y_t": y_t, "op": op, "h2_t": h2_t, "logit": logit,
                          "expert_in": expert_in, "e_t": e_t, "expert_out": expert_out})
            clear_semaphores()

        run_slots([(None, (0, 0), None), ((0, 0), (1, 1), None)], load_mod_p=0)
        with nc.Fori(0, BATCH - 1) as i:
            run_slots([((1, 2 * i + 1), (0, 2 * i + 2), (0, 2 * i)), ((0, 2 * i + 2), (1, 2 * i + 3), (1, 2 * i + 1))],
                      load_mod_p=i + 1, load_mod_m=i)
        run_slots([((1, NC - 1), None, (0, NC - 2)), (None, None, (1, NC - 1))], load_mod_m=BATCH - 1)


_INS = ("x", "norm_w", "in_w", "conv_w", "conv_b", "xproj_w", "dt_w", "dt_b", "a_log", "d_skip", "out_w",
        "gate_w", "e_in", "e_out", "c_t", "w_mod")


def kernel(L0_attn_x, L0_attn_norm_w, L0_attn_in_proj_w, L0_attn_conv_w, L0_attn_conv_b, L0_attn_x_proj_w,
           L0_attn_dt_proj_w, L0_attn_dt_proj_b, L0_attn_A_log, L0_attn_D, L0_attn_out_proj_w, L0_ffn_gate_w,
           L0_ffn_ws_in, L0_ffn_vs_in, L0_ffn_ws_out, L0_ffn_e_win, L0_ffn_e_vin, L0_ffn_e_wout, L0_c, L0_wmod):
    import concourse.bacc as bacc
    from concourse.bass_utils import run_bass_kernel_spmd

    def blocks(w):
        return np.ascontiguousarray(w.reshape(-1, P, w.shape[-1]).transpose(1, 0, 2))

    def chunks(a):
        return np.ascontiguousarray(a.reshape(NC, NJ, P, DM).transpose(0, 2, 1, 3))

    a = {k: np.asarray(v) for k, v in locals().items() if k.startswith("L0_")}
    win = np.concatenate([a["L0_ffn_e_win"], a["L0_ffn_ws_in"].reshape(DM, 2, HID).transpose(1, 0, 2)], 0)
    vin = np.concatenate([a["L0_ffn_e_vin"], a["L0_ffn_vs_in"].reshape(DM, 2, HID).transpose(1, 0, 2)], 0)
    e_in = np.concatenate([win, vin], 2)
    e_in = e_in.reshape(NPAIR, 2, NK, P, 2 * HID).transpose(3, 2, 0, 1, 4).reshape(P, NK, NPAIR, 4 * HID)
    e_out = np.concatenate([a["L0_ffn_e_wout"], a["L0_ffn_ws_out"].reshape(2, HID, DM)], 0).transpose(1, 0, 2)
    dt_at, b_at, c_at = np.arange(RANK), np.arange(RANK, RANK + NS), np.arange(RANK + NS, RANK + 2 * NS)
    columns = np.concatenate([b_at, dt_at, b_at, c_at])
    dt_w = np.zeros((NBT, DI), a["L0_attn_dt_proj_w"].dtype)
    dt_w[NS:NS + RANK] = a["L0_attn_dt_proj_w"].T
    arrays = {
        "x": chunks(a["L0_attn_x"]),
        "norm_w": a["L0_attn_norm_w"].reshape(NK, P).T,
        "in_w": blocks(a["L0_attn_in_proj_w"].T),
        "conv_w": blocks(a["L0_attn_conv_w"]),
        "conv_b": a["L0_attn_conv_b"].reshape(NB, P).T,
        "xproj_w": blocks(a["L0_attn_x_proj_w"][columns].T),
        "dt_w": dt_w,
        "dt_b": a["L0_attn_dt_proj_b"].reshape(NB, P).T,
        "a_log": blocks(a["L0_attn_A_log"]),
        "d_skip": a["L0_attn_D"].reshape(NB, P).T,
        "out_w": blocks(a["L0_attn_out_proj_w"].T),
        "gate_w": blocks(a["L0_ffn_gate_w"].T),
        "e_in": e_in,
        "e_out": e_out,
        "c_t": blocks(a["L0_c"].T),
        "w_mod": blocks(a["L0_wmod"]),
    }
    nc = bacc.Bacc("TRN2", target_bir_lowering=False, num_devices=1, dynamic_dma_scratch_size=1024)
    feed, args = {}, []
    for name in _INS:
        value = np.ascontiguousarray(arrays[name])
        feed[name + "_dram"] = value
        args.append(nc.dram_tensor(name + "_dram", value.shape, mybir.dt.from_np(value.dtype), kind="ExternalInput").ap())
    out = nc.dram_tensor("out_dram", (NC, P, NJ, DM), F32, kind="ExternalOutput").ap()
    adaln_block(nc, *args, out)
    r = run_bass_kernel_spmd(nc, [feed], core_ids=[0])
    got = r.results[0]["out_dram"]
    return np.ascontiguousarray(got.transpose(0, 2, 1, 3)).reshape(BATCH, SEQ, DM)
```

```python
from contextlib import ExitStack

import numpy as np

import concourse.bass as bass
from concourse import mybir

F32 = mybir.dt.float32
F16 = mybir.dt.float16
ALU = mybir.AluOpType
ACT = mybir.ActivationFunctionType
AX = mybir.AxisListType

BATCH, SEQ, DM = 8, 1024, 256
DI, NS, CONV, RANK = 512, 16, 4, 16
NE, TOPK, HID = 16, 4, 128
P = 128
CH = 512
NJ = CH // P
NC = BATCH * SEQ // CH
NB = DI // P
NK = DM // P
XD = RANK + 3 * NS
AT_C = RANK + 2 * NS
NBT = RANK + 2 * NS
LIFT = 64.0
NPAIR = NE // 2 + 1
NDA = 4
NWIDE, NNARROW = 3, 2
UNITS = NPAIR * NJ
EPS = 1e-5



def scan_steps(t):
    out = []
    for s in range(NS):
        out += [(4 * s - 5.414, ("b_cast", t, s)), (4 * s - 4.944, ("b_evac", t, s))]
        for b in range(NB):
            out += [(4 * s - 3.49 + b, ("scaled", t, s, b)), (4 * s - 2.24 + b, ("exp", t, s, b)), (4 * s + b + 0.2, ("scan", t, s, b))]
        for j in range(NJ):
            at = 4 * s + 4.114 + 0.725 * j
            out += [(at + 0.11, ("rows", t, s, j)), (at + 0.156, ("gather", t, s, j))] if j < NJ - 1 else \
                   [(at + 0.11, ("rows", t, s, j)), (at + 0.145, ("c_scale", t, s)), (at + 0.892, ("c_add", t, s))]
        out.append((4 * s + 3.25, ("carry", t, s)))
    return out


def prepare_steps(t):
    out = [(0, ("x_load", t))]
    for j in range(NJ):
        out.append((1 + 0.5 * j, ("x_stat", t, j)))
    out += [(3.5, ("x_rstd", t))] + [(4.5 + 0.3 * j, ("x_norm", t, j)) for j in range(NJ)]
    out += [(6.117, ("x_scale", t)), (6.117 + 1, ("x_shift", t))]
    out += [(8 + 0.3 * j, ("h_square", t, j)) for j in range(NJ)]
    out += [(10, ("h_rms", t)), (10.5, ("r_gate", t)), (11.5, ("r_add", t)), (11.6, ("r_store", t))]
    for j in range(NJ):
        out.append((12.5 + 0.4 * j, ("h_scale", t, j)))
    for k in range(NK):
        out += [(14.5 + 2 * k, ("hn_t", t, k)), (14.5 + 0.1 + 2 * k, ("hn_high", t, k)), (14.5 + 0.2 + 2 * k, ("hn_low", t, k))]
    for b in range(NB):
        at = 19.136 + 3.2 * b
        out += [(at, ("xi", t, b)), (at + 0.1, ("xi_center", t, b)), (at + 0.2, ("xi_copy", t, b)),
                (at + 0.3, ("halo", t, b))]
        out += [(at + 1.138 + 0.6 * n, ("tap", t, b, n)) for n in range(CONV - 1)]
        out += [(at + 2.7, ("u_tanh", t, b)), (at + 2.7 + 0.8, ("u", t, b))]
    out += [(34.0, ("xd", t)), (34.0 + 0.5, ("xd_evac", t))]
    out += [(35, ("xd_t", t)), (35.1, ("xd_t_evac", t)), (35.2, ("b_high", t)), (35.3, ("b_low", t))]
    for b in range(NB):
        out += [(41.0 + 0.8 * b, ("dtp", t, b)), (41.0 + 0.2 + 0.8 * b, ("dt_bias", t, b))]
        out += [(SOFT + 3.6 + b, ("delta", t, b)), (SOFT + 4.3 + 1.5 * b, ("du", t, b)),
                (SOFT + 5.8 + 1.5 * b, ("skip", t, b))]
        out += [(SOFT + 7 + 1.5 * b, ("skip_t", t, b)), (SOFT + 7.1 + 1.5 * b, ("skip_evac", t, b))]
    out += [(SOFT + at, (name, t, half)) for at, name, half in ((0, "soft_exp", 0), (1.5, "soft_exp", 1), (3, "soft_ln", 0), (3.01, "soft_ln", 1))]
    return out


def mix_steps(t):
    out = [(-0.9, ("r_load", t))]
    for j in range(NJ):
        at = -0.905 + 1.045 * j
        early = Z_AHEAD if t and j < 2 else 0.0
        out += [(at - early, ("z", t, j)), (at + 0.1 - early, ("z_tanh", t, j)), (at + 0.3 - early, ("z_gate", t, j))]
        out.append((at + (Y_LATE if t else Y_SOON), ("y_gate", t, j)))
        out += [(at + 1.5, ("y_t", t, j)), (at + 1.55, ("y_evac", t, j))]
        out += [(at + 2.205, ("op", t, j)), (at + 2.205 + 0.2, ("op_gate", t, j)), (at + 2.205 + 0.25, ("x1", t, j)), (at + 2.8, ("x1_stat", t, j))]
    out += [(6.2, ("x1_rstd", t))] + [(6.2 + 0.7 + 0.2 * j, ("x1_norm", t, j)) for j in range(NJ)]
    out += [(7.806, ("x1_scale", t)), (7.806 + 0.4, ("x1_shift", t))]
    for k in range(NK):
        out += [(9.14 + 0.6 * k, ("h2_t", t, k)), (9.14 + 0.1 + 0.6 * k, ("h2_high", t, k)), (9.14 + 0.2 + 0.6 * k, ("h2_low", t, k))]
    out += [(11.2, ("logit", t)), (11.2 + 0.1, ("logit_exp", t)), (11.2 + 0.6, ("router", t))]
    first, tick = 12.0, 51.872 / UNITS
    for u in range(UNITS):
        at = first + tick * u
        out += [(at, ("expert_in", t, u)), (at + 0.1, ("e_tanh", t, u)), (at + 0.368, ("e_act", t, u)),
                (at + 0.4, ("e_mul", t, u)), (at + 0.5, ("e_weigh", t, u)),
                (at + 0.685 + tick, ("e_t", t, u)), (at + 0.9 + tick, ("e_evac", t, u)),
                (at + 0.6 + 2 * tick, ("expert_out", t, u))]
        if u % (2 * NPAIR) == 2 * NPAIR - 1:
            out += [(at + 0.65 + 2 * tick, ("out_gate", t, u // (2 * NPAIR))), (at + 0.66 + 2 * tick, ("out_add", t, u // (2 * NPAIR))),
                    (at + 0.67 + 2 * tick, ("out_store", t, u // (2 * NPAIR)))]
    return out


LEAD_P0, LEAD_P, LEAD_M = 2.0, 8.0, 1.42
SOFT = 46.0
Z_AHEAD, Y_SOON, Y_LATE = -0.26, -1.863, 0.95
SLOT = 4 * NS + 3.236


def schedule(slots, load_mod_p, load_mod_m, first_block):
    out = [(SLOT * t - 0.95, t, 0, ("mod_m_load", t)) for t in load_mod_m]
    out += [(SLOT * t - LEAD_P + 0.5, t, 0, ("mod_p_load", t)) for t in load_mod_p]
    if first_block:
        out.append((SLOT - 2, 0, 0, ("eout_load",)))
        for n in range(NPAIR):
            at = SLOT + 2 + 6.5 * n
            out += [(at - 10, 0, 0, ("ein_load", n)), (at, 0, 0, ("ein_high", n)), (at + 0.6, 0, 0, ("ein_low", n))]
    for t, (s, p, m) in enumerate(slots):
        steps = []
        if s is not None:
            steps += scan_steps(t)
        if p is not None:
            steps += [(at - (LEAD_P0 if t == 0 else LEAD_P), what) for at, what in prepare_steps(t)]
        if m is not None:
            steps += [(at - LEAD_M if t == 0 else at, what) for at, what in mix_steps(t)]
        out += [(SLOT * t + at, t, n, what) for n, (at, what) in enumerate(steps)]
    order = [what for _, _, _, what in sorted(out, key=lambda x: (x[0], x[1], x[2]))]
    placed, done, filled = [], set(), {"wide": [], "narrow": []}
    for what in order:
        if what in done:
            continue
        ring, depth = ("wide", NWIDE) if what[0] in WIDE else ("narrow", NNARROW) if what[0] in NARROW else (None, 0)
        if ring:
            if len(filled[ring]) >= depth:
                old = filled[ring][-depth]
                for reader in (WIDE if ring == "wide" else NARROW)[old[0]]:
                    if (reader, *old[1:]) not in done:
                        done.add((reader, *old[1:]))
                        placed.append((reader, *old[1:]))
            filled[ring].append(what)
        done.add(what)
        placed.append(what)
    return placed


SPLIT = [(k, first, second) for k in range(NK) for first, second in ((0, 0), (0, 1), (1, 0))]

WIDE = {"xi": ("xi_center", "xi_copy"), "xd": ("xd_evac",), "dtp": ("dt_bias",), "z": ("z_tanh", "z_gate"),
        "op": ("op_gate",), "logit": ("logit_exp",), "expert_in": ("e_tanh", "e_act", "e_mul"), "b_cast": ("b_evac",)}
NARROW = {"hn_t": ("hn_high", "hn_low"), "xd_t": ("xd_t_evac", "b_high"), "skip_t": ("skip_evac",),
          "y_t": ("y_evac",), "h2_t": ("h2_high", "h2_low"), "e_t": ("e_evac",)}


def fills(order, names):
    return {what: n for n, what in enumerate(w for w in order if w[0] in names)}


def adaln_block(nc, x, norm_w, in_w, conv_w, conv_b, xproj_w, dt_w, dt_b, a_log, d_skip, out_w,
                gate_w, e_in, e_out, c_t, w_mod, out):
    ctx = ExitStack()
    with ctx:
        def sb(name, shape, dtype=F32):
            return ctx.enter_context(nc.sbuf_tensor(name, shape, dtype))

        def pb(name, shape):
            return ctx.enter_context(nc.psum_tensor(name, shape, F32))

        in_w16 = [sb(f"in_w_{n}", [P, NK, 2 * DI], F16) for n in ("high", "low")]
        out_sb = sb("out_sb", [P, NB, DM])
        ein_w16 = [sb(f"ein_w_{n}", [P, NK, NPAIR, 2 * 2 * HID], F16) for n in ("high", "low")]
        eout_sb = sb("eout_sb", [P, 2 * NPAIR, DM])
        xproj_sb = sb("xproj_sb", [P, NB, XD])
        dtw_sb = sb("dtw_sb", [NBT, DI])
        gate_w16 = [sb(f"gate_w_{n}", [P, NK, NE], F16) for n in ("high", "low")]
        select = sb("select", [NBT, NS], F16)
        norm_sb = sb("norm_sb", [P, NK])
        convw_sb = sb("convw_sb", [P, NB, CONV])
        convb_sb = sb("convb_sb", [P, NB])
        dtb_sb = sb("dtb_sb", [P, NB])
        skip_sb = sb("skip_sb", [P, NB])
        a_sb = sb("a_sb", [P, NB, NS])
        ident = sb("ident", [P, P])
        minus_half = sb("minus_half", [P, NJ])
        restart = sb("restart", [P, NJ, NE])
        mod_p = sb("mod_p", [P, 3, DM])
        mod_m = sb("mod_m", [P, 4, DM])
        hnT = [sb(f"hnT_{n}", [P, 2, NK, CH], F16) for n in ("high", "low")]
        xi_pad = sb("xi_pad", [P, 2, CONV - 1 + CH])
        halo_sb = sb("halo_sb", [P, NB, CONV - 1])
        conv = sb("conv", [P, 2, CH])
        r_sb = conv[:, :, :].rearrange("p a (b n) -> p (a b) n", n=DM)
        th_p = sb("th_p", [P, 2, CH])
        u_sb = sb("u_sb", [P, NB, CH])
        x_sb = th_p[:, :, :].rearrange("p a (b n) -> p (a b) n", n=DM)
        xdT = th_p[0:NBT, 1, :]
        delta = sb("delta", [P, 2, NB, CH])
        xd_sb = sb("xd_sb", [P, 2, NJ, XD])
        bT = sb("bT", [NBT, 2, CH], F16)
        du_sb = sb("du_sb", [P, 2, NB, CH])
        y_sb = sb("y_sb", [P, 2, NJ, DI])
        h_sb = u_sb[:, 0:2, :].rearrange("p a (b n) -> p (a b) n", n=DM)
        square = conv[:, 0, 0:DM]
        b_sb = sb("b_sb", [P, 2, CH])
        db_sb = sb("db_sb", [P, NB, CH])
        da_sb = sb("da_sb", [P, NDA, CH])
        states = sb("states", [P, 2 * NB, CH])
        c_rows = sb("c_rows", [P, 2, DI])
        carry = sb("carry", [P, NS, NB])
        zg = sb("zg", [P, 2, DI])
        yT = xi_pad[:, :, 0:CH].rearrange("p a (b n) -> p a b n", n=P)
        x1 = sb("x1", [P, NJ, DM])
        gated = sb("gated", [P, 2, DM])
        h2 = zg[:, :, :].rearrange("p a (b n) -> p (a b) n", n=DM)
        h2T = [sb(f"h2T_{n}", [P, NK, CH], F16) for n in ("high", "low")]
        act = sb("act", [P, 3, 2, HID])
        hidT = sb("hidT", [P, 2, 2, P])
        g_sb = sb("g_sb", [P, NJ, NE])
        rt = [sb(f"rt{n}", [P, NJ, NE]) for n in range(4)]
        rt_small = [sb(f"rt_small{n}", [P, NJ]) for n in range(2)]
        top = sb("top", [P, NJ, 8])
        weigh = sb("weigh", [P, NJ, 2 * NPAIR])
        bn = sb("bn", [P, 2, NJ, 6])
        mv = sb("mv", [P, 2, NJ, 2])
        rstd = sb("rstd", [P, 2, 2, NJ])
        ssq = sb("ssq", [P, NJ])
        rms = sb("rms", [P, 2, NJ])

        rows_ps = [pb(f"rows_ps{n}", [P, DI]) for n in range(2)]
        wide_ps = [pb(f"wide_ps{n}", [P, 512]) for n in range(NWIDE)]
        narrow_ps = [pb(f"narrow_ps{n}", [P, 512]) for n in range(NNARROW)]
        moe_ps = pb("moe_ps", [P, 2, DM])

        mod_dram = nc.dram_tensor("mod_dram", (BATCH, 6, DM), F32, kind="Internal").ap()
        r_dram = nc.dram_tensor("r_dram", (NC, P, NJ * DM), F32, kind="Internal").ap()

        SEMS = ("weights_in", "ein_in0", "ein_in1", "ein_high_done", "ein_low_done", "eout_in", "in_split", "const_made", "act_made", "folded", "mod_mm", "mod_made", "mod_stored",
                "mod_in_p", "mod_in_m", "x_in", "r_out", "r_in", "y_out",
                "x_bn", "x_mv", "x_rstd_tmp", "x_rstd_done", "x_norm_done", "h_made", "h_squared", "h_rms_done",
                "r_gated", "r_made", "h_scaled", "xi_centered", "halo_set", "tapped", "u_tanhed", "u_made",
                "halo_saved", "hn_high_done", "h2_high_done", "xd_t_read", "b_low_done", "soft_abs", "soft_exped", "soft_done", "delta_made", "du_made", "skip_made",
                "x1_bn", "x1_mv", "x1_rstd_done", "x1_normed", "h2_made", "z_tanhed", "z_gated", "y_gated",
                "x1_made", "logit_exped", "router_step", "router_done",
                "e_tanhed", "e_acted", "e_weighed", "expert_out_done", "out_gated", "out_added",
                "exp_done", "scaled_done", "c_scaled", "c_added", "scan_done", "carried", "rows_full", "gathered",
                *(f"{ring}_{what}{n}" for ring, depth in (("wide", NWIDE), ("narrow", NNARROW)) for what in ("full", "free")
                  for n in range(depth)))
        sem = {name: ctx.enter_context(nc.semaphore(name)) for name in SEMS}

        def clear_semaphores():
            engines = (nc.sync, nc.gpsimd, nc.scalar, nc.vector, nc.tensor)
            for n, s in enumerate(sem.values()):
                engines[n % len(engines)].sem_clear(s)
            nc.all_engine_barrier()

        wmod_sb = y_sb[:, :, :, :].rearrange("p a j n -> p (a j n)")[:, 0:NK * 6 * DM]
        wmod_sb = wmod_sb.rearrange("p (k n) -> p k n", k=NK)
        ct_sb = th_p[:, 0, 0:NK * BATCH].rearrange("p (k b) -> p k b", k=NK)
        ct_half = th_p[:, 1, 0:NK * BATCH].rearrange("p (k b) -> p k b", k=NK)
        ct_tanh = conv[:, 0, 0:NK * BATCH].rearrange("p (k b) -> p k b", k=NK)
        mod_row = db_sb[0:BATCH, 0:2, :].rearrange("b j n -> b (j n)")
        mod_row2 = db_sb[0:BATCH, 3, :]
        mod_tmp = db_sb[0:BATCH, 2, :]

        in_raw = states[:, 0:4, :].rearrange("p a n -> p (a n)").rearrange("p (k n) -> p k n", k=NK)
        gate_raw = conv[:, 1, 0:NK * NE].rearrange("p (k e) -> p k e", k=NK)
        ein_raw = [x1[:, :, :].rearrange("p (k a) n -> p k (a n)", k=NK), zg[:, :, :]]
        LOADS = [(in_raw, in_w), (out_sb[:, :, :], out_w),
                 (xproj_sb[:, :, :], xproj_w), (dtw_sb[:, :], dt_w), (gate_raw, gate_w), (norm_sb[:, :], norm_w),
                 (convw_sb[:, :, :], conv_w), (convb_sb[:, :], conv_b), (dtb_sb[:, :], dt_b), (skip_sb[:, :], d_skip),
                 (a_sb[:, :, :], a_log), (wmod_sb, w_mod), (ct_sb, c_t)]
        with nc.Block() as block:
            @block.sync
            def _(sp):
                for dst, src in LOADS:
                    sp.dma_start(dst, src).then_inc(sem["weights_in"], 16)
                sp.wait_ge(sem["mod_made"], 11)
                rows = [mod_row[:, 512 * n:512 * n + 512] for n in range(2)] + [mod_row2]
                for n in range(3):
                    sp.dma_start(mod_dram[:, 2 * n:2 * n + 2, :].rearrange("b a n -> b (a n)"), rows[n]).then_inc(sem["mod_stored"], 16)
                sp.wait_ge(sem["mod_stored"], 3 * 16)

            @block.gpsimd
            def _(pool):
                pool.memset(ident[:, :], 0.0).then_inc(sem["const_made"], 1)
                pool.memset(minus_half[:, :], -0.5).then_inc(sem["const_made"], 1)
                pool.memset(restart[:, :, :], 1.0).then_inc(sem["const_made"], 1)
                pool.memset(weigh[:, :, :], 0.5 / LIFT ** 2).then_inc(sem["const_made"], 1)
                pool.memset(select[:, :], 0.0).then_inc(sem["const_made"], 1)
                pool.wait_ge(sem["const_made"], 5)
                pool.affine_select(out=select[:, :], in_=select[:, :], compare_op=ALU.not_equal, fill=1.0, base=0,
                                   pattern=[[-1, NS]], channel_multiplier=1).then_inc(sem["const_made"], 1)
                pool.wait_ge(sem["const_made"], 6)
                pool.affine_select(out=select[:, :], in_=select[:, :], compare_op=ALU.not_equal, fill=1.0, base=-32,
                                   pattern=[[-1, NS]], channel_multiplier=1).then_inc(sem["const_made"], 1)
                pool.affine_select(out=ident[:, :], in_=ident[:, :], compare_op=ALU.not_equal, fill=1.0, base=0,
                                   pattern=[[-1, P]], channel_multiplier=1).then_inc(sem["const_made"], 1)
                pool.memset(restart[:, :, 0:1], 0.0).then_inc(sem["const_made"], 1)

            @block.scalar
            def _(act_e):
                act_e.wait_ge(sem["weights_in"], 16 * len(LOADS))
                act_e.activation(a_sb[:, :, :], a_sb[:, :, :], ACT.Exp).then_inc(sem["act_made"], 1)
                act_e.activation(ct_tanh, ct_sb, ACT.Tanh, scale=0.5).then_inc(sem["act_made"], 1)

            @block.vector
            def _(v):
                v.wait_ge(sem["weights_in"], 16 * len(LOADS))
                v.tensor_scalar(ct_half, ct_sb, 0.5, None, ALU.mult).then_inc(sem["folded"], 1)
                v.wait_ge(sem["folded"], 1)
                v.wait_ge(sem["act_made"], 2)
                v.scalar_tensor_tensor(ct_half, ct_tanh, 1.0, ct_half, ALU.add, ALU.mult).then_inc(sem["mod_made"], 1)
                for k in range(NK):
                    v.tensor_scalar(in_raw[:, k, :], in_raw[:, k, :], norm_sb[:, k:k + 1], LIFT, ALU.mult, ALU.mult).then_inc(sem["folded"], 1)
                v.tensor_scalar(convw_sb[:, :, :], convw_sb[:, :, :], 0.5 / LIFT, None, ALU.mult).then_inc(sem["folded"], 1)
                v.tensor_scalar(convb_sb[:, :], convb_sb[:, :], 0.5, None, ALU.mult).then_inc(sem["folded"], 1)
                v.tensor_scalar(out_sb[:, :, :], out_sb[:, :, :], 0.5 / LIFT, None, ALU.mult).then_inc(sem["folded"], 1)
                v.tensor_scalar(a_sb[:, :, :], a_sb[:, :, :], -1.0, None, ALU.mult).then_inc(sem["folded"], 1)
                v.tensor_scalar(gate_raw, gate_raw, LIFT, None, ALU.mult).then_inc(sem["folded"], 1)
                v.wait_ge(sem["folded"], NK + 6)
                v.tensor_copy(in_w16[0][:, :, :], in_raw).then_inc(sem["in_split"], 1)
                v.tensor_copy(gate_w16[0][:, :, :], gate_raw).then_inc(sem["in_split"], 1)
                v.wait_ge(sem["in_split"], 2)
                v.tensor_tensor(in_w16[1][:, :, :], in_raw, in_w16[0][:, :, :], ALU.subtract).then_inc(sem["in_split"], 1)
                v.tensor_tensor(gate_w16[1][:, :, :], gate_raw, gate_w16[0][:, :, :], ALU.subtract).then_inc(sem["in_split"], 1)
                v.wait_ge(sem["mod_mm"], 1)
                v.tensor_copy(mod_row[:, 0:512], wide_ps[0][0:BATCH, :]).then_inc(sem["mod_made"], 1)
                v.tensor_copy(mod_row[:, 512:1024], wide_ps[1][0:BATCH, :]).then_inc(sem["mod_made"], 1)
                v.tensor_copy(mod_row2, rows_ps[0][0:BATCH, :]).then_inc(sem["mod_made"], 1)
                v.wait_ge(sem["mod_made"], 4)
                v.tensor_scalar(mod_row[:, DM:2 * DM], mod_row[:, DM:2 * DM], 1.0, None, ALU.add).then_inc(sem["mod_made"], 1)
                v.tensor_scalar(mod_row2[:, 0:DM], mod_row2[:, 0:DM], 1.0, None, ALU.add).then_inc(sem["mod_made"], 1)
                gates = [mod_row[:, 2 * DM:3 * DM], mod_row2[:, DM:2 * DM]]
                for n, g in enumerate(gates):
                    v.tensor_scalar(mod_tmp[:, DM * n:DM * n + DM], g, 0.0, 2.0, ALU.is_ge, ALU.mult).then_inc(sem["mod_made"], 1)
                v.wait_ge(sem["mod_made"], 8)
                v.tensor_scalar(mod_tmp, mod_tmp, 1.0, None, ALU.subtract).then_inc(sem["mod_made"], 1)
                v.wait_ge(sem["mod_made"], 9)
                for n, g in enumerate(gates):
                    v.tensor_tensor(g, g, mod_tmp[:, DM * n:DM * n + DM], ALU.mult).then_inc(sem["folded"], 1)
                v.wait_ge(sem["folded"], NK + 8)
                for n, g in enumerate(gates):
                    v.scalar_tensor_tensor(g, g, 0.25, mod_tmp[:, DM * n:DM * n + DM], ALU.max, ALU.mult).then_inc(sem["mod_made"], 1)

            @block.tensor
            def _(pe):
                pe.wait_ge(sem["mod_made"], 1)
                for n, bank in enumerate((wide_ps[0], wide_ps[1], rows_ps[0])):
                    for k in range(NK):
                        last = pe.matmul(bank[0:BATCH, :], ct_half[:, k, :], wmod_sb[:, k, 512 * n:512 * n + 512],
                                         start=(k == 0), stop=(k == NK - 1))
                last.then_inc(sem["mod_mm"], 1)
        clear_semaphores()

        def run_slots(slots, load_mod_p, load_mod_m, first_block=False):
            order = schedule(slots, load_mod_p, load_mod_m, first_block)
            wide = fills(order, WIDE)
            narrow = fills(order, NARROW)

            def rows_in(load_mod, t):
                return sum(n <= t for n in load_mod)

            def stages_before(t, kind):
                return sum(slots[n][kind] is not None for n in range(t))

            def nS(t):
                return stages_before(t, 0)

            def nP(t):
                return stages_before(t, 1)

            def nM(t):
                return stages_before(t, 2)

            def wide_bank(key):
                return wide_ps[wide[key] % NWIDE][:, :]

            def wide_room(key):
                return sem[f"wide_free{wide[key] % NWIDE}"], wide[key] // NWIDE

            def wide_full(key):
                return sem[f"wide_full{wide[key] % NWIDE}"], wide[key] // NWIDE + 1

            def wide_read(key):
                return sem[f"wide_free{wide[key] % NWIDE}"], wide[key] // NWIDE + 1

            def narrow_bank(key):
                return narrow_ps[narrow[key] % NNARROW][:, :]

            def narrow_room(key):
                return sem[f"narrow_free{narrow[key] % NNARROW}"], narrow[key] // NNARROW

            def narrow_full(key):
                return sem[f"narrow_full{narrow[key] % NNARROW}"], narrow[key] // NNARROW + 1

            def narrow_read(key):
                return sem[f"narrow_free{narrow[key] % NNARROW}"], narrow[key] // NNARROW + 1

            def soft_place(b):
                return (th_p, conv)[b // 2][:, b % 2, :]

            def walk(steps):
                for name, *where in order:
                    if name in steps:
                        steps[name](*where)

            def pair_of(u):
                return u % (2 * NPAIR) // 2

            def tile_of(u):
                return 2 * (u // (2 * NPAIR)) + u % 2

            with nc.Block() as block:
                @block.sync
                def _(sp):
                    def mod_p_load(t):
                        if nP(t):
                            sp.wait_ge(sem["h_made"], 2 * nP(t))
                            sp.wait_ge(sem["r_gated"], nP(t))
                        row = mod_dram[bass.ds(load_mod_p[t], 1), 0:3, :].rearrange("o a n -> o (a n)")
                        sp.dma_start(mod_p[:, :, :].rearrange("p a n -> p (a n)"), row.broadcast_to([P, 3 * DM])).then_inc(sem["mod_in_p"], 16)

                    def mod_m_load(t):
                        if nM(t):
                            sp.wait_ge(sem["out_gated"], 2 * nM(t))
                        row = mod_dram[bass.ds(load_mod_m[t], 1), 2:6, :].rearrange("o a n -> o (a n)")
                        sp.dma_start(mod_m[:, :, :].rearrange("p a n -> p (a n)"), row.broadcast_to([P, 4 * DM])).then_inc(sem["mod_in_m"], 16)

                    def x_load(t):
                        if nP(t):
                            sp.wait_ge(sem["delta_made"], NB * nP(t))
                        sp.dma_start(x_sb[:, :, :], x[bass.ds(slots[t][1][1], 1)].rearrange("o p j n -> (o p) j n")).then_inc(sem["x_in"], 16)

                    def r_store(t):
                        sp.wait_ge(sem["r_made"], nP(t) + 1)
                        sp.dma_start(r_dram[bass.ds(slots[t][1][1], 1)].rearrange("o p n -> (o p) n"),
                                     conv[:, :, :].rearrange("p a n -> p (a n)")).then_inc(sem["r_out"], 16)

                    def r_load(t):
                        if nM(t):
                            sp.wait_ge(sem["y_out"], nM(t) * 32)
                        sp.dma_start(x1[:, :, :].rearrange("p j n -> p (j n)"),
                                     r_dram[bass.ds(slots[t][2][1], 1)].rearrange("o p n -> (o p) n")).then_inc(sem["r_in"], 16)

                    def out_store(t, q):
                        sp.wait_ge(sem["out_added"], 2 * nM(t) + q + 1)
                        sp.dma_start(out[bass.ds(slots[t][2][1], 1), :, 2 * q:2 * q + 2, :].rearrange("o p j n -> (o p) j n"),
                                     x1[:, 2 * q:2 * q + 2, :]).then_inc(sem["y_out"], 16)

                    def eout_load():
                        sp.dma_start(eout_sb[:, :, :], e_out).then_inc(sem["eout_in"], 16)

                    def ein_load(n):
                        if n >= 2:
                            sp.wait_ge(sem["ein_low_done"], n - 1)
                        sp.dma_start(ein_raw[n % 2], e_in[:, :, n, :]).then_inc(sem[f"ein_in{n % 2}"], 16)

                    walk({"eout_load": eout_load, "ein_load": ein_load, "mod_p_load": mod_p_load, "mod_m_load": mod_m_load, "x_load": x_load, "r_store": r_store, "r_load": r_load, "out_store": out_store})
                    if first_block:
                        sp.wait_ge(sem["eout_in"], 16)
                    sp.wait_ge(sem["r_out"], 16 * nP(len(slots)))
                    sp.wait_ge(sem["y_out"], 32 * nM(len(slots)))

                @block.gpsimd
                def _(pool):
                    def x_rstd(t):
                        pool.wait_ge(sem["x_mv"], NJ * (nP(t) + 1))
                        pool.tensor_scalar(rstd[:, 0, 0, :], mv[:, 0, :, 1], EPS, None, ALU.add).then_inc(sem["x_rstd_tmp"], 1)
                        own[0] += 1
                        pool.wait_ge(sem["x_rstd_tmp"], own[0])
                        pool.tensor_tensor(rstd[:, 0, 1, :], rstd[:, 0, 0, :], minus_half[:, :], ALU.pow).then_inc(sem["x_rstd_done"], 1)

                    def h_rms(t):
                        pool.wait_ge(sem["h_squared"], NJ * (nP(t) + 1))
                        pool.tensor_scalar(rms[:, 0, :], ssq[:, :], 1.0 / DM, EPS, ALU.mult, ALU.add).then_inc(sem["x_rstd_tmp"], 1)
                        own[0] += 1
                        pool.wait_ge(sem["x_rstd_tmp"], own[0])
                        pool.tensor_tensor(rms[:, 1, :], rms[:, 0, :], minus_half[:, :], ALU.pow).then_inc(sem["h_rms_done"], 1)

                    def r_gate(t):
                        pool.wait_ge(sem["h_made"], 2 * (nP(t) + 1))
                        pool.wait_ge(sem["h_squared"], NJ * (nP(t) + 1))
                        pool.wait_ge(sem["mod_in_p"], 16 * rows_in(load_mod_p, t))
                        pool.tensor_tensor(r_sb[:, :, :], h_sb[:, :, :], mod_p[:, 2:3, :].broadcast_to([P, NJ, DM]), ALU.mult).then_inc(sem["r_gated"], 1)

                    def r_add(t):
                        pool.wait_ge(sem["r_gated"], nP(t) + 1)
                        pool.tensor_tensor(r_sb[:, :, :], r_sb[:, :, :], x_sb[:, :, :], ALU.add).then_inc(sem["r_made"], 1)

                    def du(t, b):
                        pool.wait_ge(sem["delta_made"], NB * nP(t) + b + 1)
                        pool.tensor_tensor(du_sb[:, slots[t][1][0], b, :], delta[:, slots[t][1][0], b, :], u_sb[:, b, :], ALU.mult).then_inc(sem["du_made"], 1)

                    def scaled(t, s, b):
                        n = (NS * nS(t) + s) * NB + b
                        pool.wait_ge(*wide_read(("b_cast", t, s)))
                        if nP(t):
                            pool.wait_ge(sem["du_made"], NB * nP(t))
                        pool.wait_ge(sem["scan_done"], max(0, n - NB + 1))
                        pool.tensor_tensor(db_sb[:, b, :], du_sb[:, slots[t][0][0], b, :], b_sb[:, s % 2, :], ALU.mult).then_inc(sem["scaled_done"], 1)

                    def c_add(t, s):
                        n = NS * nS(t) + s
                        pool.wait_ge(sem["c_scaled"], n + 1)
                        pool.wait_ge(sem["c_added"], n)
                        if s == 0 and t > 0 and slots[t - 1][1] is not None:
                            pool.wait_ge(*narrow_read(("skip_t", t - 1, NB - 1)))
                        place = y_sb[:, slots[t][0][0], NJ - 1, :]
                        pool.tensor_tensor(place, place, c_rows[:, n % 2, :], ALU.add).then_inc(sem["c_added"], 1)

                    def y_gate(t, j):
                        pool.wait_ge(*wide_read(("z", t, j)))
                        if nS(t):
                            pool.wait_ge(sem["gathered"], nS(t) * NS * (NJ - 1))
                            pool.wait_ge(sem["c_added"], nS(t) * NS)
                        place = y_sb[:, slots[t][2][0], j, :]
                        pool.tensor_tensor(place, place, zg[:, j % 2, :], ALU.mult).then_inc(sem["y_gated"], 1)

                    def x1_rstd(t):
                        pool.wait_ge(sem["x1_mv"], NJ * (nM(t) + 1))
                        pool.tensor_scalar(rstd[:, 1, 0, :], mv[:, 1, :, 1], EPS, None, ALU.add).then_inc(sem["x_rstd_tmp"], 1)
                        own[0] += 1
                        pool.wait_ge(sem["x_rstd_tmp"], own[0])
                        pool.tensor_tensor(rstd[:, 1, 1, :], rstd[:, 1, 0, :], minus_half[:, :], ALU.pow).then_inc(sem["x1_rstd_done"], 1)

                    def e_weigh(t, u):
                        pool.wait_ge(sem["router_done"], nM(t) + 1)
                        pool.wait_ge(*wide_read(("expert_in", t, u)))
                        place = act[:, u % 3, :, :]
                        pool.tensor_tensor(place, place, weigh[:, tile_of(u), 2 * pair_of(u):2 * pair_of(u) + 2].unsqueeze(2).broadcast_to([P, 2, HID]),
                                           ALU.mult).then_inc(sem["e_weighed"], 1)

                    own = [0]
                    walk({"x_rstd": x_rstd, "h_rms": h_rms, "r_gate": r_gate, "r_add": r_add, "du": du,
                          "scaled": scaled, "c_add": c_add, "y_gate": y_gate, "x1_rstd": x1_rstd, "e_weigh": e_weigh})

                @block.scalar
                def _(ac):
                    def h_square(t, j):
                        ac.wait_ge(sem["h_made"], 2 * (nP(t) + 1))
                        if nP(t):
                            ac.wait_ge(sem["h_rms_done"], nP(t))
                            ac.wait_ge(sem["delta_made"], NB * nP(t))
                        ac.wait_ge(sem["h_squared"], NJ * nP(t) + j)
                        ac.activation(square, h_sb[:, j, :], ACT.Square, accum_out=ssq[:, j:j + 1]).then_inc(sem["h_squared"], 1)

                    def h_scale(t, j):
                        ac.wait_ge(sem["h_rms_done"], nP(t) + 1)
                        ac.wait_ge(sem["r_gated"], nP(t) + 1)
                        ac.wait_ge(sem["h_squared"], NJ * nP(t) + j + 1)
                        ac.activation(h_sb[:, j, :], h_sb[:, j, :], ACT.Copy, scale=rms[:, 1, j:j + 1]).then_inc(sem["h_scaled"], 1)

                    def hn_high(t, k):
                        if slots[t][2] is not None:
                            for j in range(2, NJ):
                                ac.wait_ge(*wide_full(("z", t, j)))
                        ac.wait_ge(*narrow_full(("hn_t", t, k)))
                        ac.activation(hnT[0][:, slots[t][1][0], k, :], narrow_bank(("hn_t", t, k)), ACT.Copy).then_inc(sem["hn_high_done"], 1)

                    def xi_center(t, b):
                        key = ("xi", t, b)
                        n = NB * nP(t) + b
                        ac.wait_ge(*wide_full(key))
                        ac.wait_ge(sem["u_made"], max(0, n - 1))
                        ac.wait_ge(sem["r_out"], 16 * (nP(t) + 1))
                        ac.activation(conv[:, b % 2, :], wide_bank(key), ACT.Identity, scale=convw_sb[:, b, CONV - 1:CONV],
                                      bias=convb_sb[:, b:b + 1]).then_inc(sem["xi_centered"], 1)

                    def xi_copy(t, b):
                        key = ("xi", t, b)
                        n = NB * nP(t) + b
                        if b < 2 and slots[t][2] is not None:
                            for j in range(2, NJ):
                                ac.wait_ge(*wide_full(("op", t, j)))
                        ac.wait_ge(sem["tapped"], max(0, (CONV - 1) * (n - 1)))
                        ac.wait_ge(sem["halo_saved"], max(0, n - 1))
                        ac.activation(xi_pad[:, b % 2, CONV - 1:], wide_bank(key), ACT.Copy).then_inc(wide_read(key)[0], 1)

                    def u_tanh(t, b):
                        n = NB * nP(t) + b
                        ac.wait_ge(sem["tapped"], (CONV - 1) * (n + 1))
                        ac.wait_ge(sem["u_made"], max(0, n - 1))
                        if nP(t):
                            ac.wait_ge(sem["delta_made"], NB * nP(t))
                        ac.activation(th_p[:, b % 2, :], conv[:, b % 2, :], ACT.Tanh).then_inc(sem["u_tanhed"], 1)

                    def xd_t_evac(t):
                        ac.wait_ge(sem["u_made"], NB * (nP(t) + 1))
                        ac.wait_ge(*narrow_full(("xd_t", t)))
                        ac.activation(xdT, narrow_bank(("xd_t", t))[0:NBT, :], ACT.Copy).then_inc(sem["xd_t_read"], 1)

                    def b_high(t):
                        if nS(t):
                            ac.wait_ge(sem["scaled_done"], NB * NS * nS(t))
                        ac.wait_ge(*narrow_full(("xd_t", t)))
                        ac.activation(bT[:, slots[t][1][0], :], narrow_bank(("xd_t", t))[0:NBT, :], ACT.Copy).then_inc(narrow_read(("xd_t", t))[0], 1)

                    def dt_bias(t, b):
                        key = ("dtp", t, b)
                        ac.wait_ge(*wide_full(key))
                        ac.activation(delta[:, slots[t][1][0], b, :], wide_bank(key), ACT.Identity, bias=dtb_sb[:, b:b + 1]).then_inc(wide_read(key)[0], 1)

                    def soft_exp(t, half):
                        n = 2 * nP(t) + half
                        for b in range(NB):
                            ac.wait_ge(*wide_read(("dtp", t, b)))
                        ac.wait_ge(sem["b_low_done"], nP(t) + 1)
                        place = (th_p, conv)[half][:, :, :]
                        ac.activation(place, delta[:, slots[t][1][0], 2 * half:2 * half + 2, :], ACT.Abs).then_inc(sem["soft_abs"], 1)
                        ac.wait_ge(sem["soft_abs"], n + 1)
                        ac.activation(place, place, ACT.Exp, scale=-1.0).then_inc(sem["soft_exped"], 1)

                    def soft_ln(t, half):
                        ac.wait_ge(sem["soft_exped"], 2 * nP(t) + half + 1)
                        place = (th_p, conv)[half][:, :, :]
                        ac.activation(place, place, ACT.Ln, bias=1.0).then_inc(sem["soft_done"], 1)

                    def b_evac(t, s):
                        ac.wait_ge(sem["scaled_done"], max(0, NB * (NS * nS(t) + s - 1)))
                        ac.wait_ge(*wide_full(("b_cast", t, s)))
                        ac.activation(b_sb[:, s % 2, :], wide_bank(("b_cast", t, s)), ACT.Copy).then_inc(wide_read(("b_cast", t, s))[0], 1)

                    def c_scale(t, s):
                        n = NS * nS(t) + s
                        ac.wait_ge(sem["rows_full"], NJ * (n + 1))
                        ac.wait_ge(sem["c_added"], max(0, n - 1))
                        ac.activation(c_rows[:, n % 2, :], rows_ps[1][:, :], ACT.Copy,
                                      scale=xd_sb[:, slots[t][0][0], NJ - 1, AT_C + s:AT_C + s + 1]).then_inc(sem["c_scaled"], 1)

                    def skip(t, b):
                        ac.wait_ge(sem["du_made"], NB * nP(t) + b + 1)
                        ac.activation(u_sb[:, b, :], u_sb[:, b, :], ACT.Copy, scale=skip_sb[:, b:b + 1]).then_inc(sem["skip_made"], 1)

                    def skip_evac(t, b):
                        if slots[t][2] is not None:
                            ac.wait_ge(*narrow_full(("y_t", t, NJ - 1)))
                        ac.wait_ge(*narrow_full(("skip_t", t, b)))
                        ac.activation(y_sb[:, slots[t][1][0], :, b * P:b * P + P],
                                      narrow_bank(("skip_t", t, b)).rearrange("p (j n) -> p j n", j=NJ), ACT.Copy).then_inc(narrow_read(("skip_t", t, b))[0], 1)

                    def exp(t, s, b):
                        n = (NS * nS(t) + s) * NB + b
                        if nP(t):
                            ac.wait_ge(sem["delta_made"], NB * nP(t))
                        ac.wait_ge(sem["scan_done"], max(0, n - NDA + 1))
                        ac.activation(da_sb[:, n % NDA, :], delta[:, slots[t][0][0], b, :], ACT.Exp,
                                      scale=a_sb[:, b, s:s + 1]).then_inc(sem["exp_done"], 1)

                    def z_tanh(t, j):
                        key = ("z", t, j)
                        n = NJ * nM(t) + j
                        ac.wait_ge(*wide_full(key))
                        ac.wait_ge(sem["y_gated"], max(0, n - 1))
                        if nM(t):
                            last = [q for q in range(t) if slots[q][2] is not None][-1]
                            for k in range(NK):
                                ac.wait_ge(*narrow_full(("h2_t", last, k)))
                        ac.activation(zg[:, j % 2, :], wide_bank(key), ACT.Tanh, scale=0.5 / LIFT).then_inc(sem["z_tanhed"], 1)

                    def y_evac(t, j):
                        ac.wait_ge(*narrow_full(("y_t", t, j)))
                        if j >= 2:
                            ac.wait_ge(*wide_full(("op", t, j - 2)))
                        elif nP(t):
                            ac.wait_ge(sem["tapped"], (CONV - 1) * NB * nP(t))
                            ac.wait_ge(sem["halo_saved"], NB * nP(t))
                        ac.activation(yT[:, j % 2, :, :], narrow_bank(("y_t", t, j)).rearrange("p (b n) -> p b n", b=NB), ACT.Copy).then_inc(narrow_read(("y_t", t, j))[0], 1)

                    def h2_high(t, k):
                        ac.wait_ge(*narrow_full(("h2_t", t, k)))
                        if nM(t):
                            last = [n for n in range(t) if slots[n][2] is not None][-1]
                            ac.wait_ge(*wide_full(("expert_in", last, UNITS - 1)))
                            ac.wait_ge(*wide_full(("expert_in", last, UNITS - 2)))
                        ac.activation(h2T[0][:, k, :], narrow_bank(("h2_t", t, k)), ACT.Copy).then_inc(sem["h2_high_done"], 1)

                    def logit_exp(t):
                        key = ("logit", t)
                        ac.wait_ge(*wide_full(key))
                        if nM(t):
                            ac.wait_ge(sem["router_done"], nM(t))
                        ac.activation(g_sb[:, :, :], wide_bank(key)[:, 0:NJ * NE].rearrange("p (j e) -> p j e", j=NJ), ACT.Exp, scale=-1.0 / LIFT).then_inc(wide_read(key)[0], 1)

                    def e_tanh(t, u):
                        key = ("expert_in", t, u)
                        n = UNITS * nM(t) + u
                        ac.wait_ge(*wide_full(key))
                        if n >= 3:
                            ac.wait_ge(*narrow_full(unit_key("e_t", n - 3)))
                        hin = wide_bank(key).rearrange("p (e a h) -> p e a h", e=2, a=2)[:, :, 0, :]
                        ac.activation(act[:, u % 3, :, :], hin, ACT.Tanh, scale=0.5 / LIFT).then_inc(sem["e_tanhed"], 1)

                    def unit_key(name, n):
                        tt = [t for t in range(len(slots)) if slots[t][2] is not None][n // UNITS]
                        return (name, tt, n % UNITS)

                    def e_evac(t, u):
                        n = UNITS * nM(t) + u
                        ac.wait_ge(*narrow_full(("e_t", t, u)))
                        ac.wait_ge(sem["expert_out_done"], max(0, n - 1))
                        ac.activation(hidT[:, u % 2, :, :], narrow_bank(("e_t", t, u))[:, 0:2 * P].rearrange("p (e n) -> p e n", e=2), ACT.Copy).then_inc(narrow_read(("e_t", t, u))[0], 1)

                    def ein_high(n):
                        ac.wait_ge(sem[f"ein_in{n % 2}"], 16 * (n // 2 + 1))
                        ac.activation(ein_w16[0][:, :, n, :], ein_raw[n % 2], ACT.Copy, scale=LIFT).then_inc(sem["ein_high_done"], 1)

                    walk({"ein_high": ein_high, "h_square": h_square, "h_scale": h_scale, "hn_high": hn_high, "xi_center": xi_center,
                          "xi_copy": xi_copy, "u_tanh": u_tanh, "xd_t_evac": xd_t_evac, "b_high": b_high, "dt_bias": dt_bias, "soft_exp": soft_exp, "soft_ln": soft_ln,
                          "b_evac": b_evac, "c_scale": c_scale, "skip": skip, "skip_evac": skip_evac, "exp": exp, "z_tanh": z_tanh, "y_evac": y_evac,
                          "h2_high": h2_high, "logit_exp": logit_exp, "e_tanh": e_tanh, "e_evac": e_evac})

                @block.vector
                def _(v):
                    def x_stat(t, j):
                        v.wait_ge(sem["x_in"], 16 * (nP(t) + 1))
                        if nP(t):
                            v.wait_ge(sem["x_norm_done"], NJ * nP(t))
                        v.bn_stats(bn[:, 0, j, :], x_sb[:, j, :]).then_inc(sem["x_bn"], 1)
                        v.wait_ge(sem["x_bn"], NJ * nP(t) + j + 1)
                        v.bn_aggr(mv[:, 0, j, :], bn[:, 0, j, :]).then_inc(sem["x_mv"], 1)

                    def x_norm(t, j):
                        v.wait_ge(sem["x_rstd_done"], nP(t) + 1)
                        if nP(t):
                            last = [q for q in range(t) if slots[q][1] is not None][-1]
                            v.wait_ge(*narrow_full(("skip_t", last, NB - 1)))
                        v.tensor_scalar(h_sb[:, j, :], x_sb[:, j, :], mv[:, 0, j, 0:1], rstd[:, 0, 1, j:j + 1],
                                        ALU.subtract, ALU.mult).then_inc(sem["x_norm_done"], 1)

                    def x_scale(t):
                        v.wait_ge(sem["mod_in_p"], 16 * rows_in(load_mod_p, t))
                        v.wait_ge(sem["x_norm_done"], NJ * (nP(t) + 1))
                        v.tensor_tensor(h_sb[:, :, :], h_sb[:, :, :], mod_p[:, 1:2, :].broadcast_to([P, NJ, DM]), ALU.mult).then_inc(sem["h_made"], 1)

                    def x_shift(t):
                        v.wait_ge(sem["h_made"], 2 * nP(t) + 1)
                        v.tensor_tensor(h_sb[:, :, :], h_sb[:, :, :], mod_p[:, 0:1, :].broadcast_to([P, NJ, DM]), ALU.add).then_inc(sem["h_made"], 1)

                    def halo(t, b):
                        n = NB * nP(t) + b
                        par = slots[t][1][0]
                        v.wait_ge(sem["tapped"], max(0, (CONV - 1) * (n - 1)))
                        v.wait_ge(sem["halo_saved"], max(0, n - 1))
                        if b < 2 and slots[t][2] is not None:
                            for j in range(2, NJ):
                                v.wait_ge(*wide_full(("op", t, j)))
                        if par == 0:
                            v.memset(xi_pad[:, b % 2, 0:CONV - 1], 0.0).then_inc(sem["halo_set"], 1)
                        else:
                            if nP(t):
                                v.wait_ge(sem["halo_saved"], NB * nP(t))
                            v.tensor_copy(xi_pad[:, b % 2, 0:CONV - 1], halo_sb[:, b, :]).then_inc(sem["halo_set"], 1)
                        v.wait_ge(sem["halo_set"], n + 1)
                        v.wait_ge(*wide_read(("xi", t, b)))
                        v.tensor_copy(halo_sb[:, b, :], xi_pad[:, b % 2, CH:CH + CONV - 1]).then_inc(sem["halo_saved"], 1)

                    def tap(t, b, k):
                        n = NB * nP(t) + b
                        v.wait_ge(sem["xi_centered"], n + 1)
                        v.wait_ge(sem["tapped"], (CONV - 1) * n + k)
                        place = conv[:, b % 2, :]
                        v.scalar_tensor_tensor(place, xi_pad[:, b % 2, k:k + CH], convw_sb[:, b, k:k + 1], place, ALU.mult, ALU.add).then_inc(sem["tapped"], 1)

                    def u(t, b):
                        n = NB * nP(t) + b
                        v.wait_ge(sem["u_tanhed"], n + 1)
                        if nP(t):
                            last = [q for q in range(t) if slots[q][1] is not None][-1]
                            v.wait_ge(*narrow_full(("skip_t", last, NB - 1)))
                        v.scalar_tensor_tensor(u_sb[:, b, :], th_p[:, b % 2, :], 1.0, conv[:, b % 2, :], ALU.add, ALU.mult).then_inc(sem["u_made"], 1)

                    def xd_evac(t):
                        key = ("xd", t)
                        v.wait_ge(*wide_full(key))
                        v.tensor_copy(xd_sb[:, slots[t][1][0], :, :], wide_bank(key)[:, 0:NJ * XD].rearrange("p (j n) -> p j n", j=NJ)).then_inc(wide_read(key)[0], 1)

                    def delta_(t, b):
                        n = NB * nP(t) + b
                        v.wait_ge(sem["soft_done"], 2 * nP(t) + b // 2 + 1)
                        place = delta[:, slots[t][1][0], b, :]
                        v.scalar_tensor_tensor(place, place, 0.0, soft_place(b), ALU.max, ALU.add).then_inc(sem["delta_made"], 1)

                    def hn_low(t, k):
                        v.wait_ge(sem["hn_high_done"], NK * nP(t) + k + 1)
                        par = slots[t][1][0]
                        v.tensor_tensor(hnT[1][:, par, k, :], narrow_bank(("hn_t", t, k)), hnT[0][:, par, k, :], ALU.subtract).then_inc(narrow_read(("hn_t", t, k))[0], 1)

                    def h2_low(t, k):
                        v.wait_ge(sem["h2_high_done"], NK * nM(t) + k + 1)
                        v.tensor_tensor(h2T[1][:, k, :], narrow_bank(("h2_t", t, k)), h2T[0][:, k, :], ALU.subtract).then_inc(narrow_read(("h2_t", t, k))[0], 1)

                    def b_low(t):
                        v.wait_ge(sem["xd_t_read"], nP(t) + 1)
                        v.wait_ge(*narrow_read(("xd_t", t)))
                        place = bT[32:NBT, slots[t][1][0], :]
                        v.tensor_tensor(place, xdT[32:NBT, :], place, ALU.subtract).then_inc(sem["b_low_done"], 1)

                    def scan(t, s, b):
                        n = (NS * nS(t) + s) * NB + b
                        par = slots[t][0][0]
                        v.wait_ge(sem["exp_done"], n + 1)
                        v.wait_ge(sem["scaled_done"], n + 1)
                        v.wait_ge(sem["rows_full"], max(0, (n // NB - 1) * NJ))
                        v.wait_ge(sem["carried"], carries(n // NB - 2))
                        first = 0.0
                        if par == 1:
                            first = carry[:, s, b:b + 1]
                            v.wait_ge(sem["carried"], carries(NS * nS(t) - 1))
                        v.tensor_tensor_scan(states[:, n % (2 * NB), :], da_sb[:, n % NDA, :], db_sb[:, b, :], first,
                                             ALU.mult, ALU.add).then_inc(sem["scan_done"], 1)

                    def carries(step):
                        halves = (t for t in range(len(slots)) if slots[t][0] is not None and slots[t][0][0] == 0)
                        return sum(max(0, min(NS, step + 1 - NS * nS(t))) for t in halves)

                    def carry_(t, s):
                        if slots[t][0][0] == 1:
                            return
                        n = NS * nS(t) + s
                        v.wait_ge(sem["scan_done"], NB * (n + 1))
                        at = n % 2 * NB
                        v.tensor_copy(carry[:, s, :], states[:, at:at + NB, CH - 1]).then_inc(sem["carried"], 1)

                    def gather(t, s, j):
                        step = NS * nS(t) + s
                        par = slots[t][0][0]
                        v.wait_ge(sem["rows_full"], NJ * step + j + 1)
                        v.wait_ge(sem["gathered"], max(0, (NJ - 1) * (step - 1) + j + 1))
                        if s == 0 and t > 0 and slots[t - 1][1] is not None:
                            v.wait_ge(*narrow_read(("skip_t", t - 1, NB - 1)))
                        place = y_sb[:, par, j, :]
                        v.scalar_tensor_tensor(place, rows_ps[j % 2][:, :], xd_sb[:, par, j, AT_C + s:AT_C + s + 1], place,
                                               ALU.mult, ALU.add).then_inc(sem["gathered"], 1)

                    def z_gate(t, j):
                        key = ("z", t, j)
                        v.wait_ge(sem["z_tanhed"], NJ * nM(t) + j + 1)
                        place = zg[:, j % 2, :]
                        v.scalar_tensor_tensor(place, place, 1.0, wide_bank(key), ALU.add, ALU.mult).then_inc(wide_read(key)[0], 1)

                    def op_gate(t, j):
                        key = ("op", t, j)
                        v.wait_ge(*wide_full(key))
                        v.wait_ge(sem["mod_in_m"], 16 * rows_in(load_mod_m, t))
                        v.wait_ge(sem["x1_made"], max(0, NJ * nM(t) + j - 1))
                        v.tensor_tensor(gated[:, j % 2, :], wide_bank(key)[:, 0:DM], mod_m[:, 0, :], ALU.mult).then_inc(wide_read(key)[0], 1)

                    def x1_(t, j):
                        v.wait_ge(*wide_read(("op", t, j)))
                        v.wait_ge(sem["r_in"], 16 * (nM(t) + 1))
                        v.tensor_tensor(x1[:, j, :], x1[:, j, :], gated[:, j % 2, :], ALU.add).then_inc(sem["x1_made"], 1)

                    def x1_stat(t, j):
                        v.wait_ge(sem["x1_made"], NJ * nM(t) + j + 1)
                        if nM(t):
                            v.wait_ge(sem["x1_normed"], NJ * nM(t))
                        v.bn_stats(bn[:, 1, j, :], x1[:, j, :]).then_inc(sem["x1_bn"], 1)
                        v.wait_ge(sem["x1_bn"], NJ * nM(t) + j + 1)
                        v.bn_aggr(mv[:, 1, j, :], bn[:, 1, j, :]).then_inc(sem["x1_mv"], 1)

                    def x1_norm(t, j):
                        v.wait_ge(sem["x1_rstd_done"], nM(t) + 1)
                        v.wait_ge(sem["y_gated"], NJ * (nM(t) + 1))
                        if nM(t):
                            last = [n for n in range(t) if slots[n][2] is not None][-1]
                            v.wait_ge(*narrow_full(("h2_t", last, NK - 1)))
                        v.tensor_scalar(h2[:, j, :], x1[:, j, :], mv[:, 1, j, 0:1], rstd[:, 1, 1, j:j + 1],
                                        ALU.subtract, ALU.mult).then_inc(sem["x1_normed"], 1)

                    def x1_scale(t):
                        v.wait_ge(sem["x1_normed"], NJ * (nM(t) + 1))
                        v.tensor_tensor(h2[:, :, :], h2[:, :, :], mod_m[:, 2:3, :].broadcast_to([P, NJ, DM]), ALU.mult).then_inc(sem["h2_made"], 1)

                    def x1_shift(t):
                        v.wait_ge(sem["h2_made"], 2 * nM(t) + 1)
                        v.tensor_tensor(h2[:, :, :], h2[:, :, :], mod_m[:, 1:2, :].broadcast_to([P, NJ, DM]), ALU.add).then_inc(sem["h2_made"], 1)

                    def router(t):
                        def done(instruction):
                            own[0] += 1
                            instruction.then_inc(sem["router_step"], 1)
                            v.wait_ge(sem["router_step"], own[0])

                        above, equal, rank, g = rt[0], rt[1], rt[2], rt[3]
                        count, total = rt_small
                        v.wait_ge(*wide_read(("logit", t)))
                        done(v.tensor_scalar(g_sb[:, :, :], g_sb[:, :, :], 1.0, None, ALU.add))
                        done(v.reciprocal(g[:, :, :], g_sb[:, :, :]))
                        for j in range(NJ):
                            last = v.max(top[:, j, :], g[:, j, :])
                            if j < NJ - 1:
                                last.then_inc(sem["router_step"], 1)
                                own[0] += 1
                        done(last)
                        fourth = top[:, :, TOPK - 1:TOPK].broadcast_to([P, NJ, NE])
                        done(v.tensor_tensor(above[:, :, :], g[:, :, :], fourth, ALU.is_gt))
                        done(v.tensor_tensor(equal[:, :, :], g[:, :, :], fourth, ALU.is_equal))
                        done(v.reduce_sum(count[:, :], above[:, :, :], axis=AX.X))
                        done(v.tensor_tensor_scan(rank[:, :, :].rearrange("p j e -> p (j e)"), restart[:, :, :].rearrange("p j e -> p (j e)"),
                                                  equal[:, :, :].rearrange("p j e -> p (j e)"), 0.0, ALU.mult, ALU.add))
                        done(v.tensor_tensor(rank[:, :, :], rank[:, :, :], count[:, :].unsqueeze(2).broadcast_to([P, NJ, NE]), ALU.add))
                        done(v.tensor_scalar(rank[:, :, :], rank[:, :, :], TOPK + 0.5, None, ALU.is_lt))
                        done(v.tensor_tensor(equal[:, :, :], equal[:, :, :], rank[:, :, :], ALU.mult))
                        done(v.tensor_tensor(above[:, :, :], above[:, :, :], equal[:, :, :], ALU.add))
                        done(v.tensor_tensor(g[:, :, :], g[:, :, :], above[:, :, :], ALU.mult))
                        done(v.reduce_sum(total[:, :], g[:, :, :], axis=AX.X))
                        done(v.reciprocal(total[:, :], total[:, :]))
                        if nM(t):
                            v.wait_ge(sem["e_weighed"], UNITS * nM(t))
                        v.scalar_tensor_tensor(weigh[:, :, 0:NE], g[:, :, :], 0.5 / LIFT ** 2, total[:, :].unsqueeze(2).broadcast_to([P, NJ, NE]),
                                               ALU.mult, ALU.mult).then_inc(sem["router_done"], 1)

                    def e_act(t, u):
                        key = ("expert_in", t, u)
                        v.wait_ge(sem["e_tanhed"], UNITS * nM(t) + u + 1)
                        place = act[:, u % 3, :, :]
                        hin = wide_bank(key).rearrange("p (e a h) -> p e a h", e=2, a=2)[:, :, 0, :]
                        v.scalar_tensor_tensor(place, place, 1.0, hin, ALU.add, ALU.mult).then_inc(sem["e_acted"], 1)

                    def e_mul(t, u):
                        key = ("expert_in", t, u)
                        v.wait_ge(sem["e_acted"], UNITS * nM(t) + u + 1)
                        place = act[:, u % 3, :, :]
                        vin = wide_bank(key).rearrange("p (e a h) -> p e a h", e=2, a=2)[:, :, 1, :]
                        v.tensor_tensor(place, place, vin, ALU.mult).then_inc(wide_read(key)[0], 1)

                    def out_gate(t, q):
                        n = 2 * nM(t) + q
                        v.wait_ge(sem["expert_out_done"], UNITS * nM(t) + 2 * NPAIR * (q + 1))
                        v.wait_ge(sem["out_added"], n)
                        v.tensor_tensor(gated[:, :, :], moe_ps[:, :, :], mod_m[:, 3:4, :].broadcast_to([P, 2, DM]), ALU.mult).then_inc(sem["out_gated"], 1)

                    def out_add(t, q):
                        v.wait_ge(sem["out_gated"], 2 * nM(t) + q + 1)
                        place = x1[:, 2 * q:2 * q + 2, :]
                        v.tensor_tensor(place, place, gated[:, :, :], ALU.add).then_inc(sem["out_added"], 1)

                    own = [0]
                    def ein_low(n):
                        v.wait_ge(sem["ein_high_done"], n + 1)
                        v.scalar_tensor_tensor(ein_w16[1][:, :, n, :], ein_raw[n % 2], LIFT, ein_w16[0][:, :, n, :], ALU.mult,
                                               ALU.subtract).then_inc(sem["ein_low_done"], 1)

                    walk({"ein_low": ein_low, "x_stat": x_stat, "x_norm": x_norm, "x_scale": x_scale, "x_shift": x_shift, "halo": halo, "tap": tap,
                          "u": u, "xd_evac": xd_evac, "delta": delta_, "hn_low": hn_low, "h2_low": h2_low, "b_low": b_low, "scan": scan, "carry": carry_, "gather": gather,
                          "z_gate": z_gate, "op_gate": op_gate, "x1": x1_, "x1_stat": x1_stat, "x1_norm": x1_norm,
                          "x1_scale": x1_scale, "x1_shift": x1_shift, "router": router, "e_act": e_act, "e_mul": e_mul,
                          "out_gate": out_gate, "out_add": out_add})

                @block.tensor
                def _(pe):
                    def hn_t(t, k):
                        pe.wait_ge(sem["h_scaled"], NJ * (nP(t) + 1))
                        pe.wait_ge(*narrow_room(("hn_t", t, k)))
                        for n in range(NJ):
                            last = pe.transpose(narrow_bank(("hn_t", t, k))[:, n * P:n * P + P], h_sb[:, n, k * P:k * P + P], ident[:, :])
                        last.then_inc(narrow_full(("hn_t", t, k))[0], 1)

                    def xi(t, b):
                        key = ("xi", t, b)
                        pe.wait_ge(*narrow_read(("hn_t", t, NK - 1)))
                        pe.wait_ge(*wide_room(key))
                        for n, (k, w, h) in enumerate(SPLIT):
                            last = pe.matmul(wide_bank(key), in_w16[w][:, k, b * P:b * P + P], hnT[h][:, slots[t][1][0], k, :],
                                             start=(n == 0), stop=(n == len(SPLIT) - 1))
                        last.then_inc(wide_full(key)[0], 1)

                    def xd(t):
                        key = ("xd", t)
                        pe.wait_ge(sem["u_made"], NB * (nP(t) + 1))
                        pe.wait_ge(*wide_room(key))
                        for j in range(NJ):
                            for b in range(NB):
                                last = pe.matmul(wide_bank(key)[:, j * XD:j * XD + XD], u_sb[:, b, j * P:j * P + P], xproj_sb[:, b, :],
                                                 start=(b == 0), stop=(b == NB - 1))
                        last.then_inc(wide_full(key)[0], 1)

                    def xd_t(t):
                        pe.wait_ge(*wide_read(("xd", t)))
                        pe.wait_ge(*narrow_room(("xd_t", t)))
                        for n in range(NJ):
                            last = pe.transpose(narrow_bank(("xd_t", t))[0:NBT, n * P:n * P + P], xd_sb[:, slots[t][1][0], n, 0:NBT], ident[:, :])
                        last.then_inc(narrow_full(("xd_t", t))[0], 1)

                    def dtp(t, b):
                        key = ("dtp", t, b)
                        pe.wait_ge(sem["xd_t_read"], nP(t) + 1)
                        pe.wait_ge(*wide_room(key))
                        pe.matmul(wide_bank(key), dtw_sb[:, b * P:b * P + P], xdT, start=True, stop=True).then_inc(wide_full(key)[0], 1)

                    def skip_t(t, b):
                        pe.wait_ge(sem["skip_made"], NB * nP(t) + b + 1)
                        pe.wait_ge(*narrow_room(("skip_t", t, b)))
                        for n in range(NJ):
                            last = pe.transpose(narrow_bank(("skip_t", t, b))[:, n * P:n * P + P], u_sb[:, b, n * P:n * P + P], ident[:, :])
                        last.then_inc(narrow_full(("skip_t", t, b))[0], 1)

                    def b_cast(t, s):
                        key = ("b_cast", t, s)
                        if nP(t):
                            pe.wait_ge(sem["b_low_done"], nP(t))
                        pe.wait_ge(*wide_room(key))
                        pe.matmul(wide_bank(key), select[:, s:s + 1].broadcast_to([NBT, P]), bT[:, slots[t][0][0], :], start=True, stop=True).then_inc(wide_full(key)[0], 1)

                    def rows(t, s, j):
                        step = NS * nS(t) + s
                        pe.wait_ge(sem["scan_done"], (step + 1) * NB)
                        if j == 1:
                            pe.wait_ge(sem["c_scaled"], step)
                        else:
                            pe.wait_ge(sem["gathered"], max(0, (NJ - 1) * step + (0, 0, 1, 2)[j]))
                        for b in range(NB):
                            last = pe.transpose(rows_ps[j % 2][:, b * P:b * P + P], states[:, step % 2 * NB + b, j * P:j * P + P], ident[:, :])
                        last.then_inc(sem["rows_full"], 1)

                    def z(t, j):
                        key = ("z", t, j)
                        pe.wait_ge(*wide_room(key))
                        for n, (k, h, w) in enumerate(SPLIT):
                            last = pe.matmul(wide_bank(key), hnT[h][:, slots[t][2][0], k, j * P:j * P + P], in_w16[w][:, k, DI:2 * DI],
                                             start=(n == 0), stop=(n == len(SPLIT) - 1))
                        last.then_inc(wide_full(key)[0], 1)

                    def y_t(t, j):
                        pe.wait_ge(sem["y_gated"], NJ * nM(t) + j + 1)
                        pe.wait_ge(*narrow_room(("y_t", t, j)))
                        for n in range(NB):
                            last = pe.transpose(narrow_bank(("y_t", t, j))[:, n * P:n * P + P], y_sb[:, slots[t][2][0], j, n * P:n * P + P], ident[:, :])
                        last.then_inc(narrow_full(("y_t", t, j))[0], 1)

                    def op(t, j):
                        key = ("op", t, j)
                        pe.wait_ge(*narrow_read(("y_t", t, j)))
                        pe.wait_ge(*wide_room(key))
                        for b in range(NB):
                            last = pe.matmul(wide_bank(key)[:, 0:DM], yT[:, j % 2, b, :], out_sb[:, b, :], start=(b == 0), stop=(b == NB - 1))
                        last.then_inc(wide_full(key)[0], 1)

                    def h2_t(t, k):
                        pe.wait_ge(sem["h2_made"], 2 * (nM(t) + 1))
                        pe.wait_ge(*narrow_room(("h2_t", t, k)))
                        for n in range(NJ):
                            last = pe.transpose(narrow_bank(("h2_t", t, k))[:, n * P:n * P + P], h2[:, n, k * P:k * P + P], ident[:, :])
                        last.then_inc(narrow_full(("h2_t", t, k))[0], 1)

                    def logit(t):
                        key = ("logit", t)
                        pe.wait_ge(*narrow_read(("h2_t", t, NK - 1)))
                        pe.wait_ge(*wide_room(key))
                        for j in range(NJ):
                            for n, (k, h, w) in enumerate(SPLIT):
                                last = pe.matmul(wide_bank(key)[:, j * NE:j * NE + NE], h2T[h][:, k, j * P:j * P + P], gate_w16[w][:, k, :],
                                                 start=(n == 0), stop=(n == len(SPLIT) - 1))
                        last.then_inc(wide_full(key)[0], 1)

                    def expert_in(t, u):
                        key = ("expert_in", t, u)
                        j = tile_of(u)
                        pe.wait_ge(*wide_room(key))
                        for n, (k, h, w) in enumerate(SPLIT):
                            last = pe.matmul(wide_bank(key), h2T[h][:, k, j * P:j * P + P], ein_w16[w][:, k, pair_of(u), :],
                                             start=(n == 0), stop=(n == len(SPLIT) - 1))
                        last.then_inc(wide_full(key)[0], 1)

                    def e_t(t, u):
                        pe.wait_ge(sem["e_weighed"], UNITS * nM(t) + u + 1)
                        pe.wait_ge(*narrow_room(("e_t", t, u)))
                        for n in range(2):
                            last = pe.transpose(narrow_bank(("e_t", t, u))[:, n * P:n * P + P], act[:, u % 3, n, :], ident[:, :])
                        last.then_inc(narrow_full(("e_t", t, u))[0], 1)

                    def expert_out(t, u):
                        pe.wait_ge(*narrow_read(("e_t", t, u)))
                        first = u % (2 * NPAIR) == 0
                        if first:
                            pe.wait_ge(sem["out_gated"], 2 * nM(t) + u // (2 * NPAIR))
                        for n in range(2):
                            last = pe.matmul(moe_ps[:, u % 2, :], hidT[:, u % 2, n, :], eout_sb[:, 2 * pair_of(u) + n, :],
                                             start=first and n == 0, stop=pair_of(u) == NPAIR - 1 and n == 1, skip_group_check=True)
                        last.then_inc(sem["expert_out_done"], 1)

                    walk({"hn_t": hn_t, "xi": xi, "xd": xd, "xd_t": xd_t, "dtp": dtp, "skip_t": skip_t,
                          "b_cast": b_cast, "rows": rows, "z": z, "y_t": y_t, "op": op, "h2_t": h2_t, "logit": logit,
                          "expert_in": expert_in, "e_t": e_t, "expert_out": expert_out})
            clear_semaphores()

        def full(k, i):
            c = 2 * k + i
            return [((1, c + 1), (0, c + 2), (0, c)), ((0, c + 2), (1, c + 3), (1, c + 1))]

        run_slots([(None, (0, 0), None), ((0, 0), (1, 1), None)], {0: 0}, {}, first_block=True)
        with nc.Fori(0, BATCH // 2 - 1) as i:
            run_slots(full(0, 4 * i) + full(1, 4 * i), {0: 2 * i + 1, 2: 2 * i + 2}, {0: 2 * i, 2: 2 * i + 1})
        run_slots(full(0, NC - 4) + [((1, NC - 1), None, (0, NC - 2)), (None, None, (1, NC - 1))],
                  {0: BATCH - 1}, {0: BATCH - 2, 2: BATCH - 1})


_INS = ("x", "norm_w", "in_w", "conv_w", "conv_b", "xproj_w", "dt_w", "dt_b", "a_log", "d_skip", "out_w",
        "gate_w", "e_in", "e_out", "c_t", "w_mod")


def kernel(L0_attn_x, L0_attn_norm_w, L0_attn_in_proj_w, L0_attn_conv_w, L0_attn_conv_b, L0_attn_x_proj_w,
           L0_attn_dt_proj_w, L0_attn_dt_proj_b, L0_attn_A_log, L0_attn_D, L0_attn_out_proj_w, L0_ffn_gate_w,
           L0_ffn_ws_in, L0_ffn_vs_in, L0_ffn_ws_out, L0_ffn_e_win, L0_ffn_e_vin, L0_ffn_e_wout, L0_c, L0_wmod):
    import concourse.bacc as bacc
    from concourse.bass_utils import run_bass_kernel_spmd

    def blocks(w):
        return np.ascontiguousarray(w.reshape(-1, P, w.shape[-1]).transpose(1, 0, 2))

    def chunks(a):
        return np.ascontiguousarray(a.reshape(NC, NJ, P, DM).transpose(0, 2, 1, 3))

    a = {k: np.asarray(v) for k, v in locals().items() if k.startswith("L0_")}
    win = np.concatenate([a["L0_ffn_e_win"], a["L0_ffn_ws_in"].reshape(DM, 2, HID).transpose(1, 0, 2)], 0)
    vin = np.concatenate([a["L0_ffn_e_vin"], a["L0_ffn_vs_in"].reshape(DM, 2, HID).transpose(1, 0, 2)], 0)
    e_in = np.concatenate([win, vin], 2)
    e_in = e_in.reshape(NPAIR, 2, NK, P, 2 * HID).transpose(3, 2, 0, 1, 4).reshape(P, NK, NPAIR, 4 * HID)
    e_out = np.concatenate([a["L0_ffn_e_wout"], a["L0_ffn_ws_out"].reshape(2, HID, DM)], 0).transpose(1, 0, 2)
    dt_at, b_at, c_at = np.arange(RANK), np.arange(RANK, RANK + NS), np.arange(RANK + NS, RANK + 2 * NS)
    columns = np.concatenate([b_at, dt_at, b_at, c_at])
    dt_w = np.zeros((NBT, DI), a["L0_attn_dt_proj_w"].dtype)
    dt_w[NS:NS + RANK] = a["L0_attn_dt_proj_w"].T
    arrays = {
        "x": chunks(a["L0_attn_x"]),
        "norm_w": a["L0_attn_norm_w"].reshape(NK, P).T,
        "in_w": blocks(a["L0_attn_in_proj_w"].T),
        "conv_w": blocks(a["L0_attn_conv_w"]),
        "conv_b": a["L0_attn_conv_b"].reshape(NB, P).T,
        "xproj_w": blocks(a["L0_attn_x_proj_w"][columns].T),
        "dt_w": dt_w,
        "dt_b": a["L0_attn_dt_proj_b"].reshape(NB, P).T,
        "a_log": blocks(a["L0_attn_A_log"]),
        "d_skip": a["L0_attn_D"].reshape(NB, P).T,
        "out_w": blocks(a["L0_attn_out_proj_w"].T),
        "gate_w": blocks(a["L0_ffn_gate_w"].T),
        "e_in": e_in,
        "e_out": e_out,
        "c_t": blocks(a["L0_c"].T),
        "w_mod": blocks(a["L0_wmod"]),
    }
    nc = bacc.Bacc("TRN2", target_bir_lowering=False, num_devices=1, dynamic_dma_scratch_size=1024)
    feed, args = {}, []
    for name in _INS:
        value = np.ascontiguousarray(arrays[name])
        feed[name + "_dram"] = value
        args.append(nc.dram_tensor(name + "_dram", value.shape, mybir.dt.from_np(value.dtype), kind="ExternalInput").ap())
    out = nc.dram_tensor("out_dram", (NC, P, NJ, DM), F32, kind="ExternalOutput").ap()
    adaln_block(nc, *args, out)
    r = run_bass_kernel_spmd(nc, [feed], core_ids=[0])
    got = r.results[0]["out_dram"]
    return np.ascontiguousarray(got.transpose(0, 2, 1, 3)).reshape(BATCH, SEQ, DM)
```
